# Optimizing a Trainium2 kernel written in Bass

```python
import numpy as np
import jax
import jax.numpy as jnp

def _softmax(x, axis=-1):
    return jax.nn.softmax(x, axis=axis)

def _gelu(x):
    return jax.nn.gelu(x, approximate=True)

def _silu(x):
    return jax.nn.silu(x)

def _sigmoid(x):
    return jax.nn.sigmoid(x)

def _layernorm(x, axis=-1, eps=1e-05):
    m = jnp.mean(x, axis=axis, keepdims=True)
    v = jnp.var(x, axis=axis, keepdims=True)
    return (x - m) / jnp.sqrt(v + eps)

def _scatter_add(tgt, idx, src, axis=0):
    return tgt.at[idx].add(src)

def _segment_sum(src, seg, n):
    return jax.ops.segment_sum(src, seg, n)
kernel_name = 'mk_vit_tower_cls_d1_tok_img256_r4_34b3fa'

def setup_inputs(seed: int=0):
    np.random.seed(seed)
    _w = jnp.asarray

    def _rec_inputs():
        import jax
        import jax.numpy as jnp
        _rk = jax.random.key(seed)
        x = 9.04603e-05 + 1.00016 * jax.random.normal(jax.random.fold_in(_rk, 1), (8, 1, 224, 224), jnp.float32)
        cls_tok = 0.02 * jax.random.normal(jax.random.fold_in(_rk, 5), (1, 1, 64), jnp.float32)
        return (x, cls_tok)
    x, cls_tok = _rec_inputs()

    def _L0_tok_setup():
        import jax, jax.numpy as jnp
        import numpy as np
        WS = 7
        H = W = 56
        C = 64
        NH = 8
        HD = C // NH
        SCALE = HD ** (-0.5)
        SHIFT = WS // 2
        N = WS * WS

        def _rel_pos_index():
            coords = np.stack(np.meshgrid(np.arange(WS), np.arange(WS), indexing='ij'))
            cf = coords.reshape(2, -1)
            rel = (cf[:, :, None] - cf[:, None, :]).transpose(1, 2, 0).copy()
            rel[..., 0] += WS - 1
            rel[..., 1] += WS - 1
            rel[..., 0] *= 2 * WS - 1
            return jnp.array(rel.sum(-1))

        def _attn_mask():
            img = np.zeros((H, W), np.int32)
            cnt = 0
            for h in (slice(0, -WS), slice(-WS, -SHIFT), slice(-SHIFT, None)):
                for w in (slice(0, -WS), slice(-WS, -SHIFT), slice(-SHIFT, None)):
                    cnt += 1
                    img[h, w] = cnt
            mw = img.reshape(H // WS, WS, W // WS, WS).transpose(0, 2, 1, 3).reshape(-1, N)
            diff = mw[:, None, :] - mw[:, :, None]
            return jnp.array(np.where(diff != 0, -100.0, 0.0).astype(np.float32))

        def _layernorm(x, g, b):
            m = x.mean(-1, keepdims=True)
            v = ((x - m) ** 2).mean(-1, keepdims=True)
            return (x - m) * jax.lax.rsqrt(v + 1e-05) * g + b

        def _window_partition(x):
            B = x.shape[0]
            x = x.reshape(B, H // WS, WS, W // WS, WS, C).transpose(0, 1, 3, 2, 4, 5)
            return x.reshape(-1, N, C)

        def _window_reverse(xw, B):
            x = xw.reshape(B, H // WS, W // WS, WS, WS, C).transpose(0, 1, 3, 2, 4, 5)
            return x.reshape(B, H, W, C)

        def _swin_block(x, p, shift, rpi, amask):
            B = x.shape[0]
            shortcut = x
            h = _layernorm(x, p['n1g'], p['n1b']).reshape(B, H, W, C)
            if shift > 0:
                h = jnp.roll(h, (-shift, -shift), axis=(1, 2))
            xw = _window_partition(h)
            B_ = xw.shape[0]
            qkv = (xw @ p['qkv_w'].T + p['qkv_b']).reshape(B_, N, 3, NH, HD).transpose(2, 0, 3, 1, 4)
            q, k, v = (qkv[0], qkv[1], qkv[2])
            attn = jnp.einsum('bhnd,bhmd->bhnm', q * SCALE, k)
            attn = attn + p['rpb'][rpi].transpose(2, 0, 1)[None]
            if shift > 0:
                nW = amask.shape[0]
                attn = attn.reshape(B_ // nW, nW, NH, N, N) + amask[None, :, None]
                attn = attn.reshape(B_, NH, N, N)
            attn = jax.nn.softmax(attn, axis=-1)
            o = jnp.einsum('bhnm,bhmd->bhnd', attn, v).transpose(0, 2, 1, 3).reshape(B_, N, C)
            o = o @ p['proj_w'].T + p['proj_b']
            h = _window_reverse(o, B)
            if shift > 0:
                h = jnp.roll(h, (shift, shift), axis=(1, 2))
            x = shortcut + h.reshape(B, H * W, C)
            y = _layernorm(x, p['n2g'], p['n2b'])
            y = jax.nn.gelu(y @ p['w1'].T + p['b1'], approximate=False)
            return x + y @ p['w2'].T + p['b2']
        key = jax.random.key(seed)
        ks = jax.random.split(key, 8)
        s = 0.02
        return {'x': jax.random.normal(ks[0], (16, 1, 224, 224), jnp.float32), 'pe_w': jax.random.normal(ks[1], (C, 1, 4, 4), jnp.float32) * s, 'pe_b': jnp.zeros((C,), jnp.float32), 'pe_ng': jnp.ones((C,), jnp.float32), 'pe_nb': jnp.zeros((C,), jnp.float32), 'n1g': jnp.ones((2, C), jnp.float32), 'n1b': jnp.zeros((2, C), jnp.float32), 'qkv_w': jax.random.normal(ks[2], (2, 3 * C, C), jnp.float32) * s, 'qkv_b': jnp.zeros((2, 3 * C), jnp.float32), 'rpb': jax.random.normal(ks[3], (2, (2 * WS - 1) ** 2, NH), jnp.float32) * s, 'proj_w': jax.random.normal(ks[4], (2, C, C), jnp.float32) * s, 'proj_b': jnp.zeros((2, C), jnp.float32), 'n2g': jnp.ones((2, C), jnp.float32), 'n2b': jnp.zeros((2, C), jnp.float32), 'w1': jax.random.normal(ks[5], (2, 4 * C, C), jnp.float32) * s, 'b1': jnp.zeros((2, 4 * C), jnp.float32), 'w2': jax.random.normal(ks[6], (2, C, 4 * C), jnp.float32) * s, 'b2': jnp.zeros((2, C), jnp.float32)}
    _L0_tok_all = _L0_tok_setup()
    _L0_tok_in = {k: v for k, v in _L0_tok_all.items() if k in ('pe_w', 'pe_b', 'pe_ng', 'pe_nb', 'n1g', 'n1b', 'qkv_w', 'qkv_b', 'rpb', 'proj_w', 'proj_b', 'n2g', 'n2b', 'w1', 'b1', 'w2', 'b2')}
    del _L0_tok_all

    def _L0_attn_setup():
        import jax, jax.numpy as jnp
        import numpy as np
        B, N, C, H = (4, 512, 64, 16)
        D = C // H
        key = jax.random.key(seed)
        k1, k2, k3 = jax.random.split(key, 3)
        x = jax.random.normal(k1, (B, N, C), dtype=jnp.float32)
        w_qkv = jax.random.normal(k2, (C, 3 * C), dtype=jnp.float32) * C ** (-0.5)
        b_qkv = jnp.zeros((3 * C,), dtype=jnp.float32)
        w_proj = jax.random.normal(k3, (C, C), dtype=jnp.float32) * C ** (-0.5)
        b_proj = jnp.zeros((C,), dtype=jnp.float32)
        return {'x': x, 'w_qkv': w_qkv, 'b_qkv': b_qkv, 'w_proj': w_proj, 'b_proj': b_proj}
    _L0_attn_all = _L0_attn_setup()
    _L0_attn_in = {k: v for k, v in _L0_attn_all.items() if k in ('w_qkv', 'b_qkv', 'w_proj', 'b_proj')}
    del _L0_attn_all

    def _L0_ffn_setup():
        import jax, jax.numpy as jnp
        import numpy as np
        B, T, C = (64, 96, 64)
        NH, NKV = (4, 2)
        HD = C // NH
        NREP = NH // NKV
        NE, TOPK = (8, 2)
        HID = int(8 / 3 * C)
        EPS_RMS = 1e-06

        def _rope_tables(t_len):
            inv_freq = 1.0 / 10000.0 ** (np.arange(0, HD, 2, dtype=np.float32) / HD)
            t = np.arange(t_len, dtype=np.float32)
            freqs = np.outer(t, inv_freq)
            emb = np.concatenate([freqs, freqs], axis=-1)
            return (jnp.asarray(np.cos(emb)), jnp.asarray(np.sin(emb)))

        def _rotate_half(x):
            h = x.shape[-1] // 2
            return jnp.concatenate([-x[..., h:], x[..., :h]], axis=-1)

        def _rmsnorm(v, w):
            return v * jax.lax.rsqrt(jnp.mean(v * v, axis=-1, keepdims=True) + EPS_RMS) * w
        key = jax.random.key(seed)
        ks = jax.random.split(key, 10)
        s = lambda k, shape: jax.random.normal(k, shape, jnp.float32) * 0.02
        return {'x': jax.random.normal(ks[0], (B, T, C), jnp.float32), 'ln1_w': jnp.ones((C,), jnp.float32), 'ln2_w': jnp.ones((C,), jnp.float32), 'wq': s(ks[1], (NH * HD, C)), 'wk': s(ks[2], (NKV * HD, C)), 'wv': s(ks[3], (NKV * HD, C)), 'wo': s(ks[4], (C, C)), 'router_w': s(ks[5], (NE, C)), 'w1': s(ks[6], (NE, HID, C)), 'w2': s(ks[7], (NE, C, HID)), 'w3': s(ks[8], (NE, HID, C))}
    _L0_ffn_all = _L0_ffn_setup()
    _L0_ffn_in = {k: v for k, v in _L0_ffn_all.items() if k in ('ln1_w', 'ln2_w', 'wq', 'wk', 'wv', 'wo', 'router_w', 'w1', 'w2', 'w3')}
    del _L0_ffn_all
    return {'x': x, 'cls_tok': cls_tok, 'L0_tok_pe_w': _L0_tok_in['pe_w'], 'L0_tok_pe_b': _L0_tok_in['pe_b'], 'L0_tok_pe_ng': _L0_tok_in['pe_ng'], 'L0_tok_pe_nb': _L0_tok_in['pe_nb'], 'L0_tok_n1g': _L0_tok_in['n1g'], 'L0_tok_n1b': _L0_tok_in['n1b'], 'L0_tok_qkv_w': _L0_tok_in['qkv_w'], 'L0_tok_qkv_b': _L0_tok_in['qkv_b'], 'L0_tok_rpb': _L0_tok_in['rpb'], 'L0_tok_proj_w': _L0_tok_in['proj_w'], 'L0_tok_proj_b': _L0_tok_in['proj_b'], 'L0_tok_n2g': _L0_tok_in['n2g'], 'L0_tok_n2b': _L0_tok_in['n2b'], 'L0_tok_w1': _L0_tok_in['w1'], 'L0_tok_b1': _L0_tok_in['b1'], 'L0_tok_w2': _L0_tok_in['w2'], 'L0_tok_b2': _L0_tok_in['b2'], 'L0_attn_w_qkv': _L0_attn_in['w_qkv'], 'L0_attn_b_qkv': _L0_attn_in['b_qkv'], 'L0_attn_w_proj': _L0_attn_in['w_proj'], 'L0_attn_b_proj': _L0_attn_in['b_proj'], 'L0_ffn_ln1_w': _L0_ffn_in['ln1_w'], 'L0_ffn_ln2_w': _L0_ffn_in['ln2_w'], 'L0_ffn_wq': _L0_ffn_in['wq'], 'L0_ffn_wk': _L0_ffn_in['wk'], 'L0_ffn_wv': _L0_ffn_in['wv'], 'L0_ffn_wo': _L0_ffn_in['wo'], 'L0_ffn_router_w': _L0_ffn_in['router_w'], 'L0_ffn_w1': _L0_ffn_in['w1'], 'L0_ffn_w2': _L0_ffn_in['w2'], 'L0_ffn_w3': _L0_ffn_in['w3']}

def reference(x, cls_tok, L0_tok_pe_w, L0_tok_pe_b, L0_tok_pe_ng, L0_tok_pe_nb, L0_tok_n1g, L0_tok_n1b, L0_tok_qkv_w, L0_tok_qkv_b, L0_tok_rpb, L0_tok_proj_w, L0_tok_proj_b, L0_tok_n2g, L0_tok_n2b, L0_tok_w1, L0_tok_b1, L0_tok_w2, L0_tok_b2, L0_attn_w_qkv, L0_attn_b_qkv, L0_attn_w_proj, L0_attn_b_proj, L0_ffn_ln1_w, L0_ffn_ln2_w, L0_ffn_wq, L0_ffn_wk, L0_ffn_wv, L0_ffn_wo, L0_ffn_router_w, L0_ffn_w1, L0_ffn_w2, L0_ffn_w3):
    import jax
    import jax.numpy as jnp

    def _L0_tok_ref(x, pe_w, pe_b, pe_ng, pe_nb, n1g, n1b, qkv_w, qkv_b, rpb, proj_w, proj_b, n2g, n2b, w1, b1, w2, b2):
        import jax, jax.numpy as jnp
        import numpy as np
        WS = 7
        H = W = 56
        C = 64
        NH = 8
        HD = C // NH
        SCALE = HD ** (-0.5)
        SHIFT = WS // 2
        N = WS * WS

        def _rel_pos_index():
            coords = np.stack(np.meshgrid(np.arange(WS), np.arange(WS), indexing='ij'))
            cf = coords.reshape(2, -1)
            rel = (cf[:, :, None] - cf[:, None, :]).transpose(1, 2, 0).copy()
            rel[..., 0] += WS - 1
            rel[..., 1] += WS - 1
            rel[..., 0] *= 2 * WS - 1
            return jnp.array(rel.sum(-1))

        def _attn_mask():
            img = np.zeros((H, W), np.int32)
            cnt = 0
            for h in (slice(0, -WS), slice(-WS, -SHIFT), slice(-SHIFT, None)):
                for w in (slice(0, -WS), slice(-WS, -SHIFT), slice(-SHIFT, None)):
                    cnt += 1
                    img[h, w] = cnt
            mw = img.reshape(H // WS, WS, W // WS, WS).transpose(0, 2, 1, 3).reshape(-1, N)
            diff = mw[:, None, :] - mw[:, :, None]
            return jnp.array(np.where(diff != 0, -100.0, 0.0).astype(np.float32))

        def _layernorm(x, g, b):
            m = x.mean(-1, keepdims=True)
            v = ((x - m) ** 2).mean(-1, keepdims=True)
            return (x - m) * jax.lax.rsqrt(v + 1e-05) * g + b

        def _window_partition(x):
            B = x.shape[0]
            x = x.reshape(B, H // WS, WS, W // WS, WS, C).transpose(0, 1, 3, 2, 4, 5)
            return x.reshape(-1, N, C)

        def _window_reverse(xw, B):
            x = xw.reshape(B, H // WS, W // WS, WS, WS, C).transpose(0, 1, 3, 2, 4, 5)
            return x.reshape(B, H, W, C)

        def _swin_block(x, p, shift, rpi, amask):
            B = x.shape[0]
            shortcut = x
            h = _layernorm(x, p['n1g'], p['n1b']).reshape(B, H, W, C)
            if shift > 0:
                h = jnp.roll(h, (-shift, -shift), axis=(1, 2))
            xw = _window_partition(h)
            B_ = xw.shape[0]
            qkv = (xw @ p['qkv_w'].T + p['qkv_b']).reshape(B_, N, 3, NH, HD).transpose(2, 0, 3, 1, 4)
            q, k, v = (qkv[0], qkv[1], qkv[2])
            attn = jnp.einsum('bhnd,bhmd->bhnm', q * SCALE, k)
            attn = attn + p['rpb'][rpi].transpose(2, 0, 1)[None]
            if shift > 0:
                nW = amask.shape[0]
                attn = attn.reshape(B_ // nW, nW, NH, N, N) + amask[None, :, None]
                attn = attn.reshape(B_, NH, N, N)
            attn = jax.nn.softmax(attn, axis=-1)
            o = jnp.einsum('bhnm,bhmd->bhnd', attn, v).transpose(0, 2, 1, 3).reshape(B_, N, C)
            o = o @ p['proj_w'].T + p['proj_b']
            h = _window_reverse(o, B)
            if shift > 0:
                h = jnp.roll(h, (shift, shift), axis=(1, 2))
            x = shortcut + h.reshape(B, H * W, C)
            y = _layernorm(x, p['n2g'], p['n2b'])
            y = jax.nn.gelu(y @ p['w1'].T + p['b1'], approximate=False)
            return x + y @ p['w2'].T + p['b2']
        B = x.shape[0]
        h = jax.lax.conv_general_dilated(x, pe_w, (4, 4), 'VALID', dimension_numbers=('NCHW', 'OIHW', 'NCHW'))
        h = h + pe_b[None, :, None, None]
        t = h.reshape(B, C, H * W).transpose(0, 2, 1)
        t = _layernorm(t, pe_ng, pe_nb)
        rpi = _rel_pos_index()
        amask = _attn_mask()
        for i, shift in enumerate((0, SHIFT)):
            p = {'n1g': n1g[i], 'n1b': n1b[i], 'qkv_w': qkv_w[i], 'qkv_b': qkv_b[i], 'rpb': rpb[i], 'proj_w': proj_w[i], 'proj_b': proj_b[i], 'n2g': n2g[i], 'n2b': n2b[i], 'w1': w1[i], 'b1': b1[i], 'w2': w2[i], 'b2': b2[i]}
            t = _swin_block(t, p, shift, rpi, amask)
        return t

    def _L0_attn_ref(x, w_qkv, b_qkv, w_proj, b_proj):
        import jax, jax.numpy as jnp
        import numpy as np
        B, N, C, H = (4, 512, 64, 16)
        D = C // H
        b, n, c = x.shape
        qkv = x @ w_qkv + b_qkv
        qkv = qkv.reshape(b, n, 3, H, D)
        q = jnp.transpose(qkv[:, :, 0], (0, 2, 1, 3))
        k = jnp.transpose(qkv[:, :, 1], (0, 2, 1, 3))
        v = jnp.transpose(qkv[:, :, 2], (0, 2, 1, 3))
        attn = jnp.einsum('bhqd,bhkd->bhqk', q, k)
        attn = jax.nn.softmax(attn, axis=-1)
        out = jnp.einsum('bhqk,bhkd->bhqd', attn, v)
        out = jnp.transpose(out, (0, 2, 1, 3)).reshape(b, n, c)
        return out @ w_proj + b_proj

    def _L0_ffn_ref(x, ln1_w, ln2_w, wq, wk, wv, wo, router_w, w1, w2, w3):
        import jax, jax.numpy as jnp
        import numpy as np
        B, T, C = (64, 96, 64)
        NH, NKV = (4, 2)
        HD = C // NH
        NREP = NH // NKV
        NE, TOPK = (8, 2)
        HID = int(8 / 3 * C)
        EPS_RMS = 1e-06

        def _rope_tables(t_len):
            inv_freq = 1.0 / 10000.0 ** (np.arange(0, HD, 2, dtype=np.float32) / HD)
            t = np.arange(t_len, dtype=np.float32)
            freqs = np.outer(t, inv_freq)
            emb = np.concatenate([freqs, freqs], axis=-1)
            return (jnp.asarray(np.cos(emb)), jnp.asarray(np.sin(emb)))

        def _rotate_half(x):
            h = x.shape[-1] // 2
            return jnp.concatenate([-x[..., h:], x[..., :h]], axis=-1)

        def _rmsnorm(v, w):
            return v * jax.lax.rsqrt(jnp.mean(v * v, axis=-1, keepdims=True) + EPS_RMS) * w
        Bx, Tx, Cx = x.shape
        h = _rmsnorm(x, ln1_w)
        q = (h @ wq.T).reshape(Bx, Tx, NH, HD).transpose(0, 2, 1, 3)
        k = (h @ wk.T).reshape(Bx, Tx, NKV, HD).transpose(0, 2, 1, 3)
        v = (h @ wv.T).reshape(Bx, Tx, NKV, HD).transpose(0, 2, 1, 3)
        cos, sin = _rope_tables(Tx)
        cos, sin = (cos[None, None], sin[None, None])
        q = q * cos + _rotate_half(q) * sin
        k = k * cos + _rotate_half(k) * sin
        k = jnp.repeat(k, NREP, axis=1)
        v = jnp.repeat(v, NREP, axis=1)
        scores = jnp.einsum('bhtd,bhsd->bhts', q, k) / jnp.sqrt(jnp.float32(HD))
        causal = jnp.tril(jnp.ones((Tx, Tx), dtype=bool))
        scores = jnp.where(causal[None, None], scores, jnp.float32(-1e+30))
        att = jax.nn.softmax(scores, axis=-1)
        y = jnp.einsum('bhts,bhsd->bhtd', att, v).transpose(0, 2, 1, 3).reshape(Bx, Tx, Cx)
        x = x + y @ wo.T
        flat = _rmsnorm(x, ln2_w).reshape(-1, Cx)
        probs = jax.nn.softmax(flat @ router_w.T, axis=-1)
        tp, ti = jax.lax.top_k(probs, TOPK)
        tp = tp / (jnp.sum(tp, axis=-1, keepdims=True) + 1e-09)
        weights = jnp.sum(tp[..., None] * jax.nn.one_hot(ti, NE, dtype=flat.dtype), axis=1)
        out = jnp.zeros_like(flat)
        for e in range(NE):
            hh = jax.nn.silu(flat @ w1[e].T) * (flat @ w3[e].T)
            out = out + weights[:, e:e + 1] * (hh @ w2[e].T)
        return x + out.reshape(Bx, Tx, Cx)
    h = _L0_tok_ref(x, L0_tok_pe_w, L0_tok_pe_b, L0_tok_pe_ng, L0_tok_pe_nb, L0_tok_n1g, L0_tok_n1b, L0_tok_qkv_w, L0_tok_qkv_b, L0_tok_rpb, L0_tok_proj_w, L0_tok_proj_b, L0_tok_n2g, L0_tok_n2b, L0_tok_w1, L0_tok_b1, L0_tok_w2, L0_tok_b2)
    h = jnp.concatenate([jnp.broadcast_to(cls_tok, (h.shape[0], 1, h.shape[2])), h], axis=1)
    h = h + _L0_attn_ref(_layernorm(h, axis=-1), L0_attn_w_qkv, L0_attn_b_qkv, L0_attn_w_proj, L0_attn_b_proj)
    h = h + _L0_ffn_ref(_layernorm(h, axis=-1), L0_ffn_ln1_w, L0_ffn_ln2_w, L0_ffn_wq, L0_ffn_wk, L0_ffn_wv, L0_ffn_wo, L0_ffn_router_w, L0_ffn_w1, L0_ffn_w2, L0_ffn_w3)
    return h

_drawn_inputs = setup_inputs


def setup_inputs(seed=0):
    import zlib

    import numpy as np

    out = dict(_drawn_inputs(seed))
    spreads = {'L0_tok_pe_b': (0.0, 0.1),
     'L0_tok_pe_ng': (1.0, 0.2),
     'L0_tok_pe_nb': (0.0, 0.1),
     'L0_tok_n1g': (1.0, 0.6),
     'L0_tok_n1b': (0.0, 0.8),
     'L0_tok_qkv_b': (0.0, 0.493),
     'L0_tok_proj_b': (0.0, 0.1),
     'L0_tok_n2g': (1.0, 0.6),
     'L0_tok_n2b': (0.0, 0.8),
     'L0_tok_b1': (0.0, 0.416),
     'L0_tok_b2': (0.0, 0.1),
     'L0_attn_b_qkv': (0.0, 0.1),
     'L0_attn_b_proj': (0.0, 0.1),
     'L0_ffn_ln1_w': (1.0, 0.6),
     'L0_ffn_ln2_w': (1.0, 0.6)}
    factors = {'cls_tok': 8.0,
     'L0_tok_rpb': 200.0,
     'L0_ffn_wq': 8.0,
     'L0_ffn_wk': 8.0,
     'L0_ffn_wv': 6.752,
     'L0_ffn_wo': 8.0,
     'L0_ffn_router_w': 8.0,
     'L0_ffn_w1': 8.0,
     'L0_ffn_w2': 8.0,
     'L0_ffn_w3': 8.0}
    for name, (base, spread) in spreads.items():
        noise = np.random.default_rng([zlib.crc32(name.encode()), seed]).standard_normal(out[name].shape)
        drawn = base * np.exp(spread * noise) if base else spread * noise
        out[name] = jnp.asarray(drawn.astype(out[name].dtype))
    for name, factor in factors.items():
        out[name] = (out[name] * factor).astype(out[name].dtype)
    return out
```

```python
from contextlib import ExitStack

import concourse.bass as bass
from concourse import mybir

F32 = mybir.dt.float32
BF16 = mybir.dt.bfloat16
U32 = mybir.dt.uint32
ALU = mybir.AluOpType
ACT = mybir.ActivationFunctionType
AX = mybir.AxisListType

B = 8
SIDE = 56
TOK = SIDE * SIDE
C = 64
WIN = 7
NW = WIN * WIN
ROWS = SIDE // WIN
SHIFT = WIN // 2
PAD = SIDE + SHIFT
SH = 8
SD = C // SH
SLOT = 64
LN_EPS = 1e-5
RMS_EPS = 1e-6

SEQ = TOK + 1
P = 128
TILES = -(-SEQ // P)
SEQP = TILES * P
LAST = SEQ - (TILES - 1) * P
GT = 5
GROUPS = TILES // GT
QW = 512
QBLOCKS = SEQP // QW


START = 1


def phase_tools(nc, ctx):
    def sb(name, shape, dt=F32):
        return ctx.enter_context(nc.sbuf_tensor(name, shape, dt))

    def ps(name, shape, dt=F32):
        return ctx.enter_context(nc.psum_tensor(name, shape, dt))

    sems = []

    def sem(name):
        sems.append(nc.alloc_semaphore(name))
        return sems[-1]

    def begin():
        for s in sems:
            nc.gpsimd.sem_inc(s, START)
        nc.all_engine_barrier()

    def clear():
        nc.clear_and_free_semaphores(sems)
        nc.all_engine_barrier()

    ctx.callback(clear)
    return sb, ps, sem, begin


class Steps:

    def __init__(self, eng, sem, per):
        self.eng, self.sem, self.per, self.at = eng, sem, per, 0

    def start(self, i):
        assert self.at in (0, self.per), (self.at, self.per)
        self.i, self.at = i, 0

    def link(self, ins):
        ins.then_inc(self.sem, 1)
        self.at += 1
        self.eng.wait_ge(self.sem, START + self.i * self.per + self.at)


def bcast(ap, n):
    shape = list(ap.shape)
    return ap.unsqueeze(len(shape)).to_broadcast(shape + [n])


def centred_and_variance(nc, steps, x, xs, sq, mean, var, eps, var_ready):
    steps.link(nc.vector.reduce_sum(mean, x, AX.X))
    steps.link(nc.vector.tensor_scalar(mean, mean, 1.0 / C, None, ALU.mult))
    steps.link(nc.vector.tensor_tensor(xs, x, bcast(mean, C), ALU.subtract))
    steps.link(nc.vector.tensor_tensor(sq, xs, xs, ALU.mult))
    steps.link(nc.vector.reduce_sum(var, sq, AX.X))
    nc.vector.tensor_scalar(var, var, 1.0 / C, eps, ALU.mult, ALU.add).then_inc(var_ready, 1)


def patch_embed(nc, patches, w_patch, norm_rows, tokens):
    TP, G = 112, 4
    NG = B * TOK // (TP * G)
    K = 17
    with ExitStack() as ctx:
        sb, ps, sem, begin = phase_tools(nc, ctx)
        w = sb("pe_w", [K, C])
        rows = sb("pe_rows", [TP, 2, C])
        px = [sb(f"pe_px{u}", [K, TP * G]) for u in range(2)]
        xs = [sb(f"pe_xs{u}", [TP, G, C]) for u in range(2)]
        sq = [sb(f"pe_sq{u}", [TP, G, C]) for u in range(2)]
        y = [sb(f"pe_y{u}", [TP, G, C]) for u in range(2)]
        mean = [sb(f"pe_mean{u}", [TP, G]) for u in range(2)]
        var = [sb(f"pe_var{u}", [TP, G]) for u in range(2)]
        rstd = [sb(f"pe_rstd{u}", [TP, G]) for u in range(2)]
        half = sb("pe_half", [TP, G])
        psx = [ps(f"pe_psx{u}", [TP, 512]) for u in range(2)]

        consts = sem("pe_consts")
        half_set = sem("pe_half_set")
        loaded = [sem(f"pe_loaded{u}") for u in range(2)]
        embedded = [sem(f"pe_embedded{u}") for u in range(2)]
        chain = [sem(f"pe_chain{u}") for u in range(2)]
        var_ready = [sem(f"pe_var_ready{u}") for u in range(2)]
        rstd_ready = [sem(f"pe_rstd_ready{u}") for u in range(2)]
        y_ready = [sem(f"pe_y_ready{u}") for u in range(2)]
        stored = [sem(f"pe_stored{u}") for u in range(2)]
        CH = 7
        out_v = tokens.rearrange("(n g p) c -> n p g c", g=G, p=TP)
        begin()
        with nc.Block() as block:
            @block.sync
            def _(sp):
                sp.dma_start(w[:, :], w_patch).then_inc(consts, 16)
                sp.dma_start(rows[:, :, :], norm_rows).then_inc(consts, 16)
                with sp.Fori(0, NG // 2) as i:
                    for u in range(2):
                        sp.wait_ge(embedded[u], START + i)
                        sp.dma_start(px[u][:, :], patches[:, bass.ts(i * 2 + u, TP * G)]).then_inc(loaded[u], 16)

            @block.tensor
            def _(pe):
                pe.wait_ge(consts, START + 32)
                with pe.Fori(0, NG // 2) as i:
                    for u in range(2):
                        pe.wait_ge(loaded[u], START + 16 * i + 16)
                        pe.wait_ge(chain[u], START + CH * i)
                        for g in range(G):
                            last = nc.tensor.matmul(psx[u][:, g * C:(g + 1) * C], px[u][:, g * TP:(g + 1) * TP],
                                                    w[:, :], start=True, stop=True)
                        last.then_inc(embedded[u], 1)

            @block.vector
            def _(dve):
                dve.wait_ge(consts, START + 32)
                steps = [Steps(dve, chain[u], CH) for u in range(2)]
                with dve.Fori(0, NG // 2) as i:
                    for u in range(2):
                        steps[u].start(i)
                        x = psx[u][:, 0:G * C].rearrange("p (g c) -> p g c", c=C)
                        dve.wait_ge(embedded[u], START + i + 1)
                        centred_and_variance(nc, steps[u], x, xs[u][:, :, :], sq[u][:, :, :], mean[u][:, :],
                                             var[u][:, :], LN_EPS, var_ready[u])
                        dve.wait_ge(rstd_ready[u], START + i + 1)
                        steps[u].link(nc.vector.tensor_tensor(xs[u][:, :, :], xs[u][:, :, :], bcast(rstd[u][:, :], C), ALU.mult))
                        g_row = rows[:, 0, :].unsqueeze(1).to_broadcast([TP, G, C])
                        b_row = rows[:, 1, :].unsqueeze(1).to_broadcast([TP, G, C])
                        steps[u].link(nc.vector.tensor_tensor(xs[u][:, :, :], xs[u][:, :, :], g_row, ALU.mult))
                        dve.wait_ge(stored[u], START + 16 * i)
                        nc.vector.tensor_tensor(y[u][:, :, :], xs[u][:, :, :], b_row, ALU.add).then_inc(y_ready[u], 1)

            @block.gpsimd
            def _(pool):
                nc.gpsimd.memset(half[:, :], -0.5).then_inc(half_set, 1)
                pool.wait_ge(half_set, START + 1)
                with pool.Fori(0, NG // 2) as i:
                    for u in range(2):
                        pool.wait_ge(var_ready[u], START + i + 1)
                        nc.gpsimd.tensor_tensor(rstd[u][:, :], var[u][:, :], half[:, :], ALU.pow).then_inc(rstd_ready[u], 1)

            @block.scalar
            def _(act):
                with act.Fori(0, NG // 2) as i:
                    for u in range(2):
                        act.wait_ge(y_ready[u], START + i + 1)
                        act.dma_start(out_v[i * 2 + u], y[u][:, :, :]).then_inc(stored[u], 16)
                for u in range(2):
                    act.wait_ge(stored[u], START + 16 * (NG // 2))


class Row:

    def __init__(self, quad, u):
        self.quad, self.u = quad, u
        self.n = quad * 4 + u
        self.ring4, self.ring2 = u % 4, u % 2
        self.round4 = quad + u // 4
        self.round2 = quad * 2 + u // 2

    def next(self, d):
        return Row(self.quad, self.u + d)


def window_attention(nc, tag, image, offset, norm_cols, w_q, w_k, w_v, w_proj, bias, mask, n_kinds, head_mask, ident_in):
    K = C + 1
    PAIRS = 4
    HJ = SH * NW
    HP = SH // 2
    VW = 2 * SD + 2
    ALL = B * ROWS
    with ExitStack() as ctx:
        sb, ps, sem_, begin = phase_tools(nc, ctx)
        sem = lambda name: sem_(f"{tag}_{name}")
        nm = lambda name: f"{tag}_{name}"
        ident = sb(nm("ident"), [P, P])
        ncol = sb(nm("ncol"), [C, 2])
        wq, wk, wv, wp = (sb(nm(n), [K, C]) for n in ("wq", "wk", "wv", "wp"))
        hm = sb(nm("hm"), [C, SH])
        tab = sb(nm("tab"), [P, n_kinds, PAIRS, HJ])
        mtab = sb(nm("mtab"), [P, n_kinds, PAIRS, HJ]) if mask is not None else None
        n_consts = 8 + (mask is not None)
        half = sb(nm("half"), [P, PAIRS])
        x = [sb(nm(f"x{u}"), [P, PAIRS, C]) for u in range(4)]
        xs = sb(nm("xs"), [P, PAIRS, C])
        sq = sb(nm("sq"), [P, PAIRS, C])
        mean, var, rstd = (sb(nm(n), [P, PAIRS]) for n in ("mean", "var", "rstd"))
        ht = sb(nm("ht"), [K, PAIRS, P])
        qs = sb(nm("qs"), [C, PAIRS, P])
        kx = sb(nm("kx"), [C, 8, SH, NW])
        v2 = [sb(nm(f"v2_{u}"), [P, 8, HP, VW]) for u in range(2)]
        s = sb(nm("s"), [P, PAIRS, SH, NW])
        mx = sb(nm("mx"), [P, PAIRS, SH])
        pr = sb(nm("pr"), [P, PAIRS, SH, SLOT])
        pt = [sb(nm(f"pt{j}"), [P, HP, P]) for j in range(PAIRS)]
        rden = sb(nm("rden"), [P, PAIRS * HP, 2])
        on = sb(nm("on"), [P, PAIRS, C])
        ot = sb(nm("ot"), [K, PAIRS, P])
        y = [sb(nm(f"y{u}"), [P, PAIRS, C]) for u in range(2)]
        bank_t = ps(nm("bank_t"), [P, 512])
        bank_q = ps(nm("bank_q"), [P, 512])
        bank_k = ps(nm("bank_k"), [P, 512])
        bank_v = ps(nm("bank_v"), [P, 512])
        bank_s = ps(nm("bank_s"), [P, PAIRS, 512])

        consts, zeroed, tab_ready, taken = map(sem, ("consts", "zeroed", "tab_ready", "taken"))
        loaded = [sem(f"loaded{u}") for u in range(4)]
        stored = [sem(f"stored{u}") for u in range(2)]
        (norm_chain, soft_chain, div_chain, var_ready, rstd_ready, xn_ready, xt_ready, ht_ready, q_ready, k_ready,
         v_ready, qs_ready, kx_ready, v2_ready, s_ready, sub_ready, exp_ready, ptr_ready, pt_ready, weighed, on_ready,
         ot_ps_ready, ot_ready, y_ps_ready, y_ready) = map(sem, (
             "norm_chain", "soft_chain", "div_chain", "var_ready", "rstd_ready", "xn_ready", "xt_ready", "ht_ready",
             "q_ready", "k_ready", "v_ready", "qs_ready", "kx_ready", "v2_ready", "s_ready", "sub_ready", "exp_ready",
             "ptr_ready", "pt_ready", "weighed", "on_ready", "ot_ps_ready", "ot_ready", "y_ps_ready", "y_ready"))
        FILLS = 14

        def window_row(b, r):
            rows = image[b, bass.ds(r * WIN + offset, WIN), offset:offset + SIDE, :]
            v = rows.rearrange("r (p two c) ch -> two p r c ch", two=2, c=WIN)
            return [(h, p, v[h, p]) for h in range(2) for p in range(PAIRS)]

        def all_steps(eng, step):
            step(Row(0, 0), 0)
            with eng.Fori(0, B - 1) as b:
                with eng.Fori(0, 2) as j:
                    for u in range(1, 5):
                        step(Row(b * 2 + j, u), j if u == 3 and n_kinds == 2 else 0)
            for u in range(1, ROWS):
                step(Row((B - 1) * 2, u), (n_kinds - 1) * (u == ROWS - 1))

        def exists(row):
            return not isinstance(row.n, int) or 0 <= row.n < ALL

        begin()
        with nc.Block() as block:
            @block.sync
            def _(sp):
                def load(b, r):
                    for h, p, view in window_row(b, r):
                        sp.dma_start(x[r % 4][SLOT * h:SLOT * h + NW, p, :], view).then_inc(loaded[r % 4], 16)

                def store(b, r):
                    sp.wait_ge(y_ready, START + b * ROWS + r + 1)
                    for h, p, view in window_row(b, r):
                        sp.dma_start(view, y[r % 2][SLOT * h:SLOT * h + NW, p, :]).then_inc(stored[r % 2], 16)

                for dst, src in ((ident[:, :], ident_in), (ncol[:, :], norm_cols), (wq[:, :], w_q), (wk[:, :], w_k),
                                 (wv[:, :], w_v), (wp[:, :], w_proj), (hm[:, :], head_mask),
                                 (tab[:, :, :, :], bias.rearrange("k p w n -> p k w n"))):
                    sp.dma_start(dst, src).then_inc(consts, 16)
                if mask is not None:
                    sp.dma_start(mtab[:, :, :, :], mask.rearrange("k p w n -> p k w n")).then_inc(consts, 16)
                sp.wait_ge(zeroed, START + 4)
                for r in range(4):
                    load(0, r)
                with sp.Fori(0, B - 1) as b:
                    for r in range(ROWS):
                        store(b, r)
                        load(b + (r + 4) // ROWS, (r + 4) % ROWS)
                for r in range(ROWS):
                    store(B - 1, r)
                    if r + 4 < ROWS:
                        load(B - 1, r + 4)
                for u in range(2):
                    sp.wait_ge(stored[u], START + 16 * 8 * ALL // 2)

            @block.gpsimd
            def _(pool):
                fills = ([(t[:, :, :], 0.0) for t in x] + [(pr[:, :, :, :], 0.0), (half[:, :], -0.5),
                         (ht[C:K, :, :], 1.0), (ot[C:K, :, :], 1.0)] + [(t[:, :, :, :], 0.0) for t in v2]
                         + [(t[0:SLOT, :, :, 2 * SD:2 * SD + 1], 1.0) for t in v2])
                fills += [(t[SLOT:P, :, :, 2 * SD + 1:VW], 1.0) for t in v2]
                assert len(fills) == FILLS
                for n, (dst, value) in enumerate(fills):
                    pool.wait_ge(zeroed, START + n)
                    nc.gpsimd.memset(dst, value).then_inc(zeroed, 1)

                with pool.Fori(0, ALL) as i:
                    pool.wait_ge(var_ready, START + i + 1)
                    nc.gpsimd.tensor_tensor(rstd[:, :], var[:, :], half[:, :], ALU.pow).then_inc(rstd_ready, 1)

            @block.vector
            def _(dve):
                norm_steps, soft_steps, div_steps = Steps(dve, norm_chain, 5), Steps(dve, soft_chain, 2), Steps(dve, div_chain, 1)

                def centre(row):
                    norm_steps.start(row.n)
                    dve.wait_ge(loaded[row.ring4], START + 16 * 8 * (row.round4 + 1))
                    centred_and_variance(nc, norm_steps, x[row.ring4][:, :, :], xs[:, :, :], sq[:, :, :], mean[:, :],
                                         var[:, :], LN_EPS, var_ready)

                def scale(row):
                    dve.wait_ge(rstd_ready, START + row.n + 1)
                    nc.vector.tensor_tensor(xs[:, :, :], xs[:, :, :], bcast(rstd[:, :], C), ALU.mult).then_inc(xn_ready, 1)

                def spread_keys(row):
                    dve.wait_ge(k_ready, START + row.n + 1)
                    kp = bank_k[0:C, :].rearrange("c (w j) -> c w j", j=SLOT)
                    for w in range(8):
                        ins = nc.vector.tensor_tensor(kx[:, w, :, :], kp[:, w, 0:NW].unsqueeze(1).to_broadcast([C, SH, NW]),
                                                      bcast(hm[:, :], NW), ALU.mult)
                    ins.then_inc(kx_ready, 1)

                def softmax(row, kind):
                    soft_steps.start(row.n)
                    dve.wait_ge(s_ready, START + row.n + 1)
                    flat = s[:, :, :, :].rearrange("p w h j -> p w (h j)")
                    t = tab[:, kind, :, :] if isinstance(kind, int) else tab[:, bass.ds(kind, 1), :, :].rearrange("p k w n -> p (k w) n")
                    soft_steps.link(nc.vector.tensor_tensor(flat, bank_s[:, :, 0:HJ], t, ALU.add))
                    soft_steps.link(nc.vector.reduce_max(mx[:, :, :], s[:, :, :, :], AX.X))
                    nc.vector.tensor_tensor(s[:, :, :, :].rearrange("p w h j -> p (w h) j"), s[:, :, :, :].rearrange("p w h j -> p (w h) j"),
                                            bcast(mx[:, :, :].rearrange("p w h -> p (w h)"), NW), ALU.subtract).then_inc(sub_ready, 1)

                def divide(row):
                    div_steps.start(row.n)
                    dve.wait_ge(weighed, START + PAIRS * (row.n + 1))
                    o = bank_q[:, 0:PAIRS * HP * VW].rearrange("p (a v) -> p a v", v=VW)
                    div_steps.link(nc.vector.reciprocal(rden[:, :, :], o[:, :, 2 * SD:VW]))
                    for e in range(2):
                        src = o[:, :, e * SD:(e + 1) * SD]
                        dst = on[:, :, :].rearrange("p w (a two d) -> p (w a) two d", two=2, d=SD)[:, :, e, :]
                        ins = nc.vector.tensor_tensor(dst, src, bcast(rden[:, :, e], SD), ALU.mult)
                    ins.then_inc(on_ready, 1)

                def add_residual(row):
                    dve.wait_ge(y_ps_ready, START + row.n + 1)
                    dve.wait_ge(stored[row.ring2], START + 16 * 8 * row.round2)
                    yp = bank_t[:, 0:PAIRS * C].rearrange("p (w c) -> p w c", c=C)
                    nc.vector.tensor_tensor(y[row.ring2][:, :, :], yp, x[row.ring4][:, :, :], ALU.add).then_inc(y_ready, 1)

                def step(row, kind):
                    softmax(row, kind)
                    if row.u > 0:
                        add_residual(row.next(-1))
                    if exists(row.next(1)):
                        spread_keys(row.next(1))
                    if exists(row.next(2)):
                        centre(row.next(2))
                    divide(row)
                    if exists(row.next(2)):
                        scale(row.next(2))

                dve.wait_ge(consts, START + 16 * n_consts)
                dve.wait_ge(zeroed, START + FILLS)
                if mask is not None:
                    nc.vector.tensor_tensor(tab[:, :, :, :], tab[:, :, :, :], mtab[:, :, :, :], ALU.add).then_inc(tab_ready, 1)
                    dve.wait_ge(tab_ready, START + 1)
                centre(Row(0, 0))
                scale(Row(0, 0))
                spread_keys(Row(0, 0))
                centre(Row(0, 1))
                scale(Row(0, 1))
                all_steps(dve, step)
                add_residual(Row(0, ALL - 1))

            @block.tensor
            def _(pe):
                def settled():
                    pe.sem_inc(taken, 1)

                def transpose_input(row):
                    pe.wait_ge(xn_ready, START + row.n + 1)
                    settled()
                    for p in range(PAIRS):
                        ins = nc.tensor.transpose(bank_k[0:C, p * P:(p + 1) * P], xs[:, p, :], ident[:, :])
                    ins.then_inc(xt_ready, 1)

                def embed(row):
                    pe.wait_ge(ht_ready, START + row.n + 1)
                    pe.wait_ge(v2_ready, START + row.n)
                    settled()
                    flat = ht[:, :, :].rearrange("k w t -> k (w t)")
                    nc.tensor.matmul(bank_q[0:C, :], wq[:, :], flat, start=True, stop=True).then_inc(q_ready, 1)
                    nc.tensor.matmul(bank_k[0:C, :], wk[:, :], flat, start=True, stop=True).then_inc(k_ready, 1)
                    for w in range(8):
                        for h in range(2):
                            ins = nc.tensor.matmul(bank_v[SLOT * h:SLOT * (h + 1), w * C:(w + 1) * C],
                                                   ht[:, w // 2, SLOT * (w % 2):SLOT * (w % 2) + SLOT], wv[:, :],
                                                   start=True, stop=True)
                    ins.then_inc(v_ready, 1)

                def scores(row):
                    pe.wait_ge(qs_ready, START + row.n + 1)
                    pe.wait_ge(kx_ready, START + row.n + 1)
                    pe.wait_ge(pt_ready, START + PAIRS * row.n)
                    settled()
                    for w in range(8):
                        lo = SLOT * (w % 2)
                        ins = nc.tensor.matmul(bank_s[lo:lo + SLOT, w // 2, 0:HJ], qs[:, w // 2, lo:lo + SLOT],
                                               kx[:, w, :, :].rearrange("c h j -> c (h j)"), start=True, stop=True)
                    ins.then_inc(s_ready, 1)

                def weigh(row, more):
                    def turned(p):
                        pe.wait_ge(pt_ready, START + PAIRS * row.n + p + 1)
                        settled()
                        for h in range(2):
                            for a in range(HP):
                                col = (p * HP + a) * VW
                                ins = nc.tensor.matmul(bank_q[SLOT * h:SLOT * (h + 1), col:col + VW],
                                                       pt[p][:, a, SLOT * h:SLOT * (h + 1)], v2[row.ring2][:, 2 * p + h, a, :],
                                                       start=True, stop=True)
                        ins.then_inc(weighed, 1)

                    pe.wait_ge(exp_ready, START + row.n + 1)
                    pe.wait_ge(v2_ready, START + row.n + 1)
                    if more:
                        pe.wait_ge(qs_ready, START + row.n + 2)
                    settled()
                    for p in range(PAIRS):
                        for a in range(HP):
                            ins = nc.tensor.transpose(bank_s[:, p, a * P:(a + 1) * P],
                                                      pr[:, p, 2 * a:2 * a + 2, :].rearrange("p h j -> p (h j)"), ident[:, :])
                        ins.then_inc(ptr_ready, 1)
                        if p >= 1:
                            turned(p - 1)
                    turned(PAIRS - 1)

                def transpose_output(row):
                    pe.wait_ge(on_ready, START + row.n + 1)
                    pe.wait_ge(y_ready, START + row.n)
                    settled()
                    for p in range(PAIRS):
                        ins = nc.tensor.transpose(bank_t[0:C, p * P:(p + 1) * P], on[:, p, :], ident[:, :])
                    ins.then_inc(ot_ps_ready, 1)

                def project(row):
                    pe.wait_ge(ot_ready, START + row.n + 1)
                    settled()
                    for p in range(PAIRS):
                        ins = nc.tensor.matmul(bank_t[:, p * C:(p + 1) * C], ot[:, p, :], wp[:, :], start=True, stop=True)
                    ins.then_inc(y_ps_ready, 1)

                def step(row, kind):
                    more = exists(row.next(1))
                    scores(row)
                    if row.u > 0:
                        transpose_output(row.next(-1))
                    if more:
                        transpose_input(row.next(1))
                    if row.u > 0:
                        project(row.next(-1))
                    if more:
                        embed(row.next(1))
                    weigh(row, more)

                pe.wait_ge(consts, START + 16 * n_consts)
                pe.wait_ge(zeroed, START + FILLS)
                transpose_input(Row(0, 0))
                embed(Row(0, 0))
                all_steps(pe, step)
                transpose_output(Row(0, ALL - 1))
                project(Row(0, ALL - 1))

            @block.scalar
            def _(act):
                def normed(row):
                    act.wait_ge(xt_ready, START + row.n + 1)
                    act.wait_ge(v_ready, START + row.n)
                    nc.scalar.activation(ht[0:C, :, :].rearrange("c w t -> c (w t)"), bank_k[0:C, :], ACT.Identity,
                                         bias=ncol[:, 1:2], scale=ncol[:, 0:1]).then_inc(ht_ready, 1)

                def queries(row):
                    act.wait_ge(q_ready, START + row.n + 1)
                    act.wait_ge(s_ready, START + row.n)
                    nc.scalar.activation(qs[:, :, :].rearrange("c w t -> c (w t)"), bank_q[0:C, :], ACT.Copy,
                                         scale=float(SD) ** -0.5).then_inc(qs_ready, 1)

                def values(row):
                    act.wait_ge(v_ready, START + row.n + 1)
                    for e in range(2):
                        src = bank_v[SLOT * e:SLOT * (e + 1), :].rearrange("p (w a two d) -> p (w a) two d", w=8, a=HP, two=2)[:, :, e, :]
                        dst = v2[row.ring2][SLOT * e:SLOT * (e + 1), :, :, e * SD:(e + 1) * SD].rearrange("p w a d -> p (w a) d")
                        ins = nc.scalar.activation(dst, src, ACT.Copy)
                    ins.then_inc(v2_ready, 1)

                def exponentiate(row):
                    act.wait_ge(sub_ready, START + row.n + 1)
                    act.wait_ge(weighed, START + PAIRS * row.n)
                    nc.scalar.activation(pr[:, :, :, 0:NW].rearrange("p w h j -> p (w h) j"),
                                         s[:, :, :, :].rearrange("p w h j -> p (w h) j"), ACT.Exp).then_inc(exp_ready, 1)

                def turn(row):
                    for p in range(PAIRS):
                        act.wait_ge(ptr_ready, START + PAIRS * row.n + p + 1)
                        nc.scalar.activation(pt[p][:, :, :].rearrange("p a t -> p (a t)"), bank_s[:, p, :], ACT.Copy).then_inc(pt_ready, 1)

                def outputs(row):
                    act.wait_ge(ot_ps_ready, START + row.n + 1)
                    act.wait_ge(y_ps_ready, START + row.n)
                    nc.scalar.activation(ot[0:C, :, :].rearrange("c w t -> c (w t)"), bank_t[0:C, :], ACT.Copy).then_inc(ot_ready, 1)

                def step(row, kind):
                    if row.u > 0:
                        outputs(row.next(-1))
                    if exists(row.next(1)):
                        normed(row.next(1))
                        queries(row.next(1))
                    exponentiate(row)
                    if exists(row.next(1)):
                        values(row.next(1))
                    turn(row)

                act.wait_ge(consts, START + 16 * n_consts)
                act.wait_ge(zeroed, START + FILLS)
                normed(Row(0, 0))
                queries(Row(0, 0))
                values(Row(0, 0))
                all_steps(act, step)
                outputs(Row(0, ALL - 1))


def mlp(nc, tag, src, dst, norm_cols, w_1, w_2, b_2, ident_in):
    TP, G = 112, 4
    NG = B * TOK // (TP * G)
    K, HK = C + 1, 4 * C // P
    with ExitStack() as ctx:
        sb, ps, sem_, begin = phase_tools(nc, ctx)
        sem = lambda name: sem_(f"{tag}_{name}")
        two = lambda name: [sem(f"{name}{u}") for u in range(2)]
        nm = lambda name: f"{tag}_{name}"
        ident = sb(nm("ident"), [P, P])
        ncol = sb(nm("ncol"), [C, 2])
        w1 = sb(nm("w1"), [K, HK, P])
        w2 = sb(nm("w2"), [P, HK, C])
        b2 = sb(nm("b2"), [1, C])
        ones = sb(nm("ones"), [1, TP])
        half = sb(nm("half"), [TP, G])
        pairs = lambda name, shape: [sb(nm(f"{name}{u}"), shape) for u in range(2)]
        x, xs, sq, y = (pairs(n, [TP, G, C]) for n in ("x", "xs", "sq", "y"))
        mean, var, rstd = (pairs(n, [TP, G]) for n in ("mean", "var", "rstd"))
        ht = pairs("ht", [K, G * TP])
        act_h = pairs("act_h", [P, HK, G * TP])
        ps_t = [ps(nm(f"ps_t{u}"), [P, 512]) for u in range(2)]
        ps_h = [ps(nm(f"ps_h{u}"), [P, HK, 512]) for u in range(2)]
        ps_y = [ps(nm(f"ps_y{u}"), [P, 512]) for u in range(2)]
        consts, filled, taken = sem("consts"), sem("filled"), sem("taken")
        (loaded, stored, chain, var_ready, rstd_ready, xn_ready, xt_ready, ht_ready, h_ready, act_ready, y_ps_ready,
         y_ready) = map(two, ("loaded", "stored", "chain", "var_ready", "rstd_ready", "xn_ready", "xt_ready", "ht_ready",
                              "h_ready", "act_ready", "y_ps_ready", "y_ready"))
        CH = 5
        FILLS = 4
        begin()
        with nc.Block() as block:
            @block.sync
            def _(sp):
                for d, a in ((ident[:, :], ident_in), (ncol[:, :], norm_cols), (w1[:, :, :], w_1.rearrange("k (h p) -> k h p", p=P)),
                             (w2[:, :, :], w_2), (b2[:, :], b_2)):
                    sp.dma_start(d, a).then_inc(consts, 16)
                with sp.Fori(0, NG // 2) as i:
                    for u in range(2):
                        sp.wait_ge(y_ready[u], START + i)
                        sp.dma_start(x[u][:, :, :], src[i * 2 + u]).then_inc(loaded[u], 16)

            @block.gpsimd
            def _(pool):
                for n, (d, value) in enumerate(((half[:, :], -0.5), (ones[:, :], 1.0), (ht[0][C:K, :], 1.0), (ht[1][C:K, :], 1.0))):
                    pool.wait_ge(filled, START + n)
                    nc.gpsimd.memset(d, value).then_inc(filled, 1)
                pool.wait_ge(filled, START + FILLS)
                with pool.Fori(0, NG // 2) as i:
                    for u in range(2):
                        pool.wait_ge(var_ready[u], START + i + 1)
                        nc.gpsimd.tensor_tensor(rstd[u][:, :], var[u][:, :], half[:, :], ALU.pow).then_inc(rstd_ready[u], 1)

            @block.vector
            def _(dve):
                dve.wait_ge(consts, START + 16 * 5)
                dve.wait_ge(filled, START + FILLS)
                steps = [Steps(dve, chain[u], CH) for u in range(2)]

                def normalise(i, u):
                    steps[u].start(i)
                    dve.wait_ge(loaded[u], START + 16 * i + 16)
                    centred_and_variance(nc, steps[u], x[u][:, :, :], xs[u][:, :, :], sq[u][:, :, :], mean[u][:, :],
                                         var[u][:, :], LN_EPS, var_ready[u])

                def scale(i, u):
                    dve.wait_ge(rstd_ready[u], START + i + 1)
                    nc.vector.tensor_tensor(xs[u][:, :, :], xs[u][:, :, :], bcast(rstd[u][:, :], C), ALU.mult).then_inc(xn_ready[u], 1)

                def affine(i, u):
                    dve.wait_ge(xt_ready[u], START + i + 1)
                    dve.wait_ge(h_ready[u], START + i)
                    nc.vector.tensor_scalar(ht[u][0:C, :], ps_t[u][0:C, 0:G * TP], ncol[:, 0:1], ncol[:, 1:2],
                                            ALU.mult, ALU.add).then_inc(ht_ready[u], 1)

                def residual(i, u):
                    dve.wait_ge(y_ps_ready[u], START + i + 1)
                    dve.wait_ge(stored[u], START + 16 * i)
                    nc.vector.tensor_tensor(y[u][:, :, :], ps_y[u][0:TP, 0:G * C].rearrange("p (g c) -> p g c", c=C),
                                            x[u][:, :, :], ALU.add).then_inc(y_ready[u], 1)
                with dve.Fori(0, NG // 2) as i:
                    normalise(i, 0)
                    normalise(i, 1)
                    scale(i, 0)
                    scale(i, 1)
                    affine(i, 0)
                    affine(i, 1)
                    residual(i, 0)
                    residual(i, 1)

            @block.tensor
            def _(pe):
                pe.wait_ge(consts, START + 16 * 5)
                pe.wait_ge(filled, START + FILLS)

                def turn(i, u):
                    pe.wait_ge(xn_ready[u], START + i + 1)
                    pe.sem_inc(taken, 1)
                    for g in range(G):
                        ins = nc.tensor.transpose(ps_t[u][0:C, g * TP:(g + 1) * TP], xs[u][:, g, :], ident[0:TP, 0:TP])
                    ins.then_inc(xt_ready[u], 1)

                def up(i, u):
                    pe.wait_ge(ht_ready[u], START + i + 1)
                    for k in range(HK):
                        ins = nc.tensor.matmul(ps_h[u][:, k, 0:G * TP], w1[:, k, :], ht[u][:, :], start=True, stop=True)
                    ins.then_inc(h_ready[u], 1)

                def down(i, u):
                    pe.wait_ge(act_ready[u], START + i + 1)
                    for g in range(G):
                        out = ps_y[u][0:TP, g * C:(g + 1) * C]
                        for k in range(HK):
                            nc.tensor.matmul(out, act_h[u][:, k, g * TP:(g + 1) * TP], w2[:, k, :], start=(k == 0), stop=False)
                        ins = nc.tensor.matmul(out, ones[:, :], b2[:, :], start=False, stop=True)
                    ins.then_inc(y_ps_ready[u], 1)
                with pe.Fori(0, NG // 2) as i:
                    turn(i, 0)
                    turn(i, 1)
                    up(i, 0)
                    up(i, 1)
                    down(i, 0)
                    down(i, 1)

            @block.scalar
            def _(act):
                act.wait_ge(consts, START + 16 * 5)
                act.wait_ge(filled, START + FILLS)
                with act.Fori(0, NG // 2) as i:
                    for u in range(2):
                        act.wait_ge(h_ready[u], START + i + 1)
                        nc.scalar.activation(act_h[u][:, :, :], ps_h[u][:, :, 0:G * TP], ACT.Gelu).then_inc(act_ready[u], 1)
                    for u in range(2):
                        act.wait_ge(y_ready[u], START + i + 1)
                        act.dma_start(dst[i * 2 + u], y[u][:, :, :]).then_inc(stored[u], 16)
                for u in range(2):
                    act.wait_ge(stored[u], START + 16 * (NG // 2))


def copies(nc, tag, pairs):
    with ExitStack() as ctx:
        _, _, sem, begin = phase_tools(nc, ctx)
        done = sem(f"{tag}_done")
        begin()
        with nc.Block() as block:
            @block.sync
            def _(sp):
                n = 0
                for step in pairs:
                    for to, frm in step:
                        sp.dma_start(to, frm).then_inc(done, 16)
                        n += 16
                    sp.wait_ge(done, START + n)


Q_PART = (0, 0, 1, 1, 0, 2)
K_PART = (0, 1, 0, 1, 2, 0)
LIMIT = 43.0
RING = 3
PROBS = 3


class Core:

    def __init__(self, nc, sb, ps, sem, dim):
        self.nc, self.dim = nc, dim
        self.ring = ps("ring", [P, RING, 2, 512])
        self.acc = ps("acc", [P, 512])
        self.turned = ps("turned", [P, 512])
        self.pb = [sb(f"probs{n}", [P, 4, QW]) for n in range(PROBS)]
        self.acc_sb = sb("acc_sb", [P, QW])
        self.rec = sb("rec", [P, QW // P, 4])
        self.taken, self.taken_dve = sem("taken"), sem("taken_dve")
        (self.scores_ready, self.exp_done, self.weighed, self.acc_copied, self.acc_turned, self.rec_done,
         self.block_done) = map(sem, ("scores_ready", "exp_done", "weighed", "acc_copied", "acc_turned", "rec_done",
                                      "block_done"))

        self.flag = sb("flag", [P, 1], U32)
        self.bound_part, self.bound_most = sb("bound_part", [P, 1]), sb("bound_most", [P, 1])
        self.row_max = sb("row_max", [P, 2])
        self.neg_max, self.neg_rest = sb("neg_max", [P, 1]), sb("neg_rest", [P, 1])
        (self.bound_part_ready, self.bound_most_ready, self.flag_ready, self.cleared, self.row_scores, self.row_read,
         self.row_step) = map(sem, ("bound_part_ready", "bound_most_ready", "flag_ready", "cleared",
                                         "row_scores", "row_read", "row_step"))

    def find_flag(self, dve, b, bound, shift_slots):
        nc = self.nc
        nc.vector.reduce_max(self.bound_part[:, :], bound, AX.XY).then_inc(self.bound_part_ready, 1)
        nc.vector.memset(shift_slots, 0.0).then_inc(self.cleared, 1)
        dve.wait_ge(self.bound_most_ready, START + b + 1)
        nc.vector.tensor_scalar(self.flag[:, :], self.bound_most[:, :], LIMIT, None, ALU.is_gt).then_inc(self.flag_ready, 1)
        dve.wait_ge(self.flag_ready, START + b + 1)
        dve.wait_ge(self.cleared, START + b + 1)
        dve.sem_inc(self.taken_dve, 1)

    def read_flag(self, eng):
        return eng.value_load(self.flag[0:1, 0:1], min_val=0, max_val=1)

    def widest_bound(self, pool, b):
        pool.wait_ge(self.bound_part_ready, START + b + 1)
        pool.sem_inc(self.taken, 1)
        self.nc.gpsimd.partition_all_reduce(self.bound_most[:, :], self.bound_part[:, :], P,
                                            bass.bass_isa.ReduceOp.max).then_inc(self.bound_most_ready, 1)

    def tensor_row_scores(self, pe, count, q_tile, keys_of, n_keys):
        pe.wait_ge(self.row_read, START + count)
        pe.sem_inc(self.taken, 1)
        flat = self.ring[:, :, :, :].rearrange("p a b c -> p (a b c)")
        for k0 in range(0, n_keys, 512):
            k1 = min(k0 + 512, n_keys)
            out = flat[:, k0:k1] if k0 < 3072 else self.turned[:, 0:k1 - k0]
            ins = self.nc.tensor.matmul(out, q_tile, keys_of(k0, k1), start=True, stop=True)
        ins.then_inc(self.row_scores, 1)

    def vector_row_max(self, dve, count, n_keys, shift, later=None, diagonal=None):
        v = self.nc.vector
        STEPS = 7
        done = [0]

        def link(ins):
            ins.then_inc(self.row_step, 1)
            done[0] += 1
            dve.wait_ge(self.row_step, START + STEPS * count + done[0])

        dve.wait_ge(self.row_scores, START + count + 1)
        flat = self.ring[:, :, :, :].rearrange("p a b c -> p (a b c)")
        edge = 3072 if later is None else n_keys // P * P - (P if n_keys % P == 0 else 0)
        tail = self.turned[:, 0:n_keys - edge] if edge == 3072 else flat[:, edge:n_keys]
        if later is not None:
            link(v.tensor_tensor(diagonal[:, 0:n_keys - edge], tail, later[:, 0:n_keys - edge], ALU.add))
            tail = diagonal[:, 0:n_keys - edge]
        else:
            link(v.memset(self.neg_rest[:, :], 0.0))
        if edge:
            v.reduce_max(self.row_max[:, 0:1], flat[:, 0:edge], AX.X)
        else:
            v.reduce_max(self.row_max[:, 0:1], tail, AX.X)
        link(v.reduce_max(self.row_max[:, 1:2], tail, AX.X))
        link(v.reduce_max(self.neg_max[:, :], self.row_max[:, :], AX.X, negate=True))
        link(v.tensor_copy(shift(0), self.neg_max[:, :]))
        link(v.tensor_tensor(self.neg_rest[:, :], self.neg_max[:, :], shift(0), ALU.subtract))
        link(v.tensor_copy(shift(1), self.neg_rest[:, :]))
        link(v.tensor_tensor(self.neg_rest[:, :], self.neg_rest[:, :], shift(1), ALU.subtract))
        v.tensor_copy(shift(2), self.neg_rest[:, :]).then_inc(self.row_read, 1)

    def keys(self, kt):
        return LAST if kt == TILES - 1 else P

    def tensor(self, pe, nb, units, spans, kt_of, q_of, v_of, width, ident, ident_b=None, later_b=None):
        nc = self.nc

        def weigh(kt, first, diagonal):
            if kt == 0:
                pe.wait_ge(self.acc_copied, START + nb)
            pe.wait_ge(self.exp_done, START + 2 * units + 2 * kt + 2)
            pe.sem_inc(self.taken, 1)
            for h in range(4):
                ins = nc.tensor.matmul(self.acc[32 * h:32 * h + self.dim + 1, first:width], v_of(kt, h),
                                       self.pb[kt % PROBS][0:self.keys(kt), h, first:width],
                                       start=(kt == 0), stop=(diagonal or kt == len(spans) - 1),
                                       skip_group_check=first > 0)
            ins.then_inc(self.weighed, 1)

        for kt, (first, diagonal) in enumerate(spans):
            for half in range(2):
                n = 2 * kt + half
                pe.wait_ge(self.exp_done, START + 2 * units + max(n - RING + 1, 0))
                for h in (2 * half, 2 * half + 1):
                    ins = nc.tensor.matmul(self.ring[0:self.keys(kt), n % RING, h % 2, first:width], kt_of(kt, h),
                                           q_of(h, first), start=True, stop=True)
                    if diagonal:
                        ins = nc.tensor.matmul(self.ring[0:self.keys(kt), n % RING, h % 2, first:first + P],
                                               ident_b[:, 0:self.keys(kt)], later_b, start=False, stop=True,
                                               skip_group_check=True)
                ins.then_inc(self.scores_ready, 1)
            if kt:
                weigh(kt - 1, *spans[kt - 1])
        weigh(kt, *spans[kt])
        pe.wait_ge(self.acc_copied, START + nb + 1)
        pe.wait_ge(self.block_done, START + nb)
        for t in range(width // P):
            ins = nc.tensor.transpose(self.turned[:, t * P:(t + 1) * P], self.acc_sb[:, t * P:(t + 1) * P], ident)
        ins.then_inc(self.acc_turned, 1)

    def scalar(self, act, nb, units, spans, width):
        for kt, (first, diagonal) in enumerate(spans):
            for half in range(2):
                n = 2 * kt + half
                act.wait_ge(self.scores_ready, START + 2 * units + n + 1)
                act.wait_ge(self.weighed, START + units + max(kt - PROBS + 1, 0))
                keys = self.keys(kt)
                self.nc.scalar.activation(self.pb[kt % PROBS][0:keys, 2 * half:2 * half + 2, first:width],
                                          self.ring[0:keys, n % RING, :, first:width], ACT.Exp).then_inc(self.exp_done, 1)

    def vector(self, dve, nb, units_after, width, out):
        nc = self.nc
        tiles = width // P
        dve.wait_ge(self.weighed, START + units_after)
        dve.wait_ge(self.acc_turned, START + nb)
        nc.vector.tensor_copy(self.acc_sb[:, 0:width], self.acc[:, 0:width]).then_inc(self.acc_copied, 1)
        dve.wait_ge(self.acc_turned, START + nb + 1)
        turned = self.turned[:, 0:width].rearrange("p (t h r) -> p t h r", h=4, r=32)
        nc.vector.reciprocal(self.rec[:, 0:tiles, :], turned[:, :, :, self.dim]).then_inc(self.rec_done, 1)
        dve.wait_ge(self.rec_done, START + nb + 1)
        for t in range(tiles):
            ins = nc.vector.tensor_tensor(out(t), turned[:, t, :, 0:self.dim], bcast(self.rec[:, t, :], self.dim), ALU.mult)
        ins.then_inc(self.block_done, 1)


def dense_attention(nc, src, dst, w_qkv, w_proj, ident_in):
    tag = "da"
    H, D = 16, 4
    HG = H // 4
    K = C + 1
    BLOCKS = QBLOCKS + 1
    ALL = [(0, False)] * TILES
    with ExitStack() as ctx:
        sb_, ps_, sem_, begin = phase_tools(nc, ctx)
        sb = lambda name, shape, dt=F32: sb_(f"{tag}_{name}", shape, dt)
        ps = lambda name, shape: ps_(f"{tag}_{name}", shape)
        sem = lambda name: sem_(f"{tag}_{name}")
        ident = sb("ident", [P, P])
        ident_b = sb("ident_b", [P, P], BF16)
        wqkv, wp = sb("wqkv", [K, 3 * C]), sb("wp", [K, C])
        x = sb("x", [P, TILES, C])
        xs, sq = sb("xs", [P, GT, C]), sb("sq", [P, GT, C])
        mean, var, rstd, half = (sb(n, [P, GT]) for n in ("mean", "var", "rstd", "half"))
        ht = sb("ht", [K, GT * P])
        parts = [sb(f"part{n}", [P, GT, 2 * C], BF16) for n in range(3)]
        rest = sb("rest", [P, GT, 2 * C])
        qk = sb("qk", [P, GT, 2 * C])
        squares = sb("squares", [P, GT, 2 * C])
        norm2 = sb("norm2", [P, TILES, 2 * H])
        k_part, k_most = sb("k_part", [P, H]), sb("k_most", [P, H])
        bound = sb("bound", [P, TILES, H])
        slots = [sb(f"slots_{n}", [P, TILES, H, 32], BF16) for n in ("q", "k")]
        qt = sb("qt", [P, 4, SEQP], BF16)
        kt = sb("kt", [P, SEQP], BF16)
        v = sb("v", [P, TILES, H, D + 1])
        rstd_spare = sb("rstd_spare", [1, 1])
        vg = sb("vg", [P, TILES, 4, D + 1])
        o = sb("o", [P, TILES, C])
        ot = sb("ot", [K, GT * P])
        y = sb("y", [P, GT, C])
        core = Core(nc, sb, ps, sem, D)
        flat_ring = core.ring[:, :, :, :].rearrange("p a b c -> p (a b c)")
        ps_t = flat_ring[:, 0:GT * P]
        ps_qkv = flat_ring[:, 1024:2560].rearrange("p (t c) -> p t c", c=256)
        ps_turn = [flat_ring[:, 0:GT * P], flat_ring[:, 1024:1024 + GT * P]]
        ps_y = flat_ring[:, 2560:2560 + GT * C].rearrange("p (t c) -> p t c", c=C)

        (consts, filled, ident_b_ready, zeroed_acc, loaded, chain, var_ready, rstd_ready, xn_ready, xt_ready, ht_ready,
         qkv_ready, qk_ready, part0_ready, part1_ready, rest_ready, squares_ready, v_ready, parts_ready, slots_ready,
         k_part_ready, k_most_ready, product_ready, bound_ready, shift_ready, turn_ready, turned_out, row_turn_ready, row_turned_out, vg_ready,
         ot_ps_ready, ot_ready, y_ps_ready, y_ready, stored) = map(sem, (
             "consts", "filled", "ident_b_ready", "zeroed_acc", "loaded", "chain", "var_ready", "rstd_ready",
             "xn_ready", "xt_ready", "ht_ready", "qkv_ready", "qk_ready", "part0_ready", "part1_ready", "rest_ready",
             "squares_ready", "v_ready", "parts_ready", "slots_ready", "k_part_ready", "k_most_ready",
             "product_ready", "bound_ready", "shift_ready", "turn_ready", "turned_out", "row_turn_ready",
             "row_turned_out", "vg_ready", "ot_ps_ready",
             "ot_ready", "y_ps_ready", "y_ready", "stored"))
        CH = 5
        tile_view = lambda a, b: a[b].rearrange("(t p) c -> p t c", p=P)
        fills = [(half[:, :], -0.5), (ht[C:K, :], 1.0), (ot[C:K, :], 1.0), (v[:, :, :, D:D + 1], 1.0), (qt[:, :, :], 0.0),
                 (kt[:, :], 0.0), (slots[0][:, :, :, :], 0.0), (slots[1][:, :, :, :], 0.0),
                 (slots[1][:, :, :, 24:27], 1.0)]
        FILLS = len(fills)

        begin()
        with nc.Block() as block:
            @block.sync
            def _(sp):
                for d, a in ((ident[:, :], ident_in), (wqkv[:, :], w_qkv), (wp[:, :], w_proj)):
                    sp.dma_start(d, a).then_inc(consts, 16)
                with sp.Fori(0, B) as b:
                    sp.wait_ge(y_ready, START + GROUPS * b)
                    sp.dma_start(x[:, :, :], tile_view(src, b)).then_inc(loaded, 16)

            @block.gpsimd
            def _(pool):
                for n, (d, value) in enumerate(fills):
                    pool.wait_ge(filled, START + n)
                    nc.gpsimd.memset(d, value).then_inc(filled, 1)
                pool.wait_ge(filled, START + FILLS)
                with pool.Fori(0, B) as b:
                    for g in range(GROUPS):
                        pool.wait_ge(var_ready, START + GROUPS * b + g + 1)
                        nc.gpsimd.tensor_tensor(rstd[:, :], var[:, :], half[:, :], ALU.pow).then_inc(rstd_ready, 1)
                    pool.wait_ge(k_part_ready, START + b + 1)
                    pool.sem_inc(core.taken, 1)
                    nc.gpsimd.partition_all_reduce(k_most[:, :], k_part[:, :], P, bass.bass_isa.ReduceOp.max).then_inc(k_most_ready, 1)
                    core.widest_bound(pool, b)

            @block.vector
            def _(dve):
                dve.wait_ge(consts, START + 16 * 3)
                dve.wait_ge(filled, START + FILLS)
                nc.vector.tensor_copy(ident_b[:, :], ident[:, :]).then_inc(ident_b_ready, 1)
                steps = Steps(dve, chain, CH)
                with dve.Fori(0, B) as b:
                    dve.wait_ge(loaded, START + 16 * b + 16)
                    for g in range(GROUPS):
                        n = GROUPS * b + g
                        tiles = slice(GT * g, GT * g + GT)
                        steps.start(n)
                        centred_and_variance(nc, steps, x[:, tiles, :], xs[:, :, :], sq[:, :, :], mean[:, :], var[:, :],
                                             LN_EPS, var_ready)
                        dve.wait_ge(rstd_ready, START + n + 1)
                        nc.vector.tensor_tensor(xs[:, :, :], xs[:, :, :], bcast(rstd[:, :], C), ALU.mult).then_inc(xn_ready, 1)
                        dve.wait_ge(part0_ready, START + n + 1)
                        dve.wait_ge(qk_ready, START + n + 1)
                        nc.vector.tensor_tensor(rest[:, :, :], qk[:, :, :], parts[0][:, :, :], ALU.subtract).then_inc(rest_ready, 1)
                        dve.wait_ge(rest_ready, START + n + 1)
                        nc.vector.tensor_copy(parts[1][:, :, :], rest[:, :, :]).then_inc(part1_ready, 1)
                        dve.wait_ge(part1_ready, START + n + 1)
                        nc.vector.tensor_tensor(parts[2][:, :, :], rest[:, :, :], parts[1][:, :, :], ALU.subtract).then_inc(parts_ready, 1)
                        dve.wait_ge(parts_ready, START + n + 1)
                        for s in range(6):
                            for w, part in ((0, Q_PART[s]), (1, K_PART[s])):
                                src_p = parts[part][:, :, w * C:(w + 1) * C].rearrange("p t (h d) -> p t h d", d=D)
                                ins = nc.vector.tensor_copy(slots[w][:, tiles, :, s * D:(s + 1) * D], src_p)
                        dve.wait_ge(squares_ready, START + n + 1)
                        nc.vector.reduce_sum(norm2[:, tiles, :], squares[:, :, :].rearrange("p t (h d) -> p t h d", d=D), AX.X).then_inc(slots_ready, 1)
                    dve.wait_ge(slots_ready, START + GROUPS * (b + 1))
                    nc.vector.reduce_max(k_part[:, :], norm2[:, :, H:2 * H].rearrange("p t h -> p h t"), AX.X).then_inc(k_part_ready, 1)
                    dve.wait_ge(k_most_ready, START + b + 1)
                    nc.vector.tensor_tensor(bound[:, :, :], norm2[:, :, 0:H], k_most[:, :].unsqueeze(1).to_broadcast([P, TILES, H]),
                                            ALU.mult).then_inc(product_ready, 1)
                    dve.wait_ge(bound_ready, START + b + 1)
                    core.find_flag(dve, b, bound[:, :, :], slots[0][:, :, :, 24:27])

                    def take_turned(m, ready, out):
                        for g in range(GROUPS):
                            cols = slice(GT * P * g, GT * P * (g + 1))
                            dve.wait_ge(ready, START + GROUPS * m + g + 1)
                            for h in range(4):
                                rows = slice(32 * h, 32 * h + 32)
                                nc.vector.tensor_copy(qt[rows, h, cols], ps_turn[0][rows, :])
                            nc.vector.tensor_copy(kt[:, cols], ps_turn[1]).then_inc(out, 1)

                    flag = core.read_flag(dve)
                    with dve.If(flag > 0):
                        with dve.Fori(0, HG) as hg:
                            m = b * HG + hg
                            take_turned(m, row_turn_ready, row_turned_out)
                            dve.sem_inc(core.taken_dve, 1)
                            with dve.Fori(0, TILES) as t:
                                for h in range(4):
                                    core.vector_row_max(dve, (m * TILES + t) * 4 + h, SEQ,
                                                        lambda n: slots[0][:, bass.ds(t, 1), bass.ds(hg * 4 + h, 1), 24 + n:25 + n]
                                                        .rearrange("p a b c -> p (a b c)"))
                    with dve.Else():
                        nc.vector.tensor_scalar(slots[0][:, :, :, 24], bound[:, :, :], -1.0, None, ALU.mult)
                        dve.sem_inc(row_turned_out, GROUPS * HG)
                        dve.sem_inc(core.row_read, TILES * H)
                        dve.sem_inc(core.row_step, 7 * TILES * H)
                    nc.vector.memset(rstd_spare[:, :], 0.0).then_inc(shift_ready, 1)
                    with dve.Fori(0, HG) as hg:
                        m = b * HG + hg
                        take_turned(m, turn_ready, turned_out)
                        with dve.Fori(0, QBLOCKS) as qb:
                            nb = m * BLOCKS + qb
                            core.vector(dve, nb, TILES * nb + TILES, QW,
                                        lambda t: o[:, bass.ds(qb * 4 + t, 1), bass.ds(hg * 16, 16)].rearrange("p t (h d) -> p (t h) d", d=D))
                        nb = m * BLOCKS + QBLOCKS
                        core.vector(dve, nb, TILES * nb + TILES, P,
                                    lambda t: o[:, TILES - 1, bass.ds(hg * 16, 16)].rearrange("p (h d) -> p h d", d=D))
                    for g in range(GROUPS):
                        n = GROUPS * b + g
                        dve.wait_ge(y_ps_ready, START + n + 1)
                        dve.wait_ge(stored, START + 16 * n)
                        nc.vector.tensor_tensor(y[:, :, :], ps_y, x[:, GT * g:GT * g + GT, :], ALU.add).then_inc(y_ready, 1)

            @block.tensor
            def _(pe):
                pe.wait_ge(consts, START + 16 * 3)
                pe.wait_ge(filled, START + FILLS)
                pe.wait_ge(ident_b_ready, START + 1)
                nc.tensor.matmul(core.acc[:, :], kt[:, 0:P], kt[:, 0:512], start=True, stop=True).then_inc(zeroed_acc, 1)
                with pe.Fori(0, B) as b:
                    for g in range(GROUPS):
                        n = GROUPS * b + g
                        pe.wait_ge(xn_ready, START + n + 1)
                        pe.sem_inc(core.taken, 1)
                        for t in range(GT):
                            ins = nc.tensor.transpose(ps_t[0:C, t * P:(t + 1) * P], xs[:, t, :], ident[:, :])
                        ins.then_inc(xt_ready, 1)
                        pe.wait_ge(ht_ready, START + n + 1)
                        pe.wait_ge(v_ready, START + n)
                        for t in range(GT):
                            ins = nc.tensor.matmul(ps_qkv[:, t, 0:3 * C], ht[:, t * P:(t + 1) * P], wqkv[:, :], start=True, stop=True)
                        ins.then_inc(qkv_ready, 1)

                    def turn(m, hg, ready, out):
                        for g in range(GROUPS):
                            pe.wait_ge(out, START + GROUPS * m + g)
                            for w in range(2):
                                for t in range(GT):
                                    part = slots[w][:, GT * g + t, bass.ds(hg * 4, 4), :].rearrange("p h s -> p (h s)")
                                    ins = nc.tensor.matmul(ps_turn[w][:, t * P:(t + 1) * P], part, ident_b[:, :],
                                                           start=True, stop=True)
                            ins.then_inc(ready, 1)

                    pe.wait_ge(v_ready, START + GROUPS * (b + 1))
                    pe.wait_ge(core.exp_done, START + 2 * TILES * BLOCKS * HG * b)
                    pe.wait_ge(core.flag_ready, START + b + 1)
                    pe.sem_inc(core.taken, 1)
                    flag = core.read_flag(pe)
                    with pe.If(flag > 0):
                        with pe.Fori(0, HG) as hg:
                            m = b * HG + hg
                            pe.wait_ge(core.row_read, START + m * TILES * 4)
                            turn(m, hg, row_turn_ready, row_turned_out)
                            pe.wait_ge(row_turned_out, START + GROUPS * (m + 1))
                            pe.sem_inc(core.taken, 1)
                            with pe.Fori(0, TILES) as t:
                                for h in range(4):
                                    core.tensor_row_scores(pe, (m * TILES + t) * 4 + h, qt[:, h, bass.ds(t * P, P)],
                                                           lambda k0, k1: kt[:, k0:k1], SEQ)
                    with pe.Else():
                        pe.sem_inc(row_turn_ready, GROUPS * HG)
                        pe.sem_inc(core.row_scores, TILES * H)
                    pe.wait_ge(shift_ready, START + b + 1)
                    pe.sem_inc(core.taken, 1)
                    with pe.Fori(0, HG) as hg:
                        m = b * HG + hg
                        pe.wait_ge(core.exp_done, START + 2 * TILES * BLOCKS * m)
                        turn(m, hg, turn_ready, turned_out)
                        pe.wait_ge(turned_out, START + GROUPS * (m + 1))
                        pe.wait_ge(vg_ready, START + m + 1)
                        pe.sem_inc(core.taken, 1)
                        kt_of = lambda t, h: kt[:, t * P:t * P + core.keys(t)]
                        v_of = lambda t, h: vg[0:core.keys(t), t, h, :]
                        with pe.Fori(0, QBLOCKS) as qb:
                            nb = m * BLOCKS + qb
                            core.tensor(pe, nb, TILES * nb, ALL, kt_of, lambda h, _: qt[:, h, bass.ds(qb * QW, QW)], v_of, QW, ident[:, :])
                        nb = m * BLOCKS + QBLOCKS
                        core.tensor(pe, nb, TILES * nb, ALL, kt_of, lambda h, _: qt[:, h, QBLOCKS * QW:SEQP], v_of, P, ident[:, :])
                    pe.wait_ge(core.exp_done, START + 2 * TILES * BLOCKS * HG * (b + 1))
                    for g in range(GROUPS):
                        n = GROUPS * b + g
                        pe.wait_ge(core.block_done, START + BLOCKS * HG * (b + 1))
                        pe.wait_ge(ot_ready, START + n)
                        pe.sem_inc(core.taken, 1)
                        for t in range(GT):
                            ins = nc.tensor.transpose(ps_t[0:C, t * P:(t + 1) * P], o[:, GT * g + t, :], ident[:, :])
                        ins.then_inc(ot_ps_ready, 1)
                        pe.wait_ge(ot_ready, START + n + 1)
                        pe.wait_ge(y_ready, START + n)
                        pe.sem_inc(core.taken, 1)
                        for t in range(GT):
                            ins = nc.tensor.matmul(ps_y[:, t, :], ot[:, t * P:(t + 1) * P], wp[:, :], start=True, stop=True)
                        ins.then_inc(y_ps_ready, 1)

            @block.scalar
            def _(act):
                act.wait_ge(consts, START + 16 * 3)
                act.wait_ge(filled, START + FILLS)
                with act.Fori(0, B) as b:
                    for g in range(GROUPS):
                        n = GROUPS * b + g
                        tiles = slice(GT * g, GT * g + GT)
                        act.wait_ge(xt_ready, START + n + 1)
                        act.wait_ge(qkv_ready, START + n)
                        nc.scalar.activation(ht[0:C, :], ps_t[0:C, :], ACT.Copy).then_inc(ht_ready, 1)
                        act.wait_ge(qkv_ready, START + n + 1)
                        act.wait_ge(slots_ready, START + n)
                        nc.scalar.activation(qk[:, :, :], ps_qkv[:, 0:GT, 0:2 * C], ACT.Copy).then_inc(qk_ready, 1)
                        nc.scalar.activation(parts[0][:, :, :], ps_qkv[:, 0:GT, 0:2 * C], ACT.Copy).then_inc(part0_ready, 1)
                        nc.scalar.activation(squares[:, :, :], ps_qkv[:, 0:GT, 0:2 * C], ACT.Square).then_inc(squares_ready, 1)
                        for t in range(GT):
                            ins = nc.scalar.activation(v[:, GT * g + t, :, 0:D], ps_qkv[:, t, 2 * C:3 * C].rearrange("p (h d) -> p h d", d=D), ACT.Copy)
                        ins.then_inc(v_ready, 1)
                    act.wait_ge(product_ready, START + b + 1)
                    nc.scalar.activation(bound[:, :, :], bound[:, :, :], ACT.Sqrt).then_inc(bound_ready, 1)
                    act.wait_ge(v_ready, START + GROUPS * (b + 1))
                    with act.Fori(0, HG) as hg:
                        m = b * HG + hg
                        act.wait_ge(core.weighed, START + TILES * BLOCKS * m)
                        nc.scalar.activation(vg[:, :, :, :], v[:, :, bass.ds(hg * 4, 4), :], ACT.Copy).then_inc(vg_ready, 1)
                        with act.Fori(0, QBLOCKS) as qb:
                            nb = m * BLOCKS + qb
                            core.scalar(act, nb, TILES * nb, ALL, QW)
                        nb = m * BLOCKS + QBLOCKS
                        core.scalar(act, nb, TILES * nb, ALL, P)
                    for g in range(GROUPS):
                        n = GROUPS * b + g
                        act.wait_ge(ot_ps_ready, START + n + 1)
                        act.wait_ge(y_ps_ready, START + n)
                        nc.scalar.activation(ot[0:C, :], ps_t[0:C, :], ACT.Copy).then_inc(ot_ready, 1)
                        act.wait_ge(y_ready, START + n + 1)
                        act.dma_start(tile_view(dst, b)[:, GT * g:GT * g + GT, :], y[:, :, :]).then_inc(stored, 16)
                act.wait_ge(stored, START + 16 * GROUPS * B)


def causal_attention(nc, src, x2, base, w_qkv, w_out, norm_col, cos, sin, later_in, later_t_in,
                     ident_in):
    tag = "ca"
    H, HK, D = 4, 2, 16
    NH = H + HK
    BLOCKS = QBLOCKS + 1
    WD = P
    spans = [[(P * max(kt - 4 * q, 0), kt >= 4 * q) for kt in range(4 * q + 4)] for q in range(QBLOCKS)]
    spans.append([(0, kt == TILES - 1) for kt in range(TILES)])
    before = [sum(map(len, spans[:q])) for q in range(BLOCKS + 1)]
    with ExitStack() as ctx:
        sb_, ps_, sem_, begin = phase_tools(nc, ctx)
        sb = lambda name, shape, dt=F32: sb_(f"{tag}_{name}", shape, dt)
        ps = lambda name, shape: ps_(f"{tag}_{name}", shape)
        sem = lambda name: sem_(f"{tag}_{name}")
        ident = sb("ident", [P, P])
        ident_b = sb("ident_b", [P, P], BF16)
        later, later_t, diagonal = (sb(n, [P, P]) for n in ("later", "later_t", "diagonal"))
        later_b = sb("later_b", [P, P], BF16)
        wqkv, wo, ncol = sb("wqkv", [C, 2 * C]), sb("wo", [C, C]), sb("ncol", [C, 1])
        tcos, tsin = sb("tcos", [P, TILES, D]), sb("tsin", [P, TILES, D])
        x, z = sb("x", [P, TILES, C]), sb("z", [P, TILES, C])
        xs, sq = sb("xs", [P, GT, C]), sb("sq", [P, GT, C])
        mean, var, rstd, half = (sb(n, [P, GT]) for n in ("mean", "var", "rstd", "half"))
        var2, rstd2 = sb("var2", [P, GT]), sb("rstd2", [P, GT])
        ht = sb("ht", [C, GT * P])
        qk, turned_qk = sb("qk", [P, GT, NH, D]), sb("turned_qk", [P, GT, NH, D])
        parts = [sb(f"part{n}", [P, GT, NH * D], BF16) for n in range(3)]
        rest, squares = sb("rest", [P, GT, NH * D]), sb("squares", [P, GT, NH * D])
        norm2 = sb("norm2", [P, TILES, NH])
        k_part, k_most = sb("k_part", [P, HK]), sb("k_most", [P, HK])
        bound = sb("bound", [P, TILES, H])
        spare = sb("spare", [1, 1])
        slots = sb("slots", [P, TILES, NH, WD], BF16)
        qkt = sb("qkt", [P, NH, SEQP], BF16)
        v = sb("v", [P, TILES, HK, D + 1])
        o = sb("o", [P, TILES, C])
        ot = sb("ot", [C, GT * P])
        y, y_base = sb("y", [P, GT, C]), sb("y_base", [P, GT, C])
        core = Core(nc, sb, ps, sem, D)
        flat_ring = core.ring[:, :, :, :].rearrange("p a b c -> p (a b c)")
        ps_t = flat_ring[:, 0:GT * P]
        ps_qkv = flat_ring[:, 1024:1024 + GT * P].rearrange("p (t c) -> p t c", c=P)
        ps_turn = [flat_ring[:, 1024 * n:1024 * n + NH * P].rearrange("p (h c) -> p h c", c=P) for n in range(2)]
        ps_y = flat_ring[:, 2560:2560 + GT * C].rearrange("p (t c) -> p t c", c=C)
        names = ("consts", "filled", "ident_b_ready", "zeroed_acc", "loaded", "chain", "var_ready", "rstd_ready",
                 "var2_ready", "rstd2_ready", "xn_ready", "xt_ready", "ht_ready", "qkv_ready", "qk_ready", "v_ready",
                 "rotated", "part0_ready", "part1_ready", "rest_ready", "squares_ready", "parts_ready", "slots_ready",
                 "k_part_ready", "k_most_ready", "product_ready", "bound_ready", "shift_ready", "turn_ready",
                 "turned_out", "row_turn_ready", "row_turned_out", "ot_ps_ready", "ot_ready", "y_ps_ready", "y_ready", "base_ready", "stored")
        (consts, filled, ident_b_ready, zeroed_acc, loaded, chain, var_ready, rstd_ready, var2_ready, rstd2_ready,
         xn_ready, xt_ready, ht_ready, qkv_ready, qk_ready, v_ready, rotated, part0_ready, part1_ready, rest_ready,
         squares_ready, parts_ready, slots_ready, k_part_ready, k_most_ready, product_ready, bound_ready, shift_ready,
         turn_ready, turned_out, row_turn_ready, row_turned_out, ot_ps_ready, ot_ready, y_ps_ready, y_ready, base_ready, stored) = map(sem, names)
        CH = 11
        tile_view = lambda a, b: a[b].rearrange("(t p) c -> p t c", p=P)
        fills = [(half[:, :], -0.5), (v[:, :, :, D:D + 1], 1.0), (slots[:, :, :, :], 0.0),
                 (slots[:, :, H:NH, 6 * D:6 * D + 3], 1.0), (qkt[:, 0, 0:512], 0.0)]
        FILLS = len(fills)
        tables = ((ident[:, :], ident_in), (wqkv[:, :], w_qkv), (wo[:, :], w_out), (ncol[:, :], norm_col),
                  (later[:, :], later_in), (later_t[:, :], later_t_in), (tcos[:, :, :], cos.rearrange("(t p) d -> p t d", p=P)),
                  (tsin[:, :, :], sin.rearrange("(t p) d -> p t d", p=P)))
        CONSTS = 16 * len(tables)

        begin()
        with nc.Block() as block:
            @block.sync
            def _(sp):
                for d, a in tables:
                    sp.dma_start(d, a).then_inc(consts, 16)
                with sp.Fori(0, B) as b:
                    sp.wait_ge(base_ready, START + GROUPS * b)
                    sp.dma_start(x[:, :, :], tile_view(src, b)).then_inc(loaded, 16)

            @block.gpsimd
            def _(pool):
                for n, (d, value) in enumerate(fills):
                    pool.wait_ge(filled, START + n)
                    nc.gpsimd.memset(d, value).then_inc(filled, 1)
                pool.wait_ge(filled, START + FILLS)
                with pool.Fori(0, B) as b:
                    for g in range(GROUPS):
                        n = GROUPS * b + g
                        pool.wait_ge(var_ready, START + n + 1)
                        nc.gpsimd.tensor_tensor(rstd[:, :], var[:, :], half[:, :], ALU.pow).then_inc(rstd_ready, 1)
                        pool.wait_ge(var2_ready, START + n + 1)
                        nc.gpsimd.tensor_tensor(rstd2[:, :], var2[:, :], half[:, :], ALU.pow).then_inc(rstd2_ready, 1)
                    pool.wait_ge(k_part_ready, START + b + 1)
                    pool.sem_inc(core.taken, 1)
                    nc.gpsimd.partition_all_reduce(k_most[:, :], k_part[:, :], P, bass.bass_isa.ReduceOp.max).then_inc(k_most_ready, 1)
                    core.widest_bound(pool, b)

            @block.vector
            def _(dve):
                dve.wait_ge(consts, START + CONSTS)
                dve.wait_ge(filled, START + FILLS)
                nc.vector.tensor_copy(ident_b[:, :], ident[:, :]).then_inc(ident_b_ready, 1)
                nc.vector.tensor_copy(later_b[:, :], later_t[:, :]).then_inc(ident_b_ready, 1)
                steps = Steps(dve, chain, CH)
                with dve.Fori(0, B) as b:
                    dve.wait_ge(loaded, START + 16 * b + 16)
                    for g in range(GROUPS):
                        n = GROUPS * b + g
                        tiles = slice(GT * g, GT * g + GT)
                        steps.start(n)
                        centred_and_variance(nc, steps, x[:, tiles, :], xs[:, :, :], sq[:, :, :], mean[:, :], var[:, :],
                                             LN_EPS, var_ready)
                        dve.wait_ge(rstd_ready, START + n + 1)
                        steps.link(nc.vector.tensor_tensor(z[:, tiles, :], xs[:, :, :], bcast(rstd[:, :], C), ALU.mult))
                        steps.link(nc.vector.tensor_tensor(sq[:, :, :], z[:, tiles, :], z[:, tiles, :], ALU.mult))
                        steps.link(nc.vector.reduce_sum(var2[:, :], sq[:, :, :], AX.X))
                        nc.vector.tensor_scalar(var2[:, :], var2[:, :], 1.0 / C, RMS_EPS, ALU.mult, ALU.add).then_inc(var2_ready, 1)
                        dve.wait_ge(rstd2_ready, START + n + 1)
                        nc.vector.tensor_tensor(xs[:, :, :], z[:, tiles, :], bcast(rstd2[:, :], C), ALU.mult).then_inc(xn_ready, 1)
                        dve.wait_ge(qk_ready, START + n + 1)
                        c_b = tcos[:, tiles, :].unsqueeze(2).to_broadcast([P, GT, NH, D])
                        steps.link(nc.vector.tensor_tensor(turned_qk[:, :, :, 0:D // 2], qk[:, :, :, D // 2:D],
                                                           tsin[:, tiles, 0:D // 2].unsqueeze(2).to_broadcast([P, GT, NH, D // 2]), ALU.mult))
                        steps.link(nc.vector.tensor_tensor(turned_qk[:, :, :, D // 2:D], qk[:, :, :, 0:D // 2],
                                                           tsin[:, tiles, D // 2:D].unsqueeze(2).to_broadcast([P, GT, NH, D // 2]), ALU.mult))
                        steps.link(nc.vector.tensor_tensor(qk[:, :, :, :], qk[:, :, :, :], c_b, ALU.mult))
                        flat_qk = qk[:, :, :, :].rearrange("p t h d -> p t (h d)")
                        nc.vector.tensor_tensor(flat_qk, flat_qk, turned_qk[:, :, :, :].rearrange("p t h d -> p t (h d)"), ALU.add).then_inc(rotated, 1)
                        dve.wait_ge(part0_ready, START + n + 1)
                        dve.wait_ge(rotated, START + n + 1)
                        nc.vector.tensor_tensor(rest[:, :, :], flat_qk, parts[0][:, :, :], ALU.subtract).then_inc(rest_ready, 1)
                        dve.wait_ge(rest_ready, START + n + 1)
                        nc.vector.tensor_copy(parts[1][:, :, :], rest[:, :, :]).then_inc(part1_ready, 1)
                        dve.wait_ge(part1_ready, START + n + 1)
                        nc.vector.tensor_tensor(parts[2][:, :, :], rest[:, :, :], parts[1][:, :, :], ALU.subtract).then_inc(parts_ready, 1)
                        dve.wait_ge(parts_ready, START + n + 1)
                        for s in range(6):
                            for (h0, h1), part in (((0, H), Q_PART[s]), ((H, NH), K_PART[s])):
                                src_p = parts[part][:, :, h0 * D:h1 * D].rearrange("p t (h d) -> p t h d", d=D)
                                nc.vector.tensor_copy(slots[:, tiles, h0:h1, s * D:(s + 1) * D], src_p)
                        dve.wait_ge(squares_ready, START + n + 1)
                        nc.vector.reduce_sum(norm2[:, tiles, :], squares[:, :, :].rearrange("p t (h d) -> p t h d", d=D), AX.X).then_inc(slots_ready, 1)
                    dve.wait_ge(slots_ready, START + GROUPS * (b + 1))
                    nc.vector.reduce_max(k_part[:, :], norm2[:, :, H:NH].rearrange("p t h -> p h t"), AX.X).then_inc(k_part_ready, 1)
                    dve.wait_ge(k_most_ready, START + b + 1)
                    for e in range(HK):
                        ins = nc.vector.tensor_scalar(bound[:, :, 2 * e:2 * e + 2], norm2[:, :, 2 * e:2 * e + 2], k_most[:, e:e + 1], None, ALU.mult)
                    ins.then_inc(product_ready, 1)
                    dve.wait_ge(bound_ready, START + b + 1)
                    core.find_flag(dve, b, bound[:, :, :], slots[:, :, 0:H, 6 * D:6 * D + 3])

                    def take_turned(ready, out):
                        for t in range(TILES):
                            dve.wait_ge(ready, START + TILES * b + t + 1)
                            nc.vector.tensor_copy(qkt[:, :, t * P:(t + 1) * P], ps_turn[t % 2]).then_inc(out, 1)

                    flag = core.read_flag(dve)
                    with dve.If(flag > 0):
                        take_turned(row_turn_ready, row_turned_out)
                        for t in range(TILES):
                            for h in range(H):
                                core.vector_row_max(dve, (b * TILES + t) * H + h, t * P + P if t < TILES - 1 else SEQ,
                                                    lambda n: slots[:, t, h, 6 * D + n:6 * D + n + 1], later, diagonal)
                    with dve.Else():
                        nc.vector.tensor_scalar(slots[:, :, 0:H, 6 * D], bound[:, :, :], -1.0, None, ALU.mult)
                        dve.sem_inc(row_turned_out, TILES)
                        dve.sem_inc(core.row_read, TILES * H)
                        dve.sem_inc(core.row_step, 7 * TILES * H)
                    nc.vector.memset(spare[:, :], 0.0).then_inc(shift_ready, 1)
                    take_turned(turn_ready, turned_out)
                    for q in range(BLOCKS):
                        width = QW if q < QBLOCKS else P
                        units = before[BLOCKS] * b + before[q]
                        core.vector(dve, BLOCKS * b + q, units + len(spans[q]), width,
                                    lambda t: o[:, 4 * q + t, :].rearrange("p (h d) -> p h d", d=D))
                    for g in range(GROUPS):
                        n = GROUPS * b + g
                        dve.wait_ge(y_ps_ready, START + n + 1)
                        dve.wait_ge(stored, START + 32 * n)
                        nc.vector.tensor_tensor(y[:, :, :], ps_y, z[:, GT * g:GT * g + GT, :], ALU.add).then_inc(y_ready, 1)
                        dve.wait_ge(y_ready, START + n + 1)
                        nc.vector.tensor_tensor(y_base[:, :, :], y[:, :, :], x[:, GT * g:GT * g + GT, :], ALU.add).then_inc(base_ready, 1)

            @block.tensor
            def _(pe):
                pe.wait_ge(consts, START + CONSTS)
                pe.wait_ge(filled, START + FILLS)
                pe.wait_ge(ident_b_ready, START + 2)
                nc.tensor.matmul(core.acc[:, :], qkt[:, 0, 0:P], qkt[:, 0, 0:512], start=True, stop=True).then_inc(zeroed_acc, 1)
                with pe.Fori(0, B) as b:
                    for g in range(GROUPS):
                        n = GROUPS * b + g
                        pe.wait_ge(xn_ready, START + n + 1)
                        pe.sem_inc(core.taken, 1)
                        for t in range(GT):
                            ins = nc.tensor.transpose(ps_t[0:C, t * P:(t + 1) * P], xs[:, t, :], ident[:, :])
                        ins.then_inc(xt_ready, 1)
                        pe.wait_ge(ht_ready, START + n + 1)
                        pe.wait_ge(v_ready, START + n)
                        pe.sem_inc(core.taken, 1)
                        for t in range(GT):
                            ins = nc.tensor.matmul(ps_qkv[:, t, :], ht[:, t * P:(t + 1) * P], wqkv[:, :], start=True, stop=True)
                        ins.then_inc(qkv_ready, 1)
                    def turn(ready, out):
                        for t in range(TILES):
                            pe.wait_ge(out, START + TILES * b + max(t - 1, 0))
                            for h in range(NH):
                                ins = nc.tensor.matmul(ps_turn[t % 2][:, h, :], slots[:, t, h, :], ident_b[:, :], start=True, stop=True)
                            ins.then_inc(ready, 1)

                    pe.wait_ge(v_ready, START + GROUPS * (b + 1))
                    pe.wait_ge(core.flag_ready, START + b + 1)
                    pe.sem_inc(core.taken, 1)
                    flag = core.read_flag(pe)
                    with pe.If(flag > 0):
                        turn(row_turn_ready, row_turned_out)
                        pe.wait_ge(row_turned_out, START + TILES * (b + 1))
                        for t in range(TILES):
                            for h in range(H):
                                core.tensor_row_scores(pe, (b * TILES + t) * H + h, qkt[:, h, t * P:(t + 1) * P],
                                                       lambda k0, k1: qkt[:, H + h // 2, k0:k1], t * P + P if t < TILES - 1 else SEQ)
                    with pe.Else():
                        pe.sem_inc(row_turn_ready, TILES)
                        pe.sem_inc(core.row_scores, TILES * H)
                    pe.wait_ge(shift_ready, START + b + 1)
                    turn(turn_ready, turned_out)
                    pe.wait_ge(turned_out, START + TILES * (b + 1))
                    pe.sem_inc(core.taken, 1)
                    for q in range(BLOCKS):
                        width = QW if q < QBLOCKS else P
                        core.tensor(pe, BLOCKS * b + q, before[BLOCKS] * b + before[q], spans[q],
                                    lambda t, h: qkt[:, H + h // 2, t * P:t * P + core.keys(t)],
                                    lambda h, first: qkt[:, h, QW * q + first:QW * q + width],
                                    lambda t, h: v[0:core.keys(t), t, h // 2, :], width, ident[:, :], ident_b, later_b[:, :])
                    pe.wait_ge(core.block_done, START + BLOCKS * (b + 1))
                    for g in range(GROUPS):
                        n = GROUPS * b + g
                        pe.wait_ge(ot_ready, START + n)
                        pe.sem_inc(core.taken, 1)
                        for t in range(GT):
                            ins = nc.tensor.transpose(ps_t[0:C, t * P:(t + 1) * P], o[:, GT * g + t, :], ident[:, :])
                        ins.then_inc(ot_ps_ready, 1)
                        pe.wait_ge(ot_ready, START + n + 1)
                        pe.wait_ge(y_ready, START + n)
                        pe.sem_inc(core.taken, 1)
                        for t in range(GT):
                            ins = nc.tensor.matmul(ps_y[:, t, :], ot[:, t * P:(t + 1) * P], wo[:, :], start=True, stop=True)
                        ins.then_inc(y_ps_ready, 1)

            @block.scalar
            def _(act):
                act.wait_ge(consts, START + CONSTS)
                act.wait_ge(filled, START + FILLS)
                with act.Fori(0, B) as b:
                    for g in range(GROUPS):
                        n = GROUPS * b + g
                        act.wait_ge(xt_ready, START + n + 1)
                        act.wait_ge(qkv_ready, START + n)
                        nc.scalar.activation(ht[:, :], ps_t[0:C, :], ACT.Identity, scale=ncol[:, 0:1]).then_inc(ht_ready, 1)
                        act.wait_ge(qkv_ready, START + n + 1)
                        act.wait_ge(slots_ready, START + n)
                        nc.scalar.activation(qk[:, :, 0:H, :].rearrange("p t h d -> p t (h d)"), ps_qkv[:, :, 0:H * D], ACT.Copy,
                                             scale=float(D) ** -0.5)
                        nc.scalar.activation(qk[:, :, H:NH, :].rearrange("p t h d -> p t (h d)"), ps_qkv[:, :, H * D:NH * D],
                                             ACT.Copy).then_inc(qk_ready, 1)
                        for e in range(HK):
                            ins = nc.scalar.activation(v[:, GT * g:GT * g + GT, e, 0:D], ps_qkv[:, :, (NH + e) * D:(NH + e + 1) * D], ACT.Copy)
                        ins.then_inc(v_ready, 1)
                        act.wait_ge(rotated, START + n + 1)
                        flat_qk = qk[:, :, :, :].rearrange("p t h d -> p t (h d)")
                        nc.scalar.activation(parts[0][:, :, :], flat_qk, ACT.Copy).then_inc(part0_ready, 1)
                        nc.scalar.activation(squares[:, :, :], flat_qk, ACT.Square).then_inc(squares_ready, 1)
                    act.wait_ge(product_ready, START + b + 1)
                    nc.scalar.activation(bound[:, :, :], bound[:, :, :], ACT.Sqrt).then_inc(bound_ready, 1)
                    for q in range(BLOCKS):
                        width = QW if q < QBLOCKS else P
                        core.scalar(act, BLOCKS * b + q, before[BLOCKS] * b + before[q], spans[q], width)
                    for g in range(GROUPS):
                        n = GROUPS * b + g
                        act.wait_ge(ot_ps_ready, START + n + 1)
                        act.wait_ge(y_ps_ready, START + n)
                        nc.scalar.activation(ot[:, :], ps_t[0:C, :], ACT.Copy).then_inc(ot_ready, 1)
                        act.wait_ge(base_ready, START + n + 1)
                        act.wait_ge(y_ready, START + n + 1)
                        act.dma_start(tile_view(x2, b)[:, GT * g:GT * g + GT, :], y[:, :, :]).then_inc(stored, 16)
                        act.dma_start(tile_view(base, b)[:, GT * g:GT * g + GT, :], y_base[:, :, :]).then_inc(stored, 16)
                act.wait_ge(stored, START + 32 * GROUPS * B)


def split_three(v, link, whole, rest, first, second, third, third_rows=None):
    link(v.tensor_copy(first, whole))
    link(v.tensor_tensor(rest, whole, first, ALU.subtract))
    link(v.tensor_copy(second, rest))
    if third_rows is not None:
        rest, second = rest[third_rows], second[third_rows]
    return v.tensor_tensor(third, rest, second, ALU.subtract)


def experts(nc, x2, base, out, w_1, w_2, w_3, selector, w_router, norm_col, rank_in, ident_in):
    tag = "moe"
    E = w_router.shape[1]
    HIDDEN = w_1.shape[1]
    CHUNKS = HIDDEN // P
    LAG = 3
    BLOCKS = QBLOCKS + 1
    with ExitStack() as ctx:
        sb_, ps_, sem_, begin = phase_tools(nc, ctx)
        sb = lambda name, shape, dt=F32: sb_(f"{tag}_{name}", shape, dt)
        ps = lambda name, shape: ps_(f"{tag}_{name}", shape)
        sem = lambda name: sem_(f"{tag}_{name}")
        ident = sb("ident", [P, P])
        ident_b = sb("ident_b", [P, P], BF16)
        w_whole = [sb(f"w_whole{n}", [P, HIDDEN]) for n in range(2)]
        w_rest = sb("w_rest", [P, HIDDEN])
        w_parts = [[sb(f"w{n}_part{m}", [P, HIDDEN], BF16) for m in range(3)] for n in range(2)]
        w2 = sb("w2", [P, CHUNKS, C])
        sel = sb("sel", [3 * E, HIDDEN])
        sel_b = sb("sel_b", [3 * E, HIDDEN], BF16)
        wr, ncol, rank = sb("wr", [C, E]), sb("ncol", [C, 1]), sb("rank", [P, E])
        half = sb("half", [P, TILES])
        x = sb("x", [P, TILES, C])
        acc = sb("acc", [P, TILES, C])
        sq = sb("sq", [P, TILES, C])
        var, rstd = sb("var", [P, TILES]), sb("rstd", [P, TILES])
        ft = sb("ft", [C, 512])
        ft_rest = sb("ft_rest", [C, 512])
        f_parts = [sb(f"f_part{m}", [P, SEQP], BF16) for m in range(2)]
        prob = sb("prob", [P, TILES, E])
        w_rest8 = sb("w_rest8", [P, TILES, E])
        weight_parts = sb("weight_parts", [P, TILES, 3 * E], BF16)
        weight_t = sb("weight_t", [3 * E, SEQP], BF16)
        most, total = sb("most", [P, TILES]), sb("total", [P, TILES])
        first, second = sb("first", [P, TILES]), sb("second", [P, TILES])
        is_first, is_second, work = (sb(n, [P, TILES, E]) for n in ("is_first", "is_second", "work"))
        gate = [sb(f"gate{n}", [P, QW]) for n in range(2)]
        product = [sb(f"product{n}", [P, QW]) for n in range(2)]
        RH = 5
        hid = [sb(f"hid{n}", [P, QW]) for n in range(RH)]
        out_t = sb("out_t", [P, QW])
        ps_a = [ps(f"ps_a{n}", [P, 512]) for n in range(2)]
        ps_b = [ps(f"ps_b{n}", [P, 512]) for n in range(2)]
        ps_w = [ps(f"ps_w{n}", [P, 512]) for n in range(2)]
        ps_o, ps_t = ps("ps_o", [P, 512]), ps("ps_t", [P, 512])
        names = ("consts", "filled", "taken", "loaded", "chain", "var_ready", "rstd_ready", "xn_ready", "xt_ready",
                 "ft_ready", "logits_ready", "less_max", "exp_ready", "wt_ready", "wt_copied", "parts_chain",
                 "weights_ready", "up_ready", "gate_ready", "product_ready", "hid_ready", "down_ready", "out_copied",
                 "out_turned", "added", "stored", "taken_dve", "parts_done", "half_added")
        (consts, filled, taken, loaded, chain, var_ready, rstd_ready, xn_ready, xt_ready, ft_ready, logits_ready,
         less_max, exp_ready, wt_ready, wt_copied, parts_chain, weights_ready, up_ready, gate_ready, product_ready,
         hid_ready, down_ready, out_copied, out_turned, added, stored, taken_dve, parts_done, half_added) = map(sem, names)
        NT = -(-TILES // 4)
        CH = 21 + 5 + 5 * NT
        tile_view = lambda a, b: a[b].rearrange("(t p) c -> p t c", p=P)
        tables = ((ident[:, :], ident_in), (w_whole[0][:, :], w_1), (w_whole[1][:, :], w_3), (w2[:, :, :], w_2),
                  (sel[:, :], selector), (wr[:, :], w_router), (ncol[:, :], norm_col), (rank[:, :], rank_in))
        CONSTS = 16 * len(tables)

        def all_blocks(eng, b, body):
            with eng.Fori(0, QBLOCKS) as q:
                body(b * BLOCKS + q, q, QW)
            body(b * BLOCKS + QBLOCKS, QBLOCKS, P)

        begin()
        with nc.Block() as block:
            @block.sync
            def _(sp):
                for d, a in tables:
                    sp.dma_start(d, a).then_inc(consts, 16)
                with sp.Fori(0, B) as b:
                    sp.wait_ge(xn_ready, START + b)
                    sp.dma_start(x[:, :, :], tile_view(x2, b)).then_inc(loaded, 16)
                    sp.wait_ge(stored, START + 32 * b)
                    sp.dma_start(acc[:, :, :], tile_view(base, b)).then_inc(loaded, 16)

            @block.gpsimd
            def _(pool):
                nc.gpsimd.memset(half[:, :], -0.5).then_inc(filled, 1)
                pool.wait_ge(filled, START + 1)
                with pool.Fori(0, B) as b:
                    pool.wait_ge(var_ready, START + b + 1)
                    nc.gpsimd.tensor_tensor(rstd[:, :], var[:, :], half[:, :], ALU.pow).then_inc(rstd_ready, 1)

            @block.vector
            def _(dve):
                dve.wait_ge(consts, START + CONSTS)
                dve.wait_ge(filled, START + 1)
                v = nc.vector
                v.tensor_copy(ident_b[:, :], ident[:, :])
                v.tensor_copy(sel_b[:, :], sel[:, :])
                prepare = Steps(dve, parts_chain, 6)
                for n in range(2):
                    prepare.start(n)
                    a, b_, c_ = (t[:, :] for t in w_parts[n])
                    last = split_three(v, prepare.link, w_whole[n][:, :], w_rest[:, :], a, b_, c_[0:C, :], slice(0, C))
                    prepare.link(last)
                    prepare.link(v.tensor_copy(c_[C:P, :], a[C:P, :]))
                    prepare.link(v.memset(work[:, 0:1, 0:1], 0.0))
                v.memset(most[:, 0:1], 0.0).then_inc(parts_done, 1)
                dve.wait_ge(parts_done, START + 1)
                steps = Steps(dve, chain, CH)
                with dve.Fori(0, B) as b:
                    steps.start(b)
                    dve.wait_ge(loaded, START + 32 * b + 32)
                    steps.link(v.tensor_tensor(sq[:, :, :], x[:, :, :], x[:, :, :], ALU.mult))
                    steps.link(v.reduce_sum(var[:, :], sq[:, :, :], AX.X))
                    v.tensor_scalar(var[:, :], var[:, :], 1.0 / C, RMS_EPS, ALU.mult, ALU.add).then_inc(var_ready, 1)
                    dve.wait_ge(rstd_ready, START + b + 1)
                    v.tensor_tensor(sq[:, :, :], x[:, :, :], bcast(rstd[:, :], C), ALU.mult).then_inc(xn_ready, 1)
                    for n in range(NT):
                        wd = min(512, SEQP - n * 512)
                        cols = slice(n * 512, n * 512 + wd)
                        dve.wait_ge(xt_ready, START + NT * b + n + 1)
                        dve.wait_ge(logits_ready, START + NT * b + n)
                        steps.link(v.tensor_scalar(ft[:, 0:wd], ps_t[0:C, 0:wd], ncol[:, 0:1], None, ALU.mult))
                        steps.link(split_three(v, steps.link, ft[:, 0:wd], ft_rest[:, 0:wd], f_parts[0][0:C, cols],
                                               f_parts[0][C:P, cols], f_parts[1][C:P, cols]))
                        v.tensor_copy(f_parts[1][0:C, cols], f_parts[0][0:C, cols]).then_inc(ft_ready, 1)
                    dve.wait_ge(logits_ready, START + NT * (b + 1))
                    logits = ps_o[:, 0:TILES * E].rearrange("p (t e) -> p t e", e=E)
                    steps.link(v.reduce_max(most[:, :], logits, AX.X))
                    v.tensor_tensor(prob[:, :, :], logits, bcast(most[:, :], E), ALU.subtract).then_inc(less_max, 1)
                    dve.wait_ge(exp_ready, START + b + 1)
                    steps.link(v.reduce_sum(total[:, :], prob[:, :, :], AX.X))
                    steps.link(v.reciprocal(total[:, :], total[:, :]))
                    steps.link(v.tensor_tensor(prob[:, :, :], prob[:, :, :], bcast(total[:, :], E), ALU.mult))
                    rank_b = rank[:, :].unsqueeze(1).to_broadcast([P, TILES, E])

                    def pick(values, top, chosen):
                        steps.link(v.reduce_max(top, values, AX.X))
                        steps.link(v.tensor_tensor(chosen, values, bcast(top, E), ALU.is_equal))
                        steps.link(v.tensor_tensor(chosen, chosen, rank_b, ALU.mult))
                        steps.link(v.reduce_max(most[:, :], chosen, AX.X))
                        steps.link(v.tensor_tensor(chosen, chosen, bcast(most[:, :], E), ALU.is_equal))
                    pick(prob[:, :, :], first[:, :], is_first[:, :, :])
                    steps.link(v.tensor_scalar(work[:, :, :], is_first[:, :, :], -2.0, None, ALU.mult))
                    steps.link(v.tensor_tensor(work[:, :, :], work[:, :, :], prob[:, :, :], ALU.add))
                    pick(work[:, :, :], second[:, :], is_second[:, :, :])
                    steps.link(v.scalar_tensor_tensor(out=total[:, :], in0=first[:, :], scalar=1e-9, in1=second[:, :],
                                                      op0=ALU.add, op1=ALU.add))
                    steps.link(v.tensor_tensor(is_first[:, :, :], is_first[:, :, :], is_second[:, :, :], ALU.add))
                    steps.link(v.reciprocal(total[:, :], total[:, :]))
                    steps.link(v.tensor_tensor(prob[:, :, :], prob[:, :, :], is_first[:, :, :], ALU.mult))
                    steps.link(v.tensor_tensor(prob[:, :, :], prob[:, :, :], bcast(total[:, :], E), ALU.mult))
                    split_three(v, steps.link, prob[:, :, :], w_rest8[:, :, :], weight_parts[:, :, 0:E],
                                weight_parts[:, :, E:2 * E], weight_parts[:, :, 2 * E:3 * E]).then_inc(weights_ready, 1)
                    for n in range(NT):
                        wd = min(512, SEQP - n * 512)
                        dve.wait_ge(wt_ready, START + NT * b + n + 1)
                        v.tensor_copy(weight_t[:, n * 512:n * 512 + wd], ps_t[0:3 * E, 0:wd]).then_inc(wt_copied, 1)
                    dve.sem_inc(taken_dve, 1)

                    def body(nb, q, width):
                        for k in range(CHUNKS):
                            n = CHUNKS * nb + k
                            dve.wait_ge(gate_ready, START + n + 1)
                            v.tensor_tensor(product[k % 2][:, 0:width], gate[k % 2][:, 0:width], ps_b[k % 2][:, 0:width],
                                            ALU.mult).then_inc(product_ready, 1)
                            dve.wait_ge(product_ready, START + n + 1)
                            dve.wait_ge(down_ready, START + CHUNKS * nb + max(k - RH + 1, 0))
                            v.tensor_tensor(hid[k % RH][:, 0:width], product[k % 2][:, 0:width], ps_w[k % 2][:, 0:width],
                                            ALU.mult).then_inc(hid_ready, 1)
                        tiles = width // P
                        target = acc[:, bass.ds(q * 4, tiles), :] if width == QW else acc[:, TILES - 1:TILES, :]
                        dve.wait_ge(out_turned, START + nb + 1)
                        halves = ps_t[:, 0:width].rearrange("p (t two c) -> p t two c", two=2, c=C)
                        v.tensor_tensor(target, target, halves[:, :, 0, :], ALU.add).then_inc(half_added, 1)
                        dve.wait_ge(half_added, START + nb + 1)
                        v.tensor_tensor(target, target, halves[:, :, 1, :], ALU.add).then_inc(added, 1)
                    all_blocks(dve, b, body)

            @block.tensor
            def _(pe):
                pe.wait_ge(consts, START + CONSTS)
                pe.wait_ge(parts_done, START + 1)
                with pe.Fori(0, B) as b:
                    pe.wait_ge(xn_ready, START + b + 1)
                    pe.wait_ge(added, START + BLOCKS * b)
                    for n in range(NT):
                        ts = range(4 * n, min(4 * n + 4, TILES))
                        pe.wait_ge(ft_ready, START + NT * b + n)
                        pe.sem_inc(taken, 1)
                        for t in ts:
                            ins = nc.tensor.transpose(ps_t[0:C, (t % 4) * P:(t % 4 + 1) * P], sq[:, t, :], ident[:, :])
                        ins.then_inc(xt_ready, 1)
                        pe.wait_ge(ft_ready, START + NT * b + n + 1)
                        pe.sem_inc(taken, 1)
                        for t in ts:
                            ins = nc.tensor.matmul(ps_o[:, t * E:(t + 1) * E], ft[:, (t % 4) * P:(t % 4 + 1) * P], wr[:, :], start=True, stop=True)
                        ins.then_inc(logits_ready, 1)
                    pe.wait_ge(weights_ready, START + b + 1)
                    for n in range(NT):
                        pe.wait_ge(wt_copied, START + NT * b + n)
                        pe.sem_inc(taken, 1)
                        for t in range(4 * n, min(4 * n + 4, TILES)):
                            ins = nc.tensor.matmul(ps_t[0:3 * E, (t % 4) * P:(t % 4 + 1) * P], weight_parts[:, t, :], ident_b[:, :],
                                                   start=True, stop=True)
                        ins.then_inc(wt_ready, 1)
                    pe.wait_ge(wt_copied, START + NT * (b + 1))
                    pe.sem_inc(taken, 1)

                    def body(nb, q, width):
                        tiles = width // P
                        at = lambda a: a[:, bass.ds(q * QW, width)] if width == QW else a[:, QBLOCKS * QW:SEQP]

                        def down(ks):
                            pe.wait_ge(hid_ready, START + CHUNKS * nb + ks[-1] + 1)
                            if ks[0] == 0:
                                pe.wait_ge(out_copied, START + nb)
                            pe.sem_inc(taken, 1)
                            for k in ks:
                                lo = C * (k % 2)
                                nc.tensor.matmul(ps_o[lo:lo + C, 0:width], w2[:, k, :], hid[k % RH][:, 0:width],
                                                 start=(k < 2), stop=(k >= CHUNKS - 2)).then_inc(down_ready, 1)
                        for k in range(CHUNKS):
                            pe.wait_ge(hid_ready, START + CHUNKS * nb + max(k - 1, 0))
                            units = slice(k * P, (k + 1) * P)
                            for n, bank in enumerate((ps_a[k % 2], ps_b[k % 2])):
                                for m in range(3):
                                    ins = nc.tensor.matmul(bank[:, 0:width], w_parts[n][m][:, units], at(f_parts[m // 2]),
                                                           start=(m == 0), stop=(m == 2))
                            nc.tensor.matmul(ps_w[k % 2][:, 0:width], sel_b[:, units], at(weight_t), start=True, stop=True).then_inc(up_ready, 1)
                            if k >= LAG and k % 2:
                                down((k - LAG, k - LAG + 1))
                        for k in range((CHUNKS - LAG + 1) // 2 * 2, CHUNKS, 2):
                            down(tuple(range(k, min(k + 2, CHUNKS))))
                        pe.wait_ge(out_copied, START + nb + 1)
                        for t in range(tiles):
                            ins = nc.tensor.transpose(ps_t[:, t * P:(t + 1) * P], out_t[:, t * P:(t + 1) * P], ident[:, :])
                        ins.then_inc(out_turned, 1)
                    all_blocks(pe, b, body)

            @block.scalar
            def _(act):
                with act.Fori(0, B) as b:
                    act.wait_ge(less_max, START + b + 1)
                    nc.scalar.activation(prob[:, :, :], prob[:, :, :], ACT.Exp).then_inc(exp_ready, 1)

                    def body(nb, q, width):
                        for k in range(CHUNKS):
                            n = CHUNKS * nb + k
                            act.wait_ge(up_ready, START + n + 1)
                            act.wait_ge(product_ready, START + CHUNKS * nb + max(k - 1, 0))
                            nc.scalar.activation(gate[k % 2][:, 0:width], ps_a[k % 2][:, 0:width], ACT.Silu).then_inc(gate_ready, 1)
                        act.wait_ge(down_ready, START + CHUNKS * (nb + 1))
                        act.wait_ge(out_turned, START + nb)
                        nc.scalar.activation(out_t[:, 0:width], ps_o[:, 0:width], ACT.Copy).then_inc(out_copied, 1)
                    all_blocks(act, b, body)
                    act.wait_ge(added, START + BLOCKS * (b + 1))
                    full = (TILES - 1) * P
                    act.dma_start(out[b][0:full, :].rearrange("(t p) c -> p t c", p=P), acc[:, 0:TILES - 1, :]).then_inc(stored, 16)
                    act.dma_start(out[b][full:SEQ, :], acc[0:LAST, TILES - 1, :]).then_inc(stored, 16)
                act.wait_ge(stored, START + 32 * B)


def program(nc, a, out):
    dram = lambda name, shape: nc.dram_tensor(name, shape, F32, kind="Internal").ap()
    tokens, tokens2 = dram("tokens", (B * TOK, C)), dram("tokens2", (B * TOK, C))
    padded = dram("padded", (B, PAD, PAD, C))
    seq0, seq1, x2, base = (dram(n, (B, SEQP, C)) for n in ("seq0", "seq1", "x2", "base"))
    image = lambda t: t.rearrange("(b r c) ch -> b r c ch", b=B, r=SIDE)
    groups = lambda t: t.rearrange("(n g p) c -> n p g c", g=4, p=112)
    S = SIDE

    patch_embed(nc, a["patches"], a["w_patch"], a["patch_norm"], tokens)
    window_attention(nc, "w0", image(tokens), 0, a["norm1_0"], a["wq_0"], a["wk_0"], a["wv_0"], a["wproj_0"],
                     a["bias_0"], None, 1, a["head_mask"], a["ident"])
    mlp(nc, "m0", groups(tokens), groups(tokens2), a["norm2_0"], a["w1_0"], a["w2_0"], a["b2_0"], a["ident"])

    t, t2 = image(tokens), image(tokens2)
    copies(nc, "spread", [[(padded[b, 0:S, 0:S, :], t2[b]) for b in range(B)],
                          [(padded[b, 0:S, S:PAD, :], padded[b, 0:S, 0:SHIFT, :]) for b in range(B)],
                          [(padded[b, S:PAD, :, :], padded[b, 0:SHIFT, :, :]) for b in range(B)]])
    window_attention(nc, "w1", padded, SHIFT, a["norm1_1"], a["wq_1"], a["wk_1"], a["wv_1"], a["wproj_1"],
                     a["bias_1"], a["mask"], 2, a["head_mask"], a["ident"])
    far, near = (slice(SHIFT, S), slice(SHIFT, S)), (slice(0, SHIFT), slice(S, PAD))
    copies(nc, "fold", [[(t[b, r[0], c[0], :], padded[b, r[1], c[1], :]) for b in range(B)
                         for r in (far, near) for c in (far, near)]])
    mlp(nc, "m1", groups(tokens), groups(tokens2), a["norm2_1"], a["w1_1"], a["w2_1"], a["b2_1"], a["ident"])

    flat = tokens2.rearrange("(b t) c -> b t c", b=B)
    copies(nc, "join", [[x for b in range(B) for x in ((seq0[b, 1:SEQ, :], flat[b]), (seq0[b, 0:1, :], a["cls"]),
                                                       (seq0[b, SEQ:SEQP, :], a["zeros"]))]])
    dense_attention(nc, seq0, seq1, a["w_qkv"], a["w_proj"], a["ident"])
    causal_attention(nc, seq1, x2, base, a["f_qkv"], a["f_out"], a["f_norm1"], a["cos"], a["sin"], a["later"],
                     a["later_t"], a["ident"])
    experts(nc, x2, base, out, a["e_w1"], a["e_w2"], a["e_w3"], a["selector"], a["router"],
            a["f_norm2"], a["rank"], a["ident"])


def host_layout(inputs):
    import numpy as np

    a = {k: np.asarray(v) for k, v in inputs.items()}
    f = np.float32
    out = {}
    x = a["x"].reshape(B, SIDE, 4, SIDE, 4).transpose(2, 4, 0, 1, 3).reshape(16, B * TOK)
    out["patches"] = np.concatenate([x, np.ones((1, B * TOK), f)])
    out["w_patch"] = np.concatenate([a["L0_tok_pe_w"].reshape(C, 16).T, a["L0_tok_pe_b"][None]])
    out["patch_norm"] = np.repeat(np.stack([a["L0_tok_pe_ng"], a["L0_tok_pe_nb"]])[None], 112, 0)
    out["ident"] = np.eye(P, dtype=f)
    out["head_mask"] = np.repeat(np.eye(SH, dtype=f), SD, 0)
    yx = np.stack(np.meshgrid(np.arange(WIN), np.arange(WIN), indexing="ij")).reshape(2, -1)
    rel = yx[:, :, None] - yx[:, None, :] + WIN - 1
    rpi = rel[0] * (2 * WIN - 1) + rel[1]
    rows = lambda w, b: np.concatenate([w.T, b[None]])
    for i in range(2):
        out[f"norm1_{i}"] = np.stack([a["L0_tok_n1g"][i], a["L0_tok_n1b"][i]], 1)
        out[f"norm2_{i}"] = np.stack([a["L0_tok_n2g"][i], a["L0_tok_n2b"][i]], 1)
        w, b = a["L0_tok_qkv_w"][i], a["L0_tok_qkv_b"][i]
        for n, name in enumerate(("wq", "wk", "wv")):
            out[f"{name}_{i}"] = rows(w[n * C:(n + 1) * C], b[n * C:(n + 1) * C])
        out[f"wproj_{i}"] = rows(a["L0_tok_proj_w"][i], a["L0_tok_proj_b"][i])
        table = a["L0_tok_rpb"][i][rpi].transpose(0, 2, 1).reshape(NW, SH * NW)
        wide = np.zeros((P, 4, SH * NW), f)
        for h in range(2):
            wide[SLOT * h:SLOT * h + NW] = table[:, None, :]
        out[f"bias_{i}"] = wide[None]
        out[f"w1_{i}"] = rows(a["L0_tok_w1"][i], a["L0_tok_b1"][i])
        out[f"w2_{i}"] = a["L0_tok_w2"][i].T.reshape(2, P, C).transpose(1, 0, 2)
        out[f"b2_{i}"] = a["L0_tok_b2"][i][None]
    region = lambda last: np.where(last & (np.arange(WIN) >= WIN - SHIFT), 1, 0)
    mask = np.zeros((2, P, 4, SH, NW), f)
    for kind in range(2):
        for pair in range(4):
            for h in range(2):
                ry, rx = region(kind == 1), region(2 * pair + h == ROWS - 1)
                reg = (ry[:, None] * 2 + rx[None, :]).reshape(-1)
                m = np.where(reg[:, None] != reg[None, :], f(-100), f(0))
                mask[kind, SLOT * h:SLOT * h + NW, pair] = m[:, None, :]
    out["mask"] = mask.reshape(2, P, 4, SH * NW)
    out["bias_1"] = np.repeat(out["bias_1"], 2, 0)
    out["w_qkv"] = np.concatenate([a["L0_attn_w_qkv"], a["L0_attn_b_qkv"][None]])
    out["w_proj"] = np.concatenate([a["L0_attn_w_proj"], a["L0_attn_b_proj"][None]])
    out["f_qkv"] = np.concatenate([a["L0_ffn_wq"], a["L0_ffn_wk"], a["L0_ffn_wv"]]).T
    out["f_out"] = a["L0_ffn_wo"].T
    out["f_norm1"] = a["L0_ffn_ln1_w"][:, None]
    out["f_norm2"] = a["L0_ffn_ln2_w"][:, None]
    E, unit = a["L0_ffn_w1"].shape[:2]
    hidden = -(-E * unit // P) * P
    wide = lambda w: np.concatenate([w, np.zeros((hidden - len(w), w.shape[1]), f)])
    for n in ("w1", "w3"):
        out[f"e_{n}"] = np.tile(wide(a[f"L0_ffn_{n}"].reshape(E * unit, C)).T, (2, 1))
    out["e_w2"] = wide(a["L0_ffn_w2"].transpose(0, 2, 1).reshape(E * unit, C)).reshape(-1, P, C).transpose(1, 0, 2)
    out["selector"] = np.tile(wide(np.repeat(np.eye(E, dtype=f), unit, 0)).T, (3, 1))
    out["router"] = a["L0_ffn_router_w"].T
    out["rank"] = np.repeat(np.arange(E, 0, -1, dtype=f)[None], P, 0)
    D = 16
    inv_freq = 1.0 / 10000.0 ** (np.arange(0, D, 2, dtype=f) / D)
    angles = np.outer(np.arange(SEQP, dtype=f), inv_freq).astype(f)
    out["cos"] = np.cos(np.concatenate([angles, angles], 1)).astype(f)
    out["sin"] = np.concatenate([-np.sin(angles), np.sin(angles)], 1).astype(f)
    out["later"] = np.triu(np.full((P, P), -1e30, f), 1)
    out["later_t"] = out["later"].T
    out["cls"] = a["cls_tok"].reshape(1, C)
    out["zeros"] = np.zeros((SEQP - SEQ, C), f)
    return {k: np.ascontiguousarray(v) for k, v in out.items()}


def kernel(**inputs):
    import concourse.bacc as _bacc
    from concourse.bass_utils import run_bass_kernel_spmd as _run

    arrays = host_layout(inputs)
    nc = _bacc.Bacc("TRN2", target_bir_lowering=False, num_devices=1)
    args = {k: nc.dram_tensor(f"in_{k}", v.shape, mybir.dt.from_np(v.dtype), kind="ExternalInput").ap()
            for k, v in arrays.items()}
    out = nc.dram_tensor("out_0_dram", (B, SEQ, C), F32, kind="ExternalOutput").ap()
    program(nc, args, out)
    r = _run(nc, [{f"in_{k}": v for k, v in arrays.items()}], core_ids=[0])
    return r.results[0]["out_0_dram"]
```

```python
from contextlib import ExitStack

import concourse.bass as bass
from concourse import mybir

F32 = mybir.dt.float32
BF16 = mybir.dt.bfloat16
U32 = mybir.dt.uint32
ALU = mybir.AluOpType
ACT = mybir.ActivationFunctionType
AX = mybir.AxisListType

B = 8
SIDE = 56
TOK = SIDE * SIDE
C = 64
WIN = 7
NW = WIN * WIN
ROWS = SIDE // WIN
SHIFT = WIN // 2
PAD = SIDE + SHIFT
SH = 8
SD = C // SH
SLOT = 64
LN_EPS = 1e-5
RMS_EPS = 1e-6

SEQ = TOK + 1
P = 128
TILES = -(-SEQ // P)
SEQP = TILES * P
LAST = SEQ - (TILES - 1) * P
GT = 5
GROUPS = TILES // GT
QW = 512
QBLOCKS = SEQP // QW


START = 1


def phase_tools(nc, ctx):
    def sb(name, shape, dt=F32):
        return ctx.enter_context(nc.sbuf_tensor(name, shape, dt))

    def ps(name, shape, dt=F32):
        return ctx.enter_context(nc.psum_tensor(name, shape, dt))

    sems = []

    def sem(name):
        sems.append(nc.alloc_semaphore(name))
        return sems[-1]

    def begin():
        for s in sems:
            nc.gpsimd.sem_inc(s, START)
        nc.all_engine_barrier()

    def clear():
        nc.clear_and_free_semaphores(sems)
        nc.all_engine_barrier()

    ctx.callback(clear)
    return sb, ps, sem, begin


class Steps:

    def __init__(self, eng, sem, per):
        self.eng, self.sem, self.per, self.at = eng, sem, per, 0

    def start(self, i):
        assert self.at in (0, self.per), (self.at, self.per)
        self.i, self.at = i, 0

    def link(self, ins):
        ins.then_inc(self.sem, 1)
        self.at += 1
        self.eng.wait_ge(self.sem, START + self.i * self.per + self.at)


def bcast(ap, n):
    shape = list(ap.shape)
    return ap.unsqueeze(len(shape)).to_broadcast(shape + [n])


def centred_and_variance(nc, steps, x, xs, sq, mean, var, eps, var_ready):
    steps.link(nc.vector.reduce_sum(mean, x, AX.X))
    steps.link(nc.vector.tensor_scalar(mean, mean, 1.0 / C, None, ALU.mult))
    steps.link(nc.vector.tensor_tensor(xs, x, bcast(mean, C), ALU.subtract))
    steps.link(nc.vector.tensor_tensor(sq, xs, xs, ALU.mult))
    steps.link(nc.vector.reduce_sum(var, sq, AX.X))
    nc.vector.tensor_scalar(var, var, 1.0 / C, eps, ALU.mult, ALU.add).then_inc(var_ready, 1)


def patch_embed(nc, patches, w_patch, norm_rows, tokens):
    TP, G = 112, 4
    NG = B * TOK // (TP * G)
    K = 17
    with ExitStack() as ctx:
        sb, ps, sem, begin = phase_tools(nc, ctx)
        w = sb("pe_w", [K, C])
        rows = sb("pe_rows", [TP, 2, C])
        px = [sb(f"pe_px{u}", [K, TP * G]) for u in range(2)]
        xs = [sb(f"pe_xs{u}", [TP, G, C]) for u in range(2)]
        sq = [sb(f"pe_sq{u}", [TP, G, C]) for u in range(2)]
        y = [sb(f"pe_y{u}", [TP, G, C]) for u in range(2)]
        mean = [sb(f"pe_mean{u}", [TP, G]) for u in range(2)]
        var = [sb(f"pe_var{u}", [TP, G]) for u in range(2)]
        rstd = [sb(f"pe_rstd{u}", [TP, G]) for u in range(2)]
        half = sb("pe_half", [TP, G])
        psx = [ps(f"pe_psx{u}", [TP, 512]) for u in range(2)]

        consts = sem("pe_consts")
        half_set = sem("pe_half_set")
        loaded = [sem(f"pe_loaded{u}") for u in range(2)]
        embedded = [sem(f"pe_embedded{u}") for u in range(2)]
        chain = [sem(f"pe_chain{u}") for u in range(2)]
        var_ready = [sem(f"pe_var_ready{u}") for u in range(2)]
        rstd_ready = [sem(f"pe_rstd_ready{u}") for u in range(2)]
        y_ready = [sem(f"pe_y_ready{u}") for u in range(2)]
        stored = [sem(f"pe_stored{u}") for u in range(2)]
        CH = 7
        out_v = tokens.rearrange("(n g p) c -> n p g c", g=G, p=TP)
        begin()
        with nc.Block() as block:
            @block.sync
            def _(sp):
                sp.dma_start(w[:, :], w_patch).then_inc(consts, 16)
                sp.dma_start(rows[:, :, :], norm_rows).then_inc(consts, 16)
                with sp.Fori(0, NG // 2) as i:
                    for u in range(2):
                        sp.wait_ge(embedded[u], START + i)
                        sp.dma_start(px[u][:, :], patches[:, bass.ts(i * 2 + u, TP * G)]).then_inc(loaded[u], 16)

            @block.tensor
            def _(pe):
                pe.wait_ge(consts, START + 32)
                with pe.Fori(0, NG // 2) as i:
                    for u in range(2):
                        pe.wait_ge(loaded[u], START + 16 * i + 16)
                        pe.wait_ge(chain[u], START + CH * i)
                        for g in range(G):
                            last = nc.tensor.matmul(psx[u][:, g * C:(g + 1) * C], px[u][:, g * TP:(g + 1) * TP],
                                                    w[:, :], start=True, stop=True)
                        last.then_inc(embedded[u], 1)

            @block.vector
            def _(dve):
                dve.wait_ge(consts, START + 32)
                steps = [Steps(dve, chain[u], CH) for u in range(2)]
                with dve.Fori(0, NG // 2) as i:
                    for u in range(2):
                        steps[u].start(i)
                        x = psx[u][:, 0:G * C].rearrange("p (g c) -> p g c", c=C)
                        dve.wait_ge(embedded[u], START + i + 1)
                        centred_and_variance(nc, steps[u], x, xs[u][:, :, :], sq[u][:, :, :], mean[u][:, :],
                                             var[u][:, :], LN_EPS, var_ready[u])
                        dve.wait_ge(rstd_ready[u], START + i + 1)
                        steps[u].link(nc.vector.tensor_tensor(xs[u][:, :, :], xs[u][:, :, :], bcast(rstd[u][:, :], C), ALU.mult))
                        g_row = rows[:, 0, :].unsqueeze(1).to_broadcast([TP, G, C])
                        b_row = rows[:, 1, :].unsqueeze(1).to_broadcast([TP, G, C])
                        steps[u].link(nc.vector.tensor_tensor(xs[u][:, :, :], xs[u][:, :, :], g_row, ALU.mult))
                        dve.wait_ge(stored[u], START + 16 * i)
                        nc.vector.tensor_tensor(y[u][:, :, :], xs[u][:, :, :], b_row, ALU.add).then_inc(y_ready[u], 1)

            @block.gpsimd
            def _(pool):
                nc.gpsimd.memset(half[:, :], -0.5).then_inc(half_set, 1)
                pool.wait_ge(half_set, START + 1)
                with pool.Fori(0, NG // 2) as i:
                    for u in range(2):
                        pool.wait_ge(var_ready[u], START + i + 1)
                        nc.gpsimd.tensor_tensor(rstd[u][:, :], var[u][:, :], half[:, :], ALU.pow).then_inc(rstd_ready[u], 1)

            @block.scalar
            def _(act):
                with act.Fori(0, NG // 2) as i:
                    for u in range(2):
                        act.wait_ge(y_ready[u], START + i + 1)
                        act.dma_start(out_v[i * 2 + u], y[u][:, :, :]).then_inc(stored[u], 16)
                for u in range(2):
                    act.wait_ge(stored[u], START + 16 * (NG // 2))


class Row:

    def __init__(self, quad, u):
        self.quad, self.u = quad, u
        self.n = quad * 4 + u
        self.ring4, self.ring2 = u % 4, u % 2
        self.round4 = quad + u // 4
        self.round2 = quad * 2 + u // 2

    def next(self, d):
        return Row(self.quad, self.u + d)


def window_attention(nc, tag, image, offset, norm_cols, w_q, w_k, w_v, w_proj, bias, mask, n_kinds, head_mask, ident_in):
    K = C + 1
    PAIRS = 4
    HJ = SH * NW
    HP = SH // 2
    VW = 2 * SD + 2
    ALL = B * ROWS
    with ExitStack() as ctx:
        sb, ps, sem_, begin = phase_tools(nc, ctx)
        sem = lambda name: sem_(f"{tag}_{name}")
        nm = lambda name: f"{tag}_{name}"
        ident = sb(nm("ident"), [P, P])
        ncol = sb(nm("ncol"), [C, 2])
        wq, wk, wv, wp = (sb(nm(n), [K, C]) for n in ("wq", "wk", "wv", "wp"))
        hm = sb(nm("hm"), [C, SH])
        tab = sb(nm("tab"), [P, n_kinds, PAIRS, HJ])
        mtab = sb(nm("mtab"), [P, n_kinds, PAIRS, HJ]) if mask is not None else None
        n_consts = 8 + (mask is not None)
        half = sb(nm("half"), [P, PAIRS])
        x = [sb(nm(f"x{u}"), [P, PAIRS, C]) for u in range(4)]
        xs = sb(nm("xs"), [P, PAIRS, C])
        sq = sb(nm("sq"), [P, PAIRS, C])
        mean, var, rstd = (sb(nm(n), [P, PAIRS]) for n in ("mean", "var", "rstd"))
        ht = sb(nm("ht"), [K, PAIRS, P])
        qs = sb(nm("qs"), [C, PAIRS, P])
        kx = sb(nm("kx"), [C, 8, SH, NW])
        v2 = [sb(nm(f"v2_{u}"), [P, 8, HP, VW]) for u in range(2)]
        s = sb(nm("s"), [P, PAIRS, SH, NW])
        mx = sb(nm("mx"), [P, PAIRS, SH])
        pr = sb(nm("pr"), [P, PAIRS, SH, SLOT])
        pt = [sb(nm(f"pt{j}"), [P, HP, P]) for j in range(PAIRS)]
        rden = sb(nm("rden"), [P, PAIRS * HP, 2])
        on = sb(nm("on"), [P, PAIRS, C])
        ot = sb(nm("ot"), [K, PAIRS, P])
        y = [sb(nm(f"y{u}"), [P, PAIRS, C]) for u in range(2)]
        bank_t = ps(nm("bank_t"), [P, 512])
        bank_q = ps(nm("bank_q"), [P, 512])
        bank_k = ps(nm("bank_k"), [P, 512])
        bank_v = ps(nm("bank_v"), [P, 512])
        bank_s = ps(nm("bank_s"), [P, PAIRS, 512])

        consts, zeroed, tab_ready, taken = map(sem, ("consts", "zeroed", "tab_ready", "taken"))
        loaded = [sem(f"loaded{u}") for u in range(4)]
        stored = [sem(f"stored{u}") for u in range(2)]
        (norm_chain, soft_chain, div_chain, var_ready, rstd_ready, xn_ready, xt_ready, ht_ready, q_ready, k_ready,
         v_ready, qs_ready, kx_ready, v2_ready, s_ready, sub_ready, exp_ready, ptr_ready, pt_ready, weighed, on_ready,
         ot_ps_ready, ot_ready, y_ps_ready, y_ready) = map(sem, (
             "norm_chain", "soft_chain", "div_chain", "var_ready", "rstd_ready", "xn_ready", "xt_ready", "ht_ready",
             "q_ready", "k_ready", "v_ready", "qs_ready", "kx_ready", "v2_ready", "s_ready", "sub_ready", "exp_ready",
             "ptr_ready", "pt_ready", "weighed", "on_ready", "ot_ps_ready", "ot_ready", "y_ps_ready", "y_ready"))
        FILLS = 14

        def window_row(b, r):
            rows = image[b, bass.ds(r * WIN + offset, WIN), offset:offset + SIDE, :]
            v = rows.rearrange("r (p two c) ch -> two p r c ch", two=2, c=WIN)
            return [(h, p, v[h, p]) for h in range(2) for p in range(PAIRS)]

        def all_steps(eng, step):
            step(Row(0, 0), 0)
            with eng.Fori(0, B - 1) as b:
                with eng.Fori(0, 2) as j:
                    for u in range(1, 5):
                        step(Row(b * 2 + j, u), j if u == 3 and n_kinds == 2 else 0)
            for u in range(1, ROWS):
                step(Row((B - 1) * 2, u), (n_kinds - 1) * (u == ROWS - 1))

        def exists(row):
            return not isinstance(row.n, int) or 0 <= row.n < ALL

        begin()
        with nc.Block() as block:
            @block.sync
            def _(sp):
                def load(b, r):
                    for h, p, view in window_row(b, r):
                        sp.dma_start(x[r % 4][SLOT * h:SLOT * h + NW, p, :], view).then_inc(loaded[r % 4], 16)

                def store(b, r):
                    sp.wait_ge(y_ready, START + b * ROWS + r + 1)
                    for h, p, view in window_row(b, r):
                        sp.dma_start(view, y[r % 2][SLOT * h:SLOT * h + NW, p, :]).then_inc(stored[r % 2], 16)

                for dst, src in ((ident[:, :], ident_in), (ncol[:, :], norm_cols), (wq[:, :], w_q), (wk[:, :], w_k),
                                 (wv[:, :], w_v), (wp[:, :], w_proj), (hm[:, :], head_mask),
                                 (tab[:, :, :, :], bias.rearrange("k p w n -> p k w n"))):
                    sp.dma_start(dst, src).then_inc(consts, 16)
                if mask is not None:
                    sp.dma_start(mtab[:, :, :, :], mask.rearrange("k p w n -> p k w n")).then_inc(consts, 16)
                sp.wait_ge(zeroed, START + 4)
                for r in range(4):
                    load(0, r)
                with sp.Fori(0, B - 1) as b:
                    for r in range(ROWS):
                        store(b, r)
                        load(b + (r + 4) // ROWS, (r + 4) % ROWS)
                for r in range(ROWS):
                    store(B - 1, r)
                    if r + 4 < ROWS:
                        load(B - 1, r + 4)
                for u in range(2):
                    sp.wait_ge(stored[u], START + 16 * 8 * ALL // 2)

            @block.gpsimd
            def _(pool):
                fills = ([(t[:, :, :], 0.0) for t in x] + [(pr[:, :, :, :], 0.0), (half[:, :], -0.5),
                         (ht[C:K, :, :], 1.0), (ot[C:K, :, :], 1.0)] + [(t[:, :, :, :], 0.0) for t in v2]
                         + [(t[0:SLOT, :, :, 2 * SD:2 * SD + 1], 1.0) for t in v2])
                fills += [(t[SLOT:P, :, :, 2 * SD + 1:VW], 1.0) for t in v2]
                assert len(fills) == FILLS
                for n, (dst, value) in enumerate(fills):
                    pool.wait_ge(zeroed, START + n)
                    nc.gpsimd.memset(dst, value).then_inc(zeroed, 1)

                with pool.Fori(0, ALL) as i:
                    pool.wait_ge(var_ready, START + i + 1)
                    nc.gpsimd.tensor_tensor(rstd[:, :], var[:, :], half[:, :], ALU.pow).then_inc(rstd_ready, 1)

            @block.vector
            def _(dve):
                norm_steps, soft_steps, div_steps = Steps(dve, norm_chain, 5), Steps(dve, soft_chain, 2), Steps(dve, div_chain, 1)

                def centre(row):
                    norm_steps.start(row.n)
                    dve.wait_ge(loaded[row.ring4], START + 16 * 8 * (row.round4 + 1))
                    centred_and_variance(nc, norm_steps, x[row.ring4][:, :, :], xs[:, :, :], sq[:, :, :], mean[:, :],
                                         var[:, :], LN_EPS, var_ready)

                def scale(row):
                    dve.wait_ge(rstd_ready, START + row.n + 1)
                    nc.vector.tensor_tensor(xs[:, :, :], xs[:, :, :], bcast(rstd[:, :], C), ALU.mult).then_inc(xn_ready, 1)

                def spread_keys(row):
                    dve.wait_ge(k_ready, START + row.n + 1)
                    kp = bank_k[0:C, :].rearrange("c (w j) -> c w j", j=SLOT)
                    for w in range(8):
                        ins = nc.vector.tensor_tensor(kx[:, w, :, :], kp[:, w, 0:NW].unsqueeze(1).to_broadcast([C, SH, NW]),
                                                      bcast(hm[:, :], NW), ALU.mult)
                    ins.then_inc(kx_ready, 1)

                def softmax(row, kind):
                    soft_steps.start(row.n)
                    dve.wait_ge(s_ready, START + row.n + 1)
                    flat = s[:, :, :, :].rearrange("p w h j -> p w (h j)")
                    t = tab[:, kind, :, :] if isinstance(kind, int) else tab[:, bass.ds(kind, 1), :, :].rearrange("p k w n -> p (k w) n")
                    soft_steps.link(nc.vector.tensor_tensor(flat, bank_s[:, :, 0:HJ], t, ALU.add))
                    soft_steps.link(nc.vector.reduce_max(mx[:, :, :], s[:, :, :, :], AX.X))
                    nc.vector.tensor_tensor(s[:, :, :, :].rearrange("p w h j -> p (w h) j"), s[:, :, :, :].rearrange("p w h j -> p (w h) j"),
                                            bcast(mx[:, :, :].rearrange("p w h -> p (w h)"), NW), ALU.subtract).then_inc(sub_ready, 1)

                def divide(row):
                    div_steps.start(row.n)
                    dve.wait_ge(weighed, START + PAIRS * (row.n + 1))
                    o = bank_q[:, 0:PAIRS * HP * VW].rearrange("p (a v) -> p a v", v=VW)
                    div_steps.link(nc.vector.reciprocal(rden[:, :, :], o[:, :, 2 * SD:VW]))
                    for e in range(2):
                        src = o[:, :, e * SD:(e + 1) * SD]
                        dst = on[:, :, :].rearrange("p w (a two d) -> p (w a) two d", two=2, d=SD)[:, :, e, :]
                        ins = nc.vector.tensor_tensor(dst, src, bcast(rden[:, :, e], SD), ALU.mult)
                    ins.then_inc(on_ready, 1)

                def add_residual(row):
                    dve.wait_ge(y_ps_ready, START + row.n + 1)
                    dve.wait_ge(stored[row.ring2], START + 16 * 8 * row.round2)
                    yp = bank_t[:, 0:PAIRS * C].rearrange("p (w c) -> p w c", c=C)
                    nc.vector.tensor_tensor(y[row.ring2][:, :, :], yp, x[row.ring4][:, :, :], ALU.add).then_inc(y_ready, 1)

                def step(row, kind):
                    softmax(row, kind)
                    if row.u > 0:
                        add_residual(row.next(-1))
                    if exists(row.next(1)):
                        spread_keys(row.next(1))
                    if exists(row.next(2)):
                        centre(row.next(2))
                    divide(row)
                    if exists(row.next(2)):
                        scale(row.next(2))

                dve.wait_ge(consts, START + 16 * n_consts)
                dve.wait_ge(zeroed, START + FILLS)
                if mask is not None:
                    nc.vector.tensor_tensor(tab[:, :, :, :], tab[:, :, :, :], mtab[:, :, :, :], ALU.add).then_inc(tab_ready, 1)
                    dve.wait_ge(tab_ready, START + 1)
                centre(Row(0, 0))
                scale(Row(0, 0))
                spread_keys(Row(0, 0))
                centre(Row(0, 1))
                scale(Row(0, 1))
                all_steps(dve, step)
                add_residual(Row(0, ALL - 1))

            @block.tensor
            def _(pe):
                def settled():
                    pe.sem_inc(taken, 1)

                def transpose_input(row):
                    pe.wait_ge(xn_ready, START + row.n + 1)
                    settled()
                    for p in range(PAIRS):
                        ins = nc.tensor.transpose(bank_k[0:C, p * P:(p + 1) * P], xs[:, p, :], ident[:, :])
                    ins.then_inc(xt_ready, 1)

                def embed(row):
                    pe.wait_ge(ht_ready, START + row.n + 1)
                    pe.wait_ge(v2_ready, START + row.n)
                    settled()
                    flat = ht[:, :, :].rearrange("k w t -> k (w t)")
                    nc.tensor.matmul(bank_q[0:C, :], wq[:, :], flat, start=True, stop=True).then_inc(q_ready, 1)
                    nc.tensor.matmul(bank_k[0:C, :], wk[:, :], flat, start=True, stop=True).then_inc(k_ready, 1)
                    for w in range(8):
                        for h in range(2):
                            ins = nc.tensor.matmul(bank_v[SLOT * h:SLOT * (h + 1), w * C:(w + 1) * C],
                                                   ht[:, w // 2, SLOT * (w % 2):SLOT * (w % 2) + SLOT], wv[:, :],
                                                   start=True, stop=True)
                    ins.then_inc(v_ready, 1)

                def scores(row):
                    pe.wait_ge(qs_ready, START + row.n + 1)
                    pe.wait_ge(kx_ready, START + row.n + 1)
                    pe.wait_ge(pt_ready, START + PAIRS * row.n)
                    settled()
                    for w in range(8):
                        lo = SLOT * (w % 2)
                        ins = nc.tensor.matmul(bank_s[lo:lo + SLOT, w // 2, 0:HJ], qs[:, w // 2, lo:lo + SLOT],
                                               kx[:, w, :, :].rearrange("c h j -> c (h j)"), start=True, stop=True)
                    ins.then_inc(s_ready, 1)

                def weigh(row, more):
                    def turned(p):
                        pe.wait_ge(pt_ready, START + PAIRS * row.n + p + 1)
                        settled()
                        for h in range(2):
                            for a in range(HP):
                                col = (p * HP + a) * VW
                                ins = nc.tensor.matmul(bank_q[SLOT * h:SLOT * (h + 1), col:col + VW],
                                                       pt[p][:, a, SLOT * h:SLOT * (h + 1)], v2[row.ring2][:, 2 * p + h, a, :],
                                                       start=True, stop=True)
                        ins.then_inc(weighed, 1)

                    pe.wait_ge(exp_ready, START + row.n + 1)
                    pe.wait_ge(v2_ready, START + row.n + 1)
                    if more:
                        pe.wait_ge(qs_ready, START + row.n + 2)
                    settled()
                    for p in range(PAIRS):
                        for a in range(HP):
                            ins = nc.tensor.transpose(bank_s[:, p, a * P:(a + 1) * P],
                                                      pr[:, p, 2 * a:2 * a + 2, :].rearrange("p h j -> p (h j)"), ident[:, :])
                        ins.then_inc(ptr_ready, 1)
                        if p >= 1:
                            turned(p - 1)
                    turned(PAIRS - 1)

                def transpose_output(row):
                    pe.wait_ge(on_ready, START + row.n + 1)
                    pe.wait_ge(y_ready, START + row.n)
                    settled()
                    for p in range(PAIRS):
                        ins = nc.tensor.transpose(bank_t[0:C, p * P:(p + 1) * P], on[:, p, :], ident[:, :])
                    ins.then_inc(ot_ps_ready, 1)

                def project(row):
                    pe.wait_ge(ot_ready, START + row.n + 1)
                    settled()
                    for p in range(PAIRS):
                        ins = nc.tensor.matmul(bank_t[:, p * C:(p + 1) * C], ot[:, p, :], wp[:, :], start=True, stop=True)
                    ins.then_inc(y_ps_ready, 1)

                def step(row, kind):
                    more = exists(row.next(1))
                    scores(row)
                    if row.u > 0:
                        transpose_output(row.next(-1))
                    if more:
                        transpose_input(row.next(1))
                    if row.u > 0:
                        project(row.next(-1))
                    if more:
                        embed(row.next(1))
                    weigh(row, more)

                pe.wait_ge(consts, START + 16 * n_consts)
                pe.wait_ge(zeroed, START + FILLS)
                transpose_input(Row(0, 0))
                embed(Row(0, 0))
                all_steps(pe, step)
                transpose_output(Row(0, ALL - 1))
                project(Row(0, ALL - 1))

            @block.scalar
            def _(act):
                def normed(row):
                    act.wait_ge(xt_ready, START + row.n + 1)
                    act.wait_ge(v_ready, START + row.n)
                    nc.scalar.activation(ht[0:C, :, :].rearrange("c w t -> c (w t)"), bank_k[0:C, :], ACT.Identity,
                                         bias=ncol[:, 1:2], scale=ncol[:, 0:1]).then_inc(ht_ready, 1)

                def queries(row):
                    act.wait_ge(q_ready, START + row.n + 1)
                    act.wait_ge(s_ready, START + row.n)
                    nc.scalar.activation(qs[:, :, :].rearrange("c w t -> c (w t)"), bank_q[0:C, :], ACT.Copy,
                                         scale=float(SD) ** -0.5).then_inc(qs_ready, 1)

                def values(row):
                    act.wait_ge(v_ready, START + row.n + 1)
                    for e in range(2):
                        src = bank_v[SLOT * e:SLOT * (e + 1), :].rearrange("p (w a two d) -> p (w a) two d", w=8, a=HP, two=2)[:, :, e, :]
                        dst = v2[row.ring2][SLOT * e:SLOT * (e + 1), :, :, e * SD:(e + 1) * SD].rearrange("p w a d -> p (w a) d")
                        ins = nc.scalar.activation(dst, src, ACT.Copy)
                    ins.then_inc(v2_ready, 1)

                def exponentiate(row):
                    act.wait_ge(sub_ready, START + row.n + 1)
                    act.wait_ge(weighed, START + PAIRS * row.n)
                    nc.scalar.activation(pr[:, :, :, 0:NW].rearrange("p w h j -> p (w h) j"),
                                         s[:, :, :, :].rearrange("p w h j -> p (w h) j"), ACT.Exp).then_inc(exp_ready, 1)

                def turn(row):
                    for p in range(PAIRS):
                        act.wait_ge(ptr_ready, START + PAIRS * row.n + p + 1)
                        nc.scalar.activation(pt[p][:, :, :].rearrange("p a t -> p (a t)"), bank_s[:, p, :], ACT.Copy).then_inc(pt_ready, 1)

                def outputs(row):
                    act.wait_ge(ot_ps_ready, START + row.n + 1)
                    act.wait_ge(y_ps_ready, START + row.n)
                    nc.scalar.activation(ot[0:C, :, :].rearrange("c w t -> c (w t)"), bank_t[0:C, :], ACT.Copy).then_inc(ot_ready, 1)

                def step(row, kind):
                    if row.u > 0:
                        outputs(row.next(-1))
                    if exists(row.next(1)):
                        normed(row.next(1))
                        queries(row.next(1))
                    exponentiate(row)
                    if exists(row.next(1)):
                        values(row.next(1))
                    turn(row)

                act.wait_ge(consts, START + 16 * n_consts)
                act.wait_ge(zeroed, START + FILLS)
                normed(Row(0, 0))
                queries(Row(0, 0))
                values(Row(0, 0))
                all_steps(act, step)
                outputs(Row(0, ALL - 1))


def mlp(nc, tag, src, dst, norm_cols, w_1, w_2, b_2, ident_in):
    TP, G = 112, 4
    NG = B * TOK // (TP * G)
    K, HK = C + 1, 4 * C // P
    with ExitStack() as ctx:
        sb, ps, sem_, begin = phase_tools(nc, ctx)
        sem = lambda name: sem_(f"{tag}_{name}")
        two = lambda name: [sem(f"{name}{u}") for u in range(2)]
        nm = lambda name: f"{tag}_{name}"
        ident = sb(nm("ident"), [P, P])
        ncol = sb(nm("ncol"), [C, 2])
        w1 = sb(nm("w1"), [K, HK, P])
        w2 = sb(nm("w2"), [P, HK, C])
        b2 = sb(nm("b2"), [1, C])
        ones = sb(nm("ones"), [1, TP])
        half = sb(nm("half"), [TP, G])
        pairs = lambda name, shape: [sb(nm(f"{name}{u}"), shape) for u in range(2)]
        x, xs, sq, y = (pairs(n, [TP, G, C]) for n in ("x", "xs", "sq", "y"))
        mean, var, rstd = (pairs(n, [TP, G]) for n in ("mean", "var", "rstd"))
        ht = pairs("ht", [K, G * TP])
        act_h = pairs("act_h", [P, HK, G * TP])
        ps_t = [ps(nm(f"ps_t{u}"), [P, 512]) for u in range(2)]
        ps_h = [ps(nm(f"ps_h{u}"), [P, HK, 512]) for u in range(2)]
        ps_y = [ps(nm(f"ps_y{u}"), [P, 512]) for u in range(2)]
        consts, filled, taken = sem("consts"), sem("filled"), sem("taken")
        (loaded, stored, chain, var_ready, rstd_ready, xn_ready, xt_ready, ht_ready, h_ready, act_ready, y_ps_ready,
         y_ready) = map(two, ("loaded", "stored", "chain", "var_ready", "rstd_ready", "xn_ready", "xt_ready", "ht_ready",
                              "h_ready", "act_ready", "y_ps_ready", "y_ready"))
        CH = 5
        FILLS = 4
        begin()
        with nc.Block() as block:
            @block.sync
            def _(sp):
                for d, a in ((ident[:, :], ident_in), (ncol[:, :], norm_cols), (w1[:, :, :], w_1.rearrange("k (h p) -> k h p", p=P)),
                             (w2[:, :, :], w_2), (b2[:, :], b_2)):
                    sp.dma_start(d, a).then_inc(consts, 16)
                with sp.Fori(0, NG // 2) as i:
                    for u in range(2):
                        sp.wait_ge(y_ready[u], START + i)
                        sp.dma_start(x[u][:, :, :], src[i * 2 + u]).then_inc(loaded[u], 16)

            @block.gpsimd
            def _(pool):
                for n, (d, value) in enumerate(((half[:, :], -0.5), (ones[:, :], 1.0), (ht[0][C:K, :], 1.0), (ht[1][C:K, :], 1.0))):
                    pool.wait_ge(filled, START + n)
                    nc.gpsimd.memset(d, value).then_inc(filled, 1)
                pool.wait_ge(filled, START + FILLS)
                with pool.Fori(0, NG // 2) as i:
                    for u in range(2):
                        pool.wait_ge(var_ready[u], START + i + 1)
                        nc.gpsimd.tensor_tensor(rstd[u][:, :], var[u][:, :], half[:, :], ALU.pow).then_inc(rstd_ready[u], 1)

            @block.vector
            def _(dve):
                dve.wait_ge(consts, START + 16 * 5)
                dve.wait_ge(filled, START + FILLS)
                steps = [Steps(dve, chain[u], CH) for u in range(2)]

                def normalise(i, u):
                    steps[u].start(i)
                    dve.wait_ge(loaded[u], START + 16 * i + 16)
                    centred_and_variance(nc, steps[u], x[u][:, :, :], xs[u][:, :, :], sq[u][:, :, :], mean[u][:, :],
                                         var[u][:, :], LN_EPS, var_ready[u])

                def scale(i, u):
                    dve.wait_ge(rstd_ready[u], START + i + 1)
                    nc.vector.tensor_tensor(xs[u][:, :, :], xs[u][:, :, :], bcast(rstd[u][:, :], C), ALU.mult).then_inc(xn_ready[u], 1)

                def affine(i, u):
                    dve.wait_ge(xt_ready[u], START + i + 1)
                    dve.wait_ge(h_ready[u], START + i)
                    nc.vector.tensor_scalar(ht[u][0:C, :], ps_t[u][0:C, 0:G * TP], ncol[:, 0:1], ncol[:, 1:2],
                                            ALU.mult, ALU.add).then_inc(ht_ready[u], 1)

                def residual(i, u):
                    dve.wait_ge(y_ps_ready[u], START + i + 1)
                    dve.wait_ge(stored[u], START + 16 * i)
                    nc.vector.tensor_tensor(y[u][:, :, :], ps_y[u][0:TP, 0:G * C].rearrange("p (g c) -> p g c", c=C),
                                            x[u][:, :, :], ALU.add).then_inc(y_ready[u], 1)
                with dve.Fori(0, NG // 2) as i:
                    normalise(i, 0)
                    normalise(i, 1)
                    scale(i, 0)
                    scale(i, 1)
                    affine(i, 0)
                    affine(i, 1)
                    residual(i, 0)
                    residual(i, 1)

            @block.tensor
            def _(pe):
                pe.wait_ge(consts, START + 16 * 5)
                pe.wait_ge(filled, START + FILLS)

                def turn(i, u):
                    pe.wait_ge(xn_ready[u], START + i + 1)
                    pe.sem_inc(taken, 1)
                    for g in range(G):
                        ins = nc.tensor.transpose(ps_t[u][0:C, g * TP:(g + 1) * TP], xs[u][:, g, :], ident[0:TP, 0:TP])
                    ins.then_inc(xt_ready[u], 1)

                def up(i, u):
                    pe.wait_ge(ht_ready[u], START + i + 1)
                    for k in range(HK):
                        ins = nc.tensor.matmul(ps_h[u][:, k, 0:G * TP], w1[:, k, :], ht[u][:, :], start=True, stop=True)
                    ins.then_inc(h_ready[u], 1)

                def down(i, u):
                    pe.wait_ge(act_ready[u], START + i + 1)
                    for g in range(G):
                        out = ps_y[u][0:TP, g * C:(g + 1) * C]
                        for k in range(HK):
                            nc.tensor.matmul(out, act_h[u][:, k, g * TP:(g + 1) * TP], w2[:, k, :], start=(k == 0), stop=False)
                        ins = nc.tensor.matmul(out, ones[:, :], b2[:, :], start=False, stop=True)
                    ins.then_inc(y_ps_ready[u], 1)
                with pe.Fori(0, NG // 2) as i:
                    turn(i, 0)
                    turn(i, 1)
                    up(i, 0)
                    up(i, 1)
                    down(i, 0)
                    down(i, 1)

            @block.scalar
            def _(act):
                act.wait_ge(consts, START + 16 * 5)
                act.wait_ge(filled, START + FILLS)
                with act.Fori(0, NG // 2) as i:
                    for u in range(2):
                        act.wait_ge(h_ready[u], START + i + 1)
                        nc.scalar.activation(act_h[u][:, :, :], ps_h[u][:, :, 0:G * TP], ACT.Gelu).then_inc(act_ready[u], 1)
                    for u in range(2):
                        act.wait_ge(y_ready[u], START + i + 1)
                        act.dma_start(dst[i * 2 + u], y[u][:, :, :]).then_inc(stored[u], 16)
                for u in range(2):
                    act.wait_ge(stored[u], START + 16 * (NG // 2))


def copies(nc, tag, pairs):
    with ExitStack() as ctx:
        _, _, sem, begin = phase_tools(nc, ctx)
        done = sem(f"{tag}_done")
        begin()
        with nc.Block() as block:
            @block.sync
            def _(sp):
                n = 0
                for step in pairs:
                    for to, frm in step:
                        sp.dma_start(to, frm).then_inc(done, 16)
                        n += 16
                    sp.wait_ge(done, START + n)


Q_PART = (0, 0, 1, 1, 0, 2)
K_PART = (0, 1, 0, 1, 2, 0)
LIMIT = 43.0
RING = 3
PROBS = 5


def last_before(halves, n, ring):
    return max(m for m in range(halves) if m % ring == n)


class Work:

    def __init__(self, spans, width, kt_of, q_of, v_of, ident_b=None, later_b=None):
        self.spans, self.width, self.kt_of, self.q_of, self.v_of = spans, width, kt_of, q_of, v_of
        self.ident_b, self.later_b = ident_b, later_b


class Core:

    def __init__(self, nc, sb, ps, sem, dim):
        self.nc, self.dim = nc, dim
        self.ring = ps("ring", [P, RING, 2, 512])
        self.acc = ps("acc", [P, 512])
        self.turned = ps("turned", [P, 512])
        self.pb = [sb(f"probs{n}", [P, 2, QW]) for n in range(PROBS)]
        self.acc_sb = sb("acc_sb", [P, QW])
        self.rec = sb("rec", [P, QW // P, 4])
        self.taken, self.taken_dve = sem("taken"), sem("taken_dve")
        (self.scores_ready, self.exp_done, self.weighed, self.acc_copied, self.acc_turned, self.rec_done,
         self.block_done) = map(sem, ("scores_ready", "exp_done", "weighed", "acc_copied", "acc_turned", "rec_done",
                                      "block_done"))

        self.flag = sb("flag", [P, 1], U32)
        self.bound_part, self.bound_most = sb("bound_part", [P, 1]), sb("bound_most", [P, 1])
        self.row_max = sb("row_max", [P, 2])
        self.neg_max, self.neg_rest = sb("neg_max", [P, 1]), sb("neg_rest", [P, 1])
        (self.bound_part_ready, self.bound_most_ready, self.flag_ready, self.cleared, self.row_scores, self.row_read,
         self.row_step) = map(sem, ("bound_part_ready", "bound_most_ready", "flag_ready", "cleared",
                                         "row_scores", "row_read", "row_step"))

    def find_flag(self, dve, b, bound, shift_slots):
        nc = self.nc
        nc.vector.reduce_max(self.bound_part[:, :], bound, AX.XY).then_inc(self.bound_part_ready, 1)
        nc.vector.memset(shift_slots, 0.0).then_inc(self.cleared, 1)
        dve.wait_ge(self.bound_most_ready, START + b + 1)
        nc.vector.tensor_scalar(self.flag[:, :], self.bound_most[:, :], LIMIT, None, ALU.is_gt).then_inc(self.flag_ready, 1)
        dve.wait_ge(self.flag_ready, START + b + 1)
        dve.wait_ge(self.cleared, START + b + 1)
        dve.sem_inc(self.taken_dve, 1)

    def read_flag(self, eng):
        return eng.value_load(self.flag[0:1, 0:1], min_val=0, max_val=1)

    def widest_bound(self, pool, b):
        pool.wait_ge(self.bound_part_ready, START + b + 1)
        pool.sem_inc(self.taken, 1)
        self.nc.gpsimd.partition_all_reduce(self.bound_most[:, :], self.bound_part[:, :], P,
                                            bass.bass_isa.ReduceOp.max).then_inc(self.bound_most_ready, 1)

    def tensor_row_scores(self, pe, count, q_tile, keys_of, n_keys):
        pe.wait_ge(self.row_read, START + count)
        pe.sem_inc(self.taken, 1)
        flat = self.ring[:, :, :, :].rearrange("p a b c -> p (a b c)")
        for k0 in range(0, n_keys, 512):
            k1 = min(k0 + 512, n_keys)
            out = flat[:, k0:k1] if k0 < 3072 else self.turned[:, 0:k1 - k0]
            ins = self.nc.tensor.matmul(out, q_tile, keys_of(k0, k1), start=True, stop=True)
        ins.then_inc(self.row_scores, 1)

    def vector_row_max(self, dve, count, n_keys, shift, later=None, diagonal=None):
        v = self.nc.vector
        STEPS = 7
        done = [0]

        def link(ins):
            ins.then_inc(self.row_step, 1)
            done[0] += 1
            dve.wait_ge(self.row_step, START + STEPS * count + done[0])

        dve.wait_ge(self.row_scores, START + count + 1)
        flat = self.ring[:, :, :, :].rearrange("p a b c -> p (a b c)")
        edge = 3072 if later is None else n_keys // P * P - (P if n_keys % P == 0 else 0)
        tail = self.turned[:, 0:n_keys - edge] if edge == 3072 else flat[:, edge:n_keys]
        if later is not None:
            link(v.tensor_tensor(diagonal[:, 0:n_keys - edge], tail, later[:, 0:n_keys - edge], ALU.add))
            tail = diagonal[:, 0:n_keys - edge]
        else:
            link(v.memset(self.neg_rest[:, :], 0.0))
        if edge:
            v.reduce_max(self.row_max[:, 0:1], flat[:, 0:edge], AX.X)
        else:
            v.reduce_max(self.row_max[:, 0:1], tail, AX.X)
        link(v.reduce_max(self.row_max[:, 1:2], tail, AX.X))
        link(v.reduce_max(self.neg_max[:, :], self.row_max[:, :], AX.X, negate=True))
        link(v.tensor_copy(shift(0), self.neg_max[:, :]))
        link(v.tensor_tensor(self.neg_rest[:, :], self.neg_max[:, :], shift(0), ALU.subtract))
        link(v.tensor_copy(shift(1), self.neg_rest[:, :]))
        link(v.tensor_tensor(self.neg_rest[:, :], self.neg_rest[:, :], shift(1), ALU.subtract))
        v.tensor_copy(shift(2), self.neg_rest[:, :]).then_inc(self.row_read, 1)

    def keys(self, kt):
        return LAST if kt == TILES - 1 else P

    def weigh(self, pe, nb, units, work, kt):
        first, diagonal = work.spans[kt]
        if kt == 0:
            pe.wait_ge(self.acc_copied, START + nb)
        pe.wait_ge(self.exp_done, START + 2 * units + 2 * kt + 2)
        pe.sem_inc(self.taken, 1)
        for h in range(4):
            probs = self.pb[(2 * kt + h // 2) % PROBS]
            ins = self.nc.tensor.matmul(self.acc[32 * h:32 * h + self.dim + 1, first:work.width], work.v_of(kt, h),
                                        probs[0:self.keys(kt), h % 2, first:work.width],
                                        start=(kt == 0), stop=(diagonal or kt == len(work.spans) - 1),
                                        skip_group_check=first > 0)
        ins.then_inc(self.weighed, 1)

    def turn_sums(self, pe, nb, work, ident):
        pe.wait_ge(self.acc_copied, START + nb + 1)
        pe.wait_ge(self.block_done, START + nb)
        for t in range(work.width // P):
            ins = self.nc.tensor.transpose(self.turned[:, t * P:(t + 1) * P], self.acc_sb[:, t * P:(t + 1) * P], ident)
        ins.then_inc(self.acc_turned, 1)

    def tensor(self, pe, nb, units, work, before, ident, aside=None):
        nc = self.nc
        for kt, (first, diagonal) in enumerate(work.spans):
            for half in range(2):
                n = 2 * kt + half
                if n >= RING:
                    pe.wait_ge(self.exp_done, START + 2 * units + n - RING + 1)
                elif before is None:
                    pe.wait_ge(self.exp_done, START + 2 * units)
                else:
                    halves = 2 * len(before.spans)
                    pe.wait_ge(self.exp_done, START + 2 * units - halves + last_before(halves, n, RING) + 1)
                for h in (2 * half, 2 * half + 1):
                    ins = nc.tensor.matmul(self.ring[0:self.keys(kt), n % RING, h % 2, first:work.width],
                                           work.kt_of(kt, h), work.q_of(h, first), start=True, stop=True)
                    if diagonal:
                        ins = nc.tensor.matmul(self.ring[0:self.keys(kt), n % RING, h % 2, first:first + P],
                                               work.ident_b[:, 0:self.keys(kt)], work.later_b, start=False, stop=True,
                                               skip_group_check=True)
                ins.then_inc(self.scores_ready, 1)
            if kt == 0 and before is not None:
                self.weigh(pe, nb - 1, units - len(before.spans), before, len(before.spans) - 1)
            if kt == 1 and before is not None:
                self.turn_sums(pe, nb - 1, before, ident)
            if kt >= 1:
                self.weigh(pe, nb, units, work, kt - 1)
            if aside is not None:
                aside(kt)

    def tensor_end(self, pe, nb, units, work, ident):
        self.weigh(pe, nb, units, work, len(work.spans) - 1)
        self.turn_sums(pe, nb, work, ident)

    def scalar(self, act, nb, units, spans, width, before=None):
        for kt, (first, diagonal) in enumerate(spans):
            for half in range(2):
                n = 2 * kt + half
                act.wait_ge(self.scores_ready, START + 2 * units + n + 1)
                if n >= PROBS:
                    act.wait_ge(self.weighed, START + units + (n - PROBS) // 2 + 1)
                elif before is None:
                    act.wait_ge(self.weighed, START + units)
                else:
                    last = last_before(2 * len(before), n, PROBS)
                    act.wait_ge(self.weighed, START + units - len(before) + last // 2 + 1)
                keys = self.keys(kt)
                self.nc.scalar.activation(self.pb[n % PROBS][0:keys, :, first:width],
                                          self.ring[0:keys, n % RING, :, first:width], ACT.Exp).then_inc(self.exp_done, 1)

    def vector(self, dve, nb, units_after, width, out):
        nc = self.nc
        tiles = width // P
        dve.wait_ge(self.weighed, START + units_after)
        dve.wait_ge(self.acc_turned, START + nb)
        nc.vector.tensor_copy(self.acc_sb[:, 0:width], self.acc[:, 0:width]).then_inc(self.acc_copied, 1)
        dve.wait_ge(self.acc_turned, START + nb + 1)
        turned = self.turned[:, 0:width].rearrange("p (t h r) -> p t h r", h=4, r=32)
        nc.vector.reciprocal(self.rec[:, 0:tiles, :], turned[:, :, :, self.dim]).then_inc(self.rec_done, 1)
        dve.wait_ge(self.rec_done, START + nb + 1)
        for t in range(tiles):
            ins = nc.vector.tensor_tensor(out(t), turned[:, t, :, 0:self.dim], bcast(self.rec[:, t, :], self.dim), ALU.mult)
        ins.then_inc(self.block_done, 1)


def dense_attention(nc, src, dst, w_qkv, w_proj, ident_in):
    tag = "da"
    H, D = 16, 4
    HG = H // 4
    K = C + 1
    BLOCKS = QBLOCKS + 1
    ALL = [(0, False)] * TILES
    with ExitStack() as ctx:
        sb_, ps_, sem_, begin = phase_tools(nc, ctx)
        sb = lambda name, shape, dt=F32: sb_(f"{tag}_{name}", shape, dt)
        ps = lambda name, shape: ps_(f"{tag}_{name}", shape)
        sem = lambda name: sem_(f"{tag}_{name}")
        ident = sb("ident", [P, P])
        ident_b = sb("ident_b", [P, P], BF16)
        wqkv, wp = sb("wqkv", [K, 3 * C]), sb("wp", [K, C])
        x = sb("x", [P, TILES, C])
        xs = [sb(f"xs{u}", [P, GT, C]) for u in range(2)]
        sq = sb("sq", [P, GT, C])
        mean, var, rstd, half = (sb(n, [P, GT]) for n in ("mean", "var", "rstd", "half"))
        ht = sb("ht", [K, GT * P])
        part0 = [sb(f"part0_{u}", [P, GT, 2 * C], BF16) for u in range(2)]
        part1, part2 = (sb(f"part{n}", [P, GT, 2 * C], BF16) for n in (1, 2))
        rest = sb("rest", [P, GT, 2 * C])
        qk = [sb(f"qk{u}", [P, GT, 2 * C]) for u in range(2)]
        squares = [sb(f"squares{u}", [P, GT, 2 * C]) for u in range(2)]
        norm2 = sb("norm2", [P, TILES, 2 * H])
        k_part, k_most = sb("k_part", [P, H]), sb("k_most", [P, H])
        bound = sb("bound", [P, TILES, H])
        slots = [sb(f"slots_{n}", [P, TILES, H, 32], BF16) for n in ("q", "k")]
        qt = [sb(f"qt{u}", [P, 4, SEQP], BF16) for u in range(2)]
        kt = [sb(f"kt{u}", [P, SEQP], BF16) for u in range(2)]
        v = sb("v", [P, TILES, H, D + 1])
        rstd_spare = sb("rstd_spare", [1, 1])
        o = sb("o", [P, TILES, C])
        ot = sb("ot", [K, GT * P])
        y = sb("y", [P, GT, C])
        core = Core(nc, sb, ps, sem, D)
        flat_ring = core.ring[:, :, :, :].rearrange("p a b c -> p (a b c)")
        ps_t = flat_ring[:, 0:GT * P]
        ps_qkv = flat_ring[:, 1024:2560].rearrange("p (t c) -> p t c", c=256)
        ps_turn = [flat_ring[:, 0:GT * P], flat_ring[:, 1024:1024 + GT * P]]
        ps_y = flat_ring[:, 2560:2560 + GT * C].rearrange("p (t c) -> p t c", c=C)

        (consts, filled, ident_b_ready, zeroed_acc, loaded, chain, var_ready, rstd_ready, xn_ready, xt_ready, ht_ready,
         qkv_ready, qk_ready, part0_ready, part1_ready, rest_ready, squares_ready, v_ready, parts_ready, slots_ready,
         k_part_ready, k_most_ready, product_ready, bound_ready, shift_ready, turn_ready, turned_out_act, turned_out_dve, row_turn_ready, row_turned_out,
         k_slots_ready, side_ready, side_out, ot_ps_ready, ot_ready, y_ps_ready, y_ready, stored) = map(sem, (
             "consts", "filled", "ident_b_ready", "zeroed_acc", "loaded", "chain", "var_ready", "rstd_ready",
             "xn_ready", "xt_ready", "ht_ready", "qkv_ready", "qk_ready", "part0_ready", "part1_ready", "rest_ready",
             "squares_ready", "v_ready", "parts_ready", "slots_ready", "k_part_ready", "k_most_ready",
             "product_ready", "bound_ready", "shift_ready", "turn_ready", "turned_out_act", "turned_out_dve", "row_turn_ready",
             "row_turned_out", "k_slots_ready", "side_ready", "side_out", "ot_ps_ready",
             "ot_ready", "y_ps_ready", "y_ready", "stored"))
        CH = 5
        tile_view = lambda a, b: a[b].rearrange("(t p) c -> p t c", p=P)
        fills = [(half[:, :], -0.5), (ht[C:K, :], 1.0), (ot[C:K, :], 1.0), (v[:, :, :, D:D + 1], 1.0), (qt[0][:, :, :], 0.0),
                 (qt[1][:, :, :], 0.0), (kt[0][:, :], 0.0), (slots[0][:, :, :, :], 0.0), (slots[1][:, :, :, :], 0.0),
                 (slots[1][:, :, :, 24:27], 1.0)]
        FILLS = len(fills)

        def copy_turned(eng, copy, b, units):
            u, out = (0, turned_out_act) if eng is nc.scalar else (1, turned_out_dve)
            for n in units:
                w, g = (1, n) if n < GROUPS else (0, n - GROUPS)
                cols = slice(GT * P * g, GT * P * (g + 1))
                eng.wait_ge(turn_ready, START + 2 * GROUPS * b + n + 1)
                if w:
                    ins = copy(kt[0][:, cols], ps_turn[u])
                else:
                    for h in range(4):
                        rows = slice(32 * h, 32 * h + 32)
                        ins = copy(qt[0][rows, h, cols], ps_turn[u][rows, :])
                ins.then_inc(out, 1)

        def lay_out(eng, w, slot, part, parts, tiles):
            src_p = parts[part][:, :, w * C:(w + 1) * C].rearrange("p t (h d) -> p t h d", d=D)
            return eng.tensor_copy(slots[w][:, tiles, :, slot * D:(slot + 1) * D], src_p)

        begin()
        with nc.Block() as block:
            @block.sync
            def _(sp):
                for d, a in ((ident[:, :], ident_in), (wqkv[:, :], w_qkv), (wp[:, :], w_proj)):
                    sp.dma_start(d, a).then_inc(consts, 16)
                with sp.Fori(0, B) as b:
                    sp.wait_ge(y_ready, START + GROUPS * b)
                    sp.dma_start(x[:, :, :], tile_view(src, b)).then_inc(loaded, 16)

            @block.gpsimd
            def _(pool):
                for n, (d, value) in enumerate(fills):
                    pool.wait_ge(filled, START + n)
                    nc.gpsimd.memset(d, value).then_inc(filled, 1)
                pool.wait_ge(filled, START + FILLS)
                with pool.Fori(0, B) as b:

                    def power(g):
                        pool.wait_ge(var_ready, START + GROUPS * b + g + 1)
                        nc.gpsimd.tensor_tensor(rstd[:, :], var[:, :], half[:, :], ALU.pow).then_inc(rstd_ready, 1)

                    power(0)
                    for g in range(GROUPS):
                        if g + 1 < GROUPS:
                            power(g + 1)
                        pool.wait_ge(parts_ready, START + GROUPS * b + g + 1)
                        pool.sem_inc(core.taken, 1)
                        for slot in range(6):
                            ins = lay_out(nc.gpsimd, 1, slot, K_PART[slot], (part0[g % 2], part1, part2), slice(GT * g, GT * g + GT))
                        ins.then_inc(k_slots_ready, 1)
                    pool.wait_ge(k_part_ready, START + b + 1)
                    pool.sem_inc(core.taken, 1)
                    nc.gpsimd.partition_all_reduce(k_most[:, :], k_part[:, :], P, bass.bass_isa.ReduceOp.max).then_inc(k_most_ready, 1)
                    core.widest_bound(pool, b)

            @block.vector
            def _(dve):
                dve.wait_ge(consts, START + 16 * 3)
                dve.wait_ge(filled, START + FILLS)
                nc.vector.tensor_copy(ident_b[:, :], ident[:, :]).then_inc(ident_b_ready, 1)
                steps = Steps(dve, chain, CH)
                with dve.Fori(0, B) as b:
                    dve.wait_ge(loaded, START + 16 * b + 16)

                    def normalise(g):
                        n = GROUPS * b + g
                        steps.start(n)
                        centred_and_variance(nc, steps, x[:, GT * g:GT * g + GT, :], xs[g % 2][:, :, :], sq[:, :, :], mean[:, :],
                                             var[:, :], LN_EPS, var_ready)
                        dve.wait_ge(rstd_ready, START + n + 1)
                        nc.vector.tensor_tensor(xs[g % 2][:, :, :], xs[g % 2][:, :, :], bcast(rstd[:, :], C), ALU.mult).then_inc(xn_ready, 1)

                    normalise(0)
                    for g in range(GROUPS):
                        if g + 1 < GROUPS:
                            normalise(g + 1)
                        n = GROUPS * b + g
                        tiles = slice(GT * g, GT * g + GT)
                        parts = (part0[g % 2], part1, part2)
                        dve.wait_ge(part0_ready, START + n + 1)
                        dve.wait_ge(qk_ready, START + n + 1)
                        nc.vector.tensor_tensor(rest[:, :, :], qk[g % 2][:, :, :], parts[0][:, :, :], ALU.subtract).then_inc(rest_ready, 1)
                        dve.wait_ge(rest_ready, START + n + 1)
                        dve.wait_ge(k_slots_ready, START + n)
                        nc.vector.tensor_copy(parts[1][:, :, :], rest[:, :, :]).then_inc(part1_ready, 1)
                        dve.wait_ge(part1_ready, START + n + 1)
                        nc.vector.tensor_tensor(parts[2][:, :, :], rest[:, :, :], parts[1][:, :, :], ALU.subtract).then_inc(parts_ready, 1)
                        dve.wait_ge(parts_ready, START + n + 1)
                        for slot in range(6):
                            lay_out(nc.vector, 0, slot, Q_PART[slot], parts, tiles)
                        dve.wait_ge(squares_ready, START + n + 1)
                        nc.vector.reduce_sum(norm2[:, tiles, :], squares[g % 2][:, :, :].rearrange("p t (h d) -> p t h d", d=D), AX.X).then_inc(slots_ready, 1)
                    dve.wait_ge(slots_ready, START + GROUPS * (b + 1))
                    nc.vector.reduce_max(k_part[:, :], norm2[:, :, H:2 * H].rearrange("p t h -> p h t"), AX.X).then_inc(k_part_ready, 1)
                    copy_turned(nc.vector, nc.vector.tensor_copy, b, (1, 3))
                    dve.wait_ge(k_most_ready, START + b + 1)
                    nc.vector.tensor_tensor(bound[:, :, :], norm2[:, :, 0:H], k_most[:, :].unsqueeze(1).to_broadcast([P, TILES, H]),
                                            ALU.mult).then_inc(product_ready, 1)
                    dve.wait_ge(bound_ready, START + b + 1)
                    core.find_flag(dve, b, bound[:, :, :], slots[0][:, :, :, 24:27])

                    def take_turned(m):
                        for g in range(GROUPS):
                            cols = slice(GT * P * g, GT * P * (g + 1))
                            dve.wait_ge(row_turn_ready, START + GROUPS * m + g + 1)
                            for h in range(4):
                                rows = slice(32 * h, 32 * h + 32)
                                nc.vector.tensor_copy(qt[1][rows, h, cols], ps_turn[0][rows, :])
                            nc.vector.tensor_copy(kt[1][:, cols], ps_turn[1]).then_inc(row_turned_out, 1)

                    flag = core.read_flag(dve)
                    with dve.If(flag > 0):
                        with dve.Fori(0, HG) as hg:
                            m = b * HG + hg
                            take_turned(m)
                            dve.sem_inc(core.taken_dve, 1)
                            with dve.Fori(0, TILES) as t:
                                for h in range(4):
                                    core.vector_row_max(dve, (m * TILES + t) * 4 + h, SEQ,
                                                        lambda n: slots[0][:, bass.ds(t, 1), bass.ds(hg * 4 + h, 1), 24 + n:25 + n]
                                                        .rearrange("p a b c -> p (a b c)"))
                    with dve.Else():
                        nc.vector.tensor_scalar(slots[0][:, :, :, 24], bound[:, :, :], -1.0, None, ALU.mult)
                        dve.sem_inc(row_turned_out, GROUPS * HG)
                        dve.sem_inc(core.row_read, TILES * H)
                        dve.sem_inc(core.row_step, 7 * TILES * H)
                    nc.vector.memset(rstd_spare[:, :], 0.0).then_inc(shift_ready, 1)
                    copy_turned(nc.vector, nc.vector.tensor_copy, b, (5, 7, 9))

                    def block(hg, qb, width):
                        nb = (b * HG + hg) * BLOCKS + qb
                        if hg + 1 < HG:
                            side = 2 * ((b * (HG - 1) + hg) * BLOCKS + qb)
                            cols = bass.ds(qb * QW, width)
                            dve.wait_ge(side_ready, START + side + 1)
                            for h in range(4):
                                rows = slice(32 * h, 32 * h + 32)
                                ins = nc.vector.tensor_copy(qt[(hg + 1) % 2][rows, h, cols], core.turned[rows, 0:width])
                            ins.then_inc(side_out, 1)
                            dve.wait_ge(side_ready, START + side + 2)
                            nc.vector.tensor_copy(kt[(hg + 1) % 2][:, cols], core.turned[:, 0:width]).then_inc(side_out, 1)
                        core.vector(dve, nb, TILES * nb + TILES, width,
                                    lambda t: o[:, bass.ds(qb * 4 + t, 1), hg * 16:hg * 16 + 16].rearrange("p t (h d) -> p (t h) d", d=D))

                    for hg in range(HG):
                        with dve.Fori(0, QBLOCKS) as qb:
                            block(hg, qb, QW)
                        block(hg, QBLOCKS, P)
                    for g in range(GROUPS):
                        n = GROUPS * b + g
                        dve.wait_ge(y_ps_ready, START + n + 1)
                        dve.wait_ge(stored, START + 16 * n)
                        nc.vector.tensor_tensor(y[:, :, :], ps_y, x[:, GT * g:GT * g + GT, :], ALU.add).then_inc(y_ready, 1)

            @block.tensor
            def _(pe):
                pe.wait_ge(consts, START + 16 * 3)
                pe.wait_ge(filled, START + FILLS)
                pe.wait_ge(ident_b_ready, START + 1)
                nc.tensor.matmul(core.acc[:, :], kt[0][:, 0:P], kt[0][:, 0:512], start=True, stop=True).then_inc(zeroed_acc, 1)
                with pe.Fori(0, B) as b:
                    for g in range(GROUPS):
                        n = GROUPS * b + g
                        pe.wait_ge(xn_ready, START + n + 1)
                        pe.sem_inc(core.taken, 1)
                        for t in range(GT):
                            ins = nc.tensor.transpose(ps_t[0:C, t * P:(t + 1) * P], xs[g % 2][:, t, :], ident[:, :])
                        ins.then_inc(xt_ready, 1)
                        pe.wait_ge(ht_ready, START + n + 1)
                        pe.wait_ge(v_ready, START + n)
                        for t in range(GT):
                            ins = nc.tensor.matmul(ps_qkv[:, t, 0:3 * C], ht[:, t * P:(t + 1) * P], wqkv[:, :], start=True, stop=True)
                        ins.then_inc(qkv_ready, 1)

                    def turn_unit(n):
                        w, g = (1, n) if n < GROUPS else (0, n - GROUPS)
                        pe.wait_ge((turned_out_act, turned_out_dve)[n % 2], START + GROUPS * b + n // 2)
                        for t in range(GT):
                            part = slots[w][:, GT * g + t, 0:4, :].rearrange("p h s -> p (h s)")
                            ins = nc.tensor.matmul(ps_turn[n % 2][:, t * P:(t + 1) * P], part, ident_b[:, :], start=True, stop=True)
                        ins.then_inc(turn_ready, 1)

                    def turn_for_maxima(m, hg):
                        for g in range(GROUPS):
                            pe.wait_ge(row_turned_out, START + GROUPS * m + g)
                            for w in range(2):
                                for t in range(GT):
                                    part = slots[w][:, GT * g + t, bass.ds(hg * 4, 4), :].rearrange("p h s -> p (h s)")
                                    ins = nc.tensor.matmul(ps_turn[w][:, t * P:(t + 1) * P], part, ident_b[:, :],
                                                           start=True, stop=True)
                            ins.then_inc(row_turn_ready, 1)

                    pe.wait_ge(v_ready, START + GROUPS * (b + 1))
                    pe.wait_ge(core.exp_done, START + 2 * TILES * BLOCKS * HG * b)
                    pe.wait_ge(k_slots_ready, START + GROUPS * (b + 1))
                    for n in range(GROUPS):
                        turn_unit(n)
                    for out, units in ((turned_out_act, 3), (turned_out_dve, 2)):
                        pe.wait_ge(out, START + GROUPS * b + units)
                    pe.wait_ge(core.flag_ready, START + b + 1)
                    pe.sem_inc(core.taken, 1)
                    flag = core.read_flag(pe)
                    with pe.If(flag > 0):
                        with pe.Fori(0, HG) as hg:
                            m = b * HG + hg
                            pe.wait_ge(core.row_read, START + m * TILES * 4)
                            turn_for_maxima(m, hg)
                            pe.wait_ge(row_turned_out, START + GROUPS * (m + 1))
                            pe.sem_inc(core.taken, 1)
                            with pe.Fori(0, TILES) as t:
                                for h in range(4):
                                    core.tensor_row_scores(pe, (m * TILES + t) * 4 + h, qt[1][:, h, bass.ds(t * P, P)],
                                                           lambda k0, k1: kt[1][:, k0:k1], SEQ)
                    with pe.Else():
                        pe.sem_inc(row_turn_ready, GROUPS * HG)
                        pe.sem_inc(core.row_scores, TILES * H)
                    pe.wait_ge(shift_ready, START + b + 1)
                    pe.sem_inc(core.taken, 1)
                    for n in range(GROUPS, 2 * GROUPS):
                        turn_unit(n)
                    for out in (turned_out_act, turned_out_dve):
                        pe.wait_ge(out, START + GROUPS * (b + 1))
                    pe.sem_inc(core.taken, 1)

                    def work_of(hg, qb, width):
                        u = hg % 2
                        return Work(ALL, width, lambda t, h: kt[u][:, t * P:t * P + core.keys(t)],
                                    lambda h, _: qt[u][:, h, bass.ds(qb * QW, width)],
                                    lambda t, h: v[0:core.keys(t), t, 4 * hg + h, :])

                    def block(hg, qb, width, before):
                        nb = (b * HG + hg) * BLOCKS + qb

                        def turn_next(step):
                            if step not in (6, 12, 18):
                                return
                            w = (step - 6) // 6
                            side = 2 * ((b * (HG - 1) + hg) * BLOCKS + qb)
                            pe.wait_ge(core.block_done, START + nb)
                            pe.wait_ge(side_out, START + side + w)
                            pe.sem_inc(core.taken, 1)
                            if w == 2:
                                return
                            for t in range(width // P):
                                part = slots[w][:, bass.ds(qb * 4 + t, 1), 4 * (hg + 1):4 * (hg + 2), :].rearrange("p t h s -> p (t h s)")
                                ins = nc.tensor.matmul(core.turned[:, t * P:(t + 1) * P], part, ident_b[:, :], start=True, stop=True)
                            ins.then_inc(side_ready, 1)

                        work = work_of(hg, qb, width)
                        core.tensor(pe, nb, TILES * nb, work, before, ident[:, :], turn_next if hg + 1 < HG else None)
                        return work

                    before = None
                    for hg in range(HG):
                        if hg:
                            pe.wait_ge(side_out, START + 2 * (b * (HG - 1) + hg) * BLOCKS)
                            pe.sem_inc(core.taken, 1)
                        before = block(hg, 0, QW, before)
                        with pe.Fori(0, QBLOCKS - 1) as i:
                            block(hg, i + 1, QW, before)
                        before = block(hg, QBLOCKS, P, before)
                    nb = (b + 1) * HG * BLOCKS - 1
                    core.tensor_end(pe, nb, TILES * nb, before, ident[:, :])
                    pe.wait_ge(core.exp_done, START + 2 * TILES * BLOCKS * HG * (b + 1))
                    for g in range(GROUPS):
                        n = GROUPS * b + g
                        pe.wait_ge(core.block_done, START + BLOCKS * HG * (b + 1))
                        pe.wait_ge(ot_ready, START + n)
                        pe.sem_inc(core.taken, 1)
                        for t in range(GT):
                            ins = nc.tensor.transpose(ps_t[0:C, t * P:(t + 1) * P], o[:, GT * g + t, :], ident[:, :])
                        ins.then_inc(ot_ps_ready, 1)
                        pe.wait_ge(ot_ready, START + n + 1)
                        pe.wait_ge(y_ready, START + n)
                        pe.sem_inc(core.taken, 1)
                        for t in range(GT):
                            ins = nc.tensor.matmul(ps_y[:, t, :], ot[:, t * P:(t + 1) * P], wp[:, :], start=True, stop=True)
                        ins.then_inc(y_ps_ready, 1)

            @block.scalar
            def _(act):
                act.wait_ge(consts, START + 16 * 3)
                act.wait_ge(filled, START + FILLS)
                with act.Fori(0, B) as b:
                    for g in range(GROUPS):
                        n = GROUPS * b + g
                        tiles = slice(GT * g, GT * g + GT)
                        act.wait_ge(xt_ready, START + n + 1)
                        act.wait_ge(qkv_ready, START + n)
                        nc.scalar.activation(ht[0:C, :], ps_t[0:C, :], ACT.Copy).then_inc(ht_ready, 1)
                        act.wait_ge(qkv_ready, START + n + 1)
                        act.wait_ge(slots_ready, START + n - (g > 0))
                        act.wait_ge(k_slots_ready, START + n - (g > 0))
                        nc.scalar.activation(qk[g % 2][:, :, :], ps_qkv[:, 0:GT, 0:2 * C], ACT.Copy).then_inc(qk_ready, 1)
                        nc.scalar.activation(part0[g % 2][:, :, :], ps_qkv[:, 0:GT, 0:2 * C], ACT.Copy).then_inc(part0_ready, 1)
                        nc.scalar.activation(squares[g % 2][:, :, :], ps_qkv[:, 0:GT, 0:2 * C], ACT.Square).then_inc(squares_ready, 1)
                        for t in range(GT):
                            ins = nc.scalar.activation(v[:, GT * g + t, :, 0:D], ps_qkv[:, t, 2 * C:3 * C].rearrange("p (h d) -> p h d", d=D), ACT.Copy)
                        ins.then_inc(v_ready, 1)
                    to = lambda out, in_: nc.scalar.activation(out, in_, ACT.Copy)
                    copy_turned(nc.scalar, to, b, (0, 2, 4))
                    act.wait_ge(product_ready, START + b + 1)
                    nc.scalar.activation(bound[:, :, :], bound[:, :, :], ACT.Sqrt).then_inc(bound_ready, 1)
                    copy_turned(nc.scalar, to, b, (6, 8))
                    with act.Fori(0, HG) as hg:
                        m = b * HG + hg
                        core.scalar(act, m * BLOCKS, TILES * m * BLOCKS, ALL, QW)
                        with act.Fori(0, QBLOCKS - 1) as i:
                            nb = m * BLOCKS + 1 + i
                            core.scalar(act, nb, TILES * nb, ALL, QW, ALL)
                        nb = m * BLOCKS + QBLOCKS
                        core.scalar(act, nb, TILES * nb, ALL, P, ALL)
                    for g in range(GROUPS):
                        n = GROUPS * b + g
                        act.wait_ge(ot_ps_ready, START + n + 1)
                        act.wait_ge(y_ps_ready, START + n)
                        nc.scalar.activation(ot[0:C, :], ps_t[0:C, :], ACT.Copy).then_inc(ot_ready, 1)
                        act.wait_ge(y_ready, START + n + 1)
                        act.dma_start(tile_view(dst, b)[:, GT * g:GT * g + GT, :], y[:, :, :]).then_inc(stored, 16)
                act.wait_ge(stored, START + 16 * GROUPS * B)


def causal_attention(nc, src, x2, base, w_qkv, w_out, norm_col, cos, sin, later_in, later_t_in,
                     ident_in):
    tag = "ca"
    H, HK, D = 4, 2, 16
    NH = H + HK
    BLOCKS = QBLOCKS + 1
    WD = P
    spans = [[(P * max(kt - 4 * q, 0), kt >= 4 * q) for kt in range(4 * q + 4)] for q in range(QBLOCKS)]
    spans.append([(0, kt == TILES - 1) for kt in range(TILES)])
    before = [sum(map(len, spans[:q])) for q in range(BLOCKS + 1)]
    with ExitStack() as ctx:
        sb_, ps_, sem_, begin = phase_tools(nc, ctx)
        sb = lambda name, shape, dt=F32: sb_(f"{tag}_{name}", shape, dt)
        ps = lambda name, shape: ps_(f"{tag}_{name}", shape)
        sem = lambda name: sem_(f"{tag}_{name}")
        ident = sb("ident", [P, P])
        ident_b = sb("ident_b", [P, P], BF16)
        later, later_t, diagonal = (sb(n, [P, P]) for n in ("later", "later_t", "diagonal"))
        later_b = sb("later_b", [P, P], BF16)
        wqkv, wo, ncol = sb("wqkv", [C, 2 * C]), sb("wo", [C, C]), sb("ncol", [C, 1])
        tcos, tsin = sb("tcos", [P, TILES, D]), sb("tsin", [P, TILES, D])
        x, z = sb("x", [P, TILES, C]), sb("z", [P, TILES, C])
        xs = [sb(f"xs{u}", [P, GT, C]) for u in range(2)]
        sq = sb("sq", [P, GT, C])
        mean, var, rstd, half = (sb(n, [P, GT]) for n in ("mean", "var", "rstd", "half"))
        var2, rstd2 = sb("var2", [P, GT]), sb("rstd2", [P, GT])
        ht = sb("ht", [C, GT * P])
        qk = [sb(f"qk{u}", [P, GT, NH, D]) for u in range(2)]
        turned_qk = sb("turned_qk", [P, GT, NH, D])
        parts = [sb(f"part{n}", [P, GT, NH * D], BF16) for n in range(3)]
        rest, squares = sb("rest", [P, GT, NH * D]), sb("squares", [P, GT, NH * D])
        norm2 = sb("norm2", [P, TILES, NH])
        k_part, k_most = sb("k_part", [P, HK]), sb("k_most", [P, HK])
        bound = sb("bound", [P, TILES, H])
        spare = sb("spare", [1, 1])
        slots = sb("slots", [P, TILES, NH, WD], BF16)
        qkt = sb("qkt", [P, NH, SEQP], BF16)
        v = sb("v", [P, TILES, HK, D + 1])
        o = sb("o", [P, TILES, C])
        ot = sb("ot", [C, GT * P])
        y, y_base = sb("y", [P, GT, C]), sb("y_base", [P, GT, C])
        core = Core(nc, sb, ps, sem, D)
        flat_ring = core.ring[:, :, :, :].rearrange("p a b c -> p (a b c)")
        ps_t = flat_ring[:, 0:GT * P]
        ps_qkv = flat_ring[:, 1024:1024 + GT * P].rearrange("p (t c) -> p t c", c=P)
        ps_turn = [flat_ring[:, 1024 * n:1024 * n + NH * P].rearrange("p (h c) -> p h c", c=P) for n in range(2)]
        ps_y = flat_ring[:, 2560:2560 + GT * C].rearrange("p (t c) -> p t c", c=C)
        names = ("consts", "filled", "ident_b_ready", "zeroed_acc", "loaded", "chain", "var_ready", "rstd_ready",
                 "var2_ready", "rstd2_ready", "xn_ready", "xt_ready", "ht_ready", "qkv_ready", "qk_ready", "v_ready",
                 "rotated", "part0_ready", "part1_ready", "rest_ready", "squares_ready", "parts_ready", "slots_ready",
                 "k_part_ready", "k_most_ready", "product_ready", "bound_ready", "shift_ready", "turn_ready",
                 "turned_out_act", "turned_out_dve", "rotary_chain", "k_slots_ready", "row_turn_ready", "row_turned_out", "ot_ps_ready", "ot_ready", "y_ps_ready", "y_ready", "base_ready", "stored")
        (consts, filled, ident_b_ready, zeroed_acc, loaded, chain, var_ready, rstd_ready, var2_ready, rstd2_ready,
         xn_ready, xt_ready, ht_ready, qkv_ready, qk_ready, v_ready, rotated, part0_ready, part1_ready, rest_ready,
         squares_ready, parts_ready, slots_ready, k_part_ready, k_most_ready, product_ready, bound_ready, shift_ready,
         turn_ready, turned_out_act, turned_out_dve, rotary_chain, k_slots_ready, row_turn_ready, row_turned_out, ot_ps_ready, ot_ready, y_ps_ready, y_ready, base_ready, stored) = map(sem, names)
        CH = 8
        EVEN, ODD = (TILES + 1) // 2, TILES // 2
        tile_view = lambda a, b: a[b].rearrange("(t p) c -> p t c", p=P)
        fills = [(half[:, :], -0.5), (v[:, :, :, D:D + 1], 1.0), (slots[:, :, :, :], 0.0),
                 (slots[:, :, H:NH, 6 * D:6 * D + 3], 1.0), (qkt[:, 0, 0:512], 0.0)]
        FILLS = len(fills)
        tables = ((ident[:, :], ident_in), (wqkv[:, :], w_qkv), (wo[:, :], w_out), (ncol[:, :], norm_col),
                  (later[:, :], later_in), (later_t[:, :], later_t_in), (tcos[:, :, :], cos.rearrange("(t p) d -> p t d", p=P)),
                  (tsin[:, :, :], sin.rearrange("(t p) d -> p t d", p=P)))
        CONSTS = 16 * len(tables)

        def lay_out(eng, h0, h1, slot, part, tiles):
            src_p = parts[part][:, :, h0 * D:h1 * D].rearrange("p t (h d) -> p t h d", d=D)
            return eng.tensor_copy(slots[:, tiles, h0:h1, slot * D:(slot + 1) * D], src_p)

        begin()
        with nc.Block() as block:
            @block.sync
            def _(sp):
                for d, a in tables:
                    sp.dma_start(d, a).then_inc(consts, 16)
                with sp.Fori(0, B) as b:
                    sp.wait_ge(base_ready, START + GROUPS * b)
                    sp.dma_start(x[:, :, :], tile_view(src, b)).then_inc(loaded, 16)

            @block.gpsimd
            def _(pool):
                for n, (d, value) in enumerate(fills):
                    pool.wait_ge(filled, START + n)
                    nc.gpsimd.memset(d, value).then_inc(filled, 1)
                pool.wait_ge(filled, START + FILLS)
                with pool.Fori(0, B) as b:

                    def powers(g):
                        n = GROUPS * b + g
                        pool.wait_ge(var_ready, START + n + 1)
                        nc.gpsimd.tensor_tensor(rstd[:, :], var[:, :], half[:, :], ALU.pow).then_inc(rstd_ready, 1)
                        pool.wait_ge(var2_ready, START + n + 1)
                        nc.gpsimd.tensor_tensor(rstd2[:, :], var2[:, :], half[:, :], ALU.pow).then_inc(rstd2_ready, 1)

                    powers(0)
                    for g in range(GROUPS):
                        if g + 1 < GROUPS:
                            powers(g + 1)
                        pool.wait_ge(parts_ready, START + GROUPS * b + g + 1)
                        pool.sem_inc(core.taken, 1)
                        for slot in range(6):
                            ins = lay_out(nc.gpsimd, H, NH, slot, K_PART[slot], slice(GT * g, GT * g + GT))
                        ins.then_inc(k_slots_ready, 1)
                    pool.wait_ge(k_part_ready, START + b + 1)
                    pool.sem_inc(core.taken, 1)
                    nc.gpsimd.partition_all_reduce(k_most[:, :], k_part[:, :], P, bass.bass_isa.ReduceOp.max).then_inc(k_most_ready, 1)
                    core.widest_bound(pool, b)

            @block.vector
            def _(dve):
                dve.wait_ge(consts, START + CONSTS)
                dve.wait_ge(filled, START + FILLS)
                nc.vector.tensor_copy(ident_b[:, :], ident[:, :]).then_inc(ident_b_ready, 1)
                nc.vector.tensor_copy(later_b[:, :], later_t[:, :]).then_inc(ident_b_ready, 1)
                steps, rotary = Steps(dve, chain, CH), Steps(dve, rotary_chain, 2)
                with dve.Fori(0, B) as b:
                    dve.wait_ge(loaded, START + 16 * b + 16)

                    def normalise(g):
                        n = GROUPS * b + g
                        tiles = slice(GT * g, GT * g + GT)
                        h = xs[g % 2][:, :, :]
                        steps.start(n)
                        centred_and_variance(nc, steps, x[:, tiles, :], h, sq[:, :, :], mean[:, :], var[:, :],
                                             LN_EPS, var_ready)
                        dve.wait_ge(rstd_ready, START + n + 1)
                        steps.link(nc.vector.tensor_tensor(z[:, tiles, :], h, bcast(rstd[:, :], C), ALU.mult))
                        steps.link(nc.vector.tensor_tensor(sq[:, :, :], z[:, tiles, :], z[:, tiles, :], ALU.mult))
                        steps.link(nc.vector.reduce_sum(var2[:, :], sq[:, :, :], AX.X))
                        nc.vector.tensor_scalar(var2[:, :], var2[:, :], 1.0 / C, RMS_EPS, ALU.mult, ALU.add).then_inc(var2_ready, 1)
                        dve.wait_ge(rstd2_ready, START + n + 1)
                        nc.vector.tensor_tensor(h, z[:, tiles, :], bcast(rstd2[:, :], C), ALU.mult).then_inc(xn_ready, 1)

                    normalise(0)
                    for g in range(GROUPS):
                        if g + 1 < GROUPS:
                            normalise(g + 1)
                        n = GROUPS * b + g
                        tiles = slice(GT * g, GT * g + GT)
                        rotary.start(n)
                        dve.wait_ge(qk_ready, START + n + 1)
                        t = qk[g % 2]
                        c_b = tcos[:, tiles, :].unsqueeze(2).to_broadcast([P, GT, NH, D])
                        nc.vector.tensor_tensor(turned_qk[:, :, :, 0:D // 2], t[:, :, :, D // 2:D],
                                                tsin[:, tiles, 0:D // 2].unsqueeze(2).to_broadcast([P, GT, NH, D // 2]), ALU.mult)
                        rotary.link(nc.vector.tensor_tensor(turned_qk[:, :, :, D // 2:D], t[:, :, :, 0:D // 2],
                                                            tsin[:, tiles, D // 2:D].unsqueeze(2).to_broadcast([P, GT, NH, D // 2]), ALU.mult))
                        rotary.link(nc.vector.tensor_tensor(t[:, :, :, :], t[:, :, :, :], c_b, ALU.mult))
                        flat_qk = t[:, :, :, :].rearrange("p t h d -> p t (h d)")
                        nc.vector.tensor_tensor(flat_qk, flat_qk, turned_qk[:, :, :, :].rearrange("p t h d -> p t (h d)"), ALU.add).then_inc(rotated, 1)
                        dve.wait_ge(part0_ready, START + n + 1)
                        dve.wait_ge(rotated, START + n + 1)
                        nc.vector.tensor_tensor(rest[:, :, :], flat_qk, parts[0][:, :, :], ALU.subtract).then_inc(rest_ready, 1)
                        dve.wait_ge(rest_ready, START + n + 1)
                        dve.wait_ge(k_slots_ready, START + n)
                        nc.vector.tensor_copy(parts[1][:, :, :], rest[:, :, :]).then_inc(part1_ready, 1)
                        dve.wait_ge(part1_ready, START + n + 1)
                        nc.vector.tensor_tensor(parts[2][:, :, :], rest[:, :, :], parts[1][:, :, :], ALU.subtract).then_inc(parts_ready, 1)
                        dve.wait_ge(parts_ready, START + n + 1)
                        for slot in range(6):
                            lay_out(nc.vector, 0, H, slot, Q_PART[slot], tiles)
                        dve.wait_ge(squares_ready, START + n + 1)
                        nc.vector.reduce_sum(norm2[:, tiles, :], squares[:, :, :].rearrange("p t (h d) -> p t h d", d=D), AX.X).then_inc(slots_ready, 1)
                    dve.wait_ge(slots_ready, START + GROUPS * (b + 1))
                    nc.vector.reduce_max(k_part[:, :], norm2[:, :, H:NH].rearrange("p t h -> p h t"), AX.X).then_inc(k_part_ready, 1)
                    dve.wait_ge(k_most_ready, START + b + 1)
                    for e in range(HK):
                        ins = nc.vector.tensor_scalar(bound[:, :, 2 * e:2 * e + 2], norm2[:, :, 2 * e:2 * e + 2], k_most[:, e:e + 1], None, ALU.mult)
                    ins.then_inc(product_ready, 1)
                    dve.wait_ge(bound_ready, START + b + 1)
                    core.find_flag(dve, b, bound[:, :, :], slots[:, :, 0:H, 6 * D:6 * D + 3])

                    def take_turned_for_maxima():
                        for t in range(TILES):
                            dve.wait_ge(row_turn_ready, START + TILES * b + t + 1)
                            nc.vector.tensor_copy(qkt[:, :, t * P:(t + 1) * P], ps_turn[t % 2]).then_inc(row_turned_out, 1)

                    flag = core.read_flag(dve)
                    with dve.If(flag > 0):
                        take_turned_for_maxima()
                        for t in range(TILES):
                            for h in range(H):
                                core.vector_row_max(dve, (b * TILES + t) * H + h, t * P + P if t < TILES - 1 else SEQ,
                                                    lambda n: slots[:, t, h, 6 * D + n:6 * D + n + 1], later, diagonal)
                    with dve.Else():
                        nc.vector.tensor_scalar(slots[:, :, 0:H, 6 * D], bound[:, :, :], -1.0, None, ALU.mult)
                        dve.sem_inc(row_turned_out, TILES)
                        dve.sem_inc(core.row_read, TILES * H)
                        dve.sem_inc(core.row_step, 7 * TILES * H)
                    nc.vector.memset(spare[:, :], 0.0).then_inc(shift_ready, 1)
                    for t in range(1, TILES, 2):
                        dve.wait_ge(turn_ready, START + TILES * b + t + 1)
                        nc.vector.tensor_copy(qkt[:, :, t * P:(t + 1) * P], ps_turn[1]).then_inc(turned_out_dve, 1)
                    for q in range(BLOCKS):
                        width = QW if q < QBLOCKS else P
                        units = before[BLOCKS] * b + before[q]
                        core.vector(dve, BLOCKS * b + q, units + len(spans[q]), width,
                                    lambda t: o[:, 4 * q + t, :].rearrange("p (h d) -> p h d", d=D))
                    for g in range(GROUPS):
                        n = GROUPS * b + g
                        dve.wait_ge(y_ps_ready, START + n + 1)
                        dve.wait_ge(stored, START + 32 * n)
                        nc.vector.tensor_tensor(y[:, :, :], ps_y, z[:, GT * g:GT * g + GT, :], ALU.add).then_inc(y_ready, 1)
                        dve.wait_ge(y_ready, START + n + 1)
                        nc.vector.tensor_tensor(y_base[:, :, :], y[:, :, :], x[:, GT * g:GT * g + GT, :], ALU.add).then_inc(base_ready, 1)

            @block.tensor
            def _(pe):
                pe.wait_ge(consts, START + CONSTS)
                pe.wait_ge(filled, START + FILLS)
                pe.wait_ge(ident_b_ready, START + 2)
                nc.tensor.matmul(core.acc[:, :], qkt[:, 0, 0:P], qkt[:, 0, 0:512], start=True, stop=True).then_inc(zeroed_acc, 1)
                with pe.Fori(0, B) as b:
                    for g in range(GROUPS):
                        n = GROUPS * b + g
                        pe.wait_ge(xn_ready, START + n + 1)
                        pe.sem_inc(core.taken, 1)
                        for t in range(GT):
                            ins = nc.tensor.transpose(ps_t[0:C, t * P:(t + 1) * P], xs[g % 2][:, t, :], ident[:, :])
                        ins.then_inc(xt_ready, 1)
                        pe.wait_ge(ht_ready, START + n + 1)
                        pe.wait_ge(v_ready, START + n)
                        pe.sem_inc(core.taken, 1)
                        for t in range(GT):
                            ins = nc.tensor.matmul(ps_qkv[:, t, :], ht[:, t * P:(t + 1) * P], wqkv[:, :], start=True, stop=True)
                        ins.then_inc(qkv_ready, 1)
                    def turn(ready, copied):
                        for t in range(TILES):
                            pe.wait_ge(*copied(t))
                            for h in range(NH):
                                ins = nc.tensor.matmul(ps_turn[t % 2][:, h, :], slots[:, t, h, :], ident_b[:, :], start=True, stop=True)
                            ins.then_inc(ready, 1)

                    pe.wait_ge(v_ready, START + GROUPS * (b + 1))
                    pe.wait_ge(k_slots_ready, START + GROUPS * (b + 1))
                    pe.wait_ge(core.flag_ready, START + b + 1)
                    pe.sem_inc(core.taken, 1)
                    flag = core.read_flag(pe)
                    with pe.If(flag > 0):
                        turn(row_turn_ready, lambda t: (row_turned_out, START + TILES * b + max(t - 1, 0)))
                        pe.wait_ge(row_turned_out, START + TILES * (b + 1))
                        for t in range(TILES):
                            for h in range(H):
                                core.tensor_row_scores(pe, (b * TILES + t) * H + h, qkt[:, h, t * P:(t + 1) * P],
                                                       lambda k0, k1: qkt[:, H + h // 2, k0:k1], t * P + P if t < TILES - 1 else SEQ)
                    with pe.Else():
                        pe.sem_inc(row_turn_ready, TILES)
                        pe.sem_inc(core.row_scores, TILES * H)
                    pe.wait_ge(shift_ready, START + b + 1)
                    turn(turn_ready, lambda t: (turned_out_dve, START + ODD * b + t // 2) if t % 2
                         else (turned_out_act, START + EVEN * b + t // 2))
                    pe.wait_ge(turned_out_act, START + EVEN * (b + 1))
                    pe.wait_ge(turned_out_dve, START + ODD * (b + 1))
                    pe.sem_inc(core.taken, 1)
                    work = None
                    for q in range(BLOCKS):
                        width = QW if q < QBLOCKS else P
                        last, work = work, Work(spans[q], width, lambda t, h: qkt[:, H + h // 2, t * P:t * P + core.keys(t)],
                                                lambda h, first, q=q, width=width: qkt[:, h, QW * q + first:QW * q + width],
                                                lambda t, h: v[0:core.keys(t), t, h // 2, :], ident_b, later_b[:, :])
                        nb, units = BLOCKS * b + q, before[BLOCKS] * b + before[q]
                        core.tensor(pe, nb, units, work, last, ident[:, :])
                    core.tensor_end(pe, nb, units, work, ident[:, :])
                    pe.wait_ge(core.block_done, START + BLOCKS * (b + 1))
                    for g in range(GROUPS):
                        n = GROUPS * b + g
                        pe.wait_ge(ot_ready, START + n)
                        pe.sem_inc(core.taken, 1)
                        for t in range(GT):
                            ins = nc.tensor.transpose(ps_t[0:C, t * P:(t + 1) * P], o[:, GT * g + t, :], ident[:, :])
                        ins.then_inc(ot_ps_ready, 1)
                        pe.wait_ge(ot_ready, START + n + 1)
                        pe.wait_ge(y_ready, START + n)
                        pe.sem_inc(core.taken, 1)
                        for t in range(GT):
                            ins = nc.tensor.matmul(ps_y[:, t, :], ot[:, t * P:(t + 1) * P], wo[:, :], start=True, stop=True)
                        ins.then_inc(y_ps_ready, 1)

            @block.scalar
            def _(act):
                act.wait_ge(consts, START + CONSTS)
                act.wait_ge(filled, START + FILLS)
                with act.Fori(0, B) as b:

                    def project(g):
                        n = GROUPS * b + g
                        act.wait_ge(xt_ready, START + n + 1)
                        act.wait_ge(qkv_ready, START + n)
                        nc.scalar.activation(ht[:, :], ps_t[0:C, :], ACT.Identity, scale=ncol[:, 0:1]).then_inc(ht_ready, 1)
                        act.wait_ge(qkv_ready, START + n + 1)
                        act.wait_ge(parts_ready, START + n - (g > 0))
                        nc.scalar.activation(qk[g % 2][:, :, 0:H, :].rearrange("p t h d -> p t (h d)"), ps_qkv[:, :, 0:H * D], ACT.Copy,
                                             scale=float(D) ** -0.5)
                        nc.scalar.activation(qk[g % 2][:, :, H:NH, :].rearrange("p t h d -> p t (h d)"), ps_qkv[:, :, H * D:NH * D],
                                             ACT.Copy).then_inc(qk_ready, 1)
                        for e in range(HK):
                            ins = nc.scalar.activation(v[:, GT * g:GT * g + GT, e, 0:D], ps_qkv[:, :, (NH + e) * D:(NH + e + 1) * D], ACT.Copy)
                        ins.then_inc(v_ready, 1)

                    project(0)
                    for g in range(GROUPS):
                        if g + 1 < GROUPS:
                            project(g + 1)
                        n = GROUPS * b + g
                        act.wait_ge(rotated, START + n + 1)
                        act.wait_ge(slots_ready, START + n)
                        act.wait_ge(k_slots_ready, START + n)
                        flat_qk = qk[g % 2][:, :, :, :].rearrange("p t h d -> p t (h d)")
                        nc.scalar.activation(parts[0][:, :, :], flat_qk, ACT.Copy).then_inc(part0_ready, 1)
                        nc.scalar.activation(squares[:, :, :], flat_qk, ACT.Square).then_inc(squares_ready, 1)
                    act.wait_ge(product_ready, START + b + 1)
                    nc.scalar.activation(bound[:, :, :], bound[:, :, :], ACT.Sqrt).then_inc(bound_ready, 1)
                    for t in range(0, TILES, 2):
                        act.wait_ge(turn_ready, START + TILES * b + t + 1)
                        nc.scalar.activation(qkt[:, :, t * P:(t + 1) * P], ps_turn[0], ACT.Copy).then_inc(turned_out_act, 1)
                    for q in range(BLOCKS):
                        width = QW if q < QBLOCKS else P
                        core.scalar(act, BLOCKS * b + q, before[BLOCKS] * b + before[q], spans[q], width,
                                    spans[q - 1] if q else None)
                    for g in range(GROUPS):
                        n = GROUPS * b + g
                        act.wait_ge(ot_ps_ready, START + n + 1)
                        act.wait_ge(y_ps_ready, START + n)
                        nc.scalar.activation(ot[:, :], ps_t[0:C, :], ACT.Copy).then_inc(ot_ready, 1)
                        act.wait_ge(base_ready, START + n + 1)
                        act.wait_ge(y_ready, START + n + 1)
                        act.dma_start(tile_view(x2, b)[:, GT * g:GT * g + GT, :], y[:, :, :]).then_inc(stored, 16)
                        act.dma_start(tile_view(base, b)[:, GT * g:GT * g + GT, :], y_base[:, :, :]).then_inc(stored, 16)
                act.wait_ge(stored, START + 32 * GROUPS * B)


def split_three(v, link, whole, rest, first, second, third, third_rows=None):
    link(v.tensor_copy(first, whole))
    link(v.tensor_tensor(rest, whole, first, ALU.subtract))
    link(v.tensor_copy(second, rest))
    if third_rows is not None:
        rest, second = rest[third_rows], second[third_rows]
    return v.tensor_tensor(third, rest, second, ALU.subtract)


def experts(nc, x2, base, out, w_1, w_2, w_3, selector, w_router, norm_col, rank_in, ident_in):
    tag = "moe"
    E = w_router.shape[1]
    HIDDEN = w_1.shape[1]
    CHUNKS = HIDDEN // P
    LAG = 3
    BLOCKS = QBLOCKS + 1
    with ExitStack() as ctx:
        sb_, ps_, sem_, begin = phase_tools(nc, ctx)
        sb = lambda name, shape, dt=F32: sb_(f"{tag}_{name}", shape, dt)
        ps = lambda name, shape: ps_(f"{tag}_{name}", shape)
        sem = lambda name: sem_(f"{tag}_{name}")
        ident = sb("ident", [P, P])
        ident_b = sb("ident_b", [P, P], BF16)
        w_whole = [sb(f"w_whole{n}", [P, HIDDEN]) for n in range(2)]
        w_rest = sb("w_rest", [P, HIDDEN])
        w_parts = [[sb(f"w{n}_part{m}", [P, HIDDEN], BF16) for m in range(3)] for n in range(2)]
        w2 = sb("w2", [P, CHUNKS, C])
        sel = sb("sel", [3 * E, HIDDEN])
        sel_b = sb("sel_b", [3 * E, HIDDEN], BF16)
        wr, ncol, rank = sb("wr", [C, E]), sb("ncol", [C, 1]), sb("rank", [P, E])
        half = sb("half", [P, TILES])
        x = sb("x", [P, TILES, C])
        acc = sb("acc", [P, TILES, C])
        sq = sb("sq", [P, TILES, C])
        var, rstd = sb("var", [P, TILES]), sb("rstd", [P, TILES])
        ft = sb("ft", [C, 512])
        ft_rest = sb("ft_rest", [C, 512])
        f_parts = [sb(f"f_part{m}", [P, SEQP], BF16) for m in range(2)]
        prob = sb("prob", [P, TILES, E])
        w_rest8 = sb("w_rest8", [P, TILES, E])
        weight_parts = sb("weight_parts", [P, TILES, 3 * E], BF16)
        weight_t = sb("weight_t", [3 * E, SEQP], BF16)
        most, total = sb("most", [P, TILES]), sb("total", [P, TILES])
        first, second = sb("first", [P, TILES]), sb("second", [P, TILES])
        is_first, is_second, work = (sb(n, [P, TILES, E]) for n in ("is_first", "is_second", "work"))
        gate = [sb(f"gate{n}", [P, QW]) for n in range(2)]
        product = [sb(f"product{n}", [P, QW]) for n in range(2)]
        RH = 5
        hid = [sb(f"hid{n}", [P, QW]) for n in range(RH)]
        out_t = sb("out_t", [P, QW])
        ps_a = [ps(f"ps_a{n}", [P, 512]) for n in range(2)]
        ps_b = [ps(f"ps_b{n}", [P, 512]) for n in range(2)]
        ps_w = [ps(f"ps_w{n}", [P, 512]) for n in range(2)]
        ps_o, ps_t = ps("ps_o", [P, 512]), ps("ps_t", [P, 512])
        names = ("consts", "filled", "taken", "loaded", "chain", "var_ready", "rstd_ready", "xn_ready", "xt_ready",
                 "ft_ready", "logits_ready", "less_max", "exp_ready", "wt_ready", "wt_copied", "parts_chain",
                 "weights_ready", "up_ready", "gate_ready", "product_ready", "hid_ready", "down_ready", "out_copied",
                 "out_turned", "added", "stored", "taken_dve", "parts_done", "half_added")
        (consts, filled, taken, loaded, chain, var_ready, rstd_ready, xn_ready, xt_ready, ft_ready, logits_ready,
         less_max, exp_ready, wt_ready, wt_copied, parts_chain, weights_ready, up_ready, gate_ready, product_ready,
         hid_ready, down_ready, out_copied, out_turned, added, stored, taken_dve, parts_done, half_added) = map(sem, names)
        NT = -(-TILES // 4)
        CH = 21 + 5 + 5 * NT
        tile_view = lambda a, b: a[b].rearrange("(t p) c -> p t c", p=P)
        tables = ((ident[:, :], ident_in), (w_whole[0][:, :], w_1), (w_whole[1][:, :], w_3), (w2[:, :, :], w_2),
                  (sel[:, :], selector), (wr[:, :], w_router), (ncol[:, :], norm_col), (rank[:, :], rank_in))
        CONSTS = 16 * len(tables)

        def all_blocks(eng, b, body):
            with eng.Fori(0, QBLOCKS) as q:
                body(b * BLOCKS + q, q, QW)
            body(b * BLOCKS + QBLOCKS, QBLOCKS, P)

        begin()
        with nc.Block() as block:
            @block.sync
            def _(sp):
                for d, a in tables:
                    sp.dma_start(d, a).then_inc(consts, 16)
                with sp.Fori(0, B) as b:
                    sp.wait_ge(xn_ready, START + b)
                    sp.dma_start(x[:, :, :], tile_view(x2, b)).then_inc(loaded, 16)
                    sp.wait_ge(stored, START + 32 * b)
                    sp.dma_start(acc[:, :, :], tile_view(base, b)).then_inc(loaded, 16)

            @block.gpsimd
            def _(pool):
                nc.gpsimd.memset(half[:, :], -0.5).then_inc(filled, 1)
                pool.wait_ge(filled, START + 1)
                with pool.Fori(0, B) as b:
                    pool.wait_ge(var_ready, START + b + 1)
                    nc.gpsimd.tensor_tensor(rstd[:, :], var[:, :], half[:, :], ALU.pow).then_inc(rstd_ready, 1)

            @block.vector
            def _(dve):
                dve.wait_ge(consts, START + CONSTS)
                dve.wait_ge(filled, START + 1)
                v = nc.vector
                v.tensor_copy(ident_b[:, :], ident[:, :])
                v.tensor_copy(sel_b[:, :], sel[:, :])
                prepare = Steps(dve, parts_chain, 6)
                for n in range(2):
                    prepare.start(n)
                    a, b_, c_ = (t[:, :] for t in w_parts[n])
                    last = split_three(v, prepare.link, w_whole[n][:, :], w_rest[:, :], a, b_, c_[0:C, :], slice(0, C))
                    prepare.link(last)
                    prepare.link(v.tensor_copy(c_[C:P, :], a[C:P, :]))
                    prepare.link(v.memset(work[:, 0:1, 0:1], 0.0))
                v.memset(most[:, 0:1], 0.0).then_inc(parts_done, 1)
                dve.wait_ge(parts_done, START + 1)
                steps = Steps(dve, chain, CH)
                with dve.Fori(0, B) as b:
                    steps.start(b)
                    dve.wait_ge(loaded, START + 32 * b + 32)
                    steps.link(v.tensor_tensor(sq[:, :, :], x[:, :, :], x[:, :, :], ALU.mult))
                    steps.link(v.reduce_sum(var[:, :], sq[:, :, :], AX.X))
                    v.tensor_scalar(var[:, :], var[:, :], 1.0 / C, RMS_EPS, ALU.mult, ALU.add).then_inc(var_ready, 1)
                    dve.wait_ge(rstd_ready, START + b + 1)
                    v.tensor_tensor(sq[:, :, :], x[:, :, :], bcast(rstd[:, :], C), ALU.mult).then_inc(xn_ready, 1)
                    for n in range(NT):
                        wd = min(512, SEQP - n * 512)
                        cols = slice(n * 512, n * 512 + wd)
                        dve.wait_ge(xt_ready, START + NT * b + n + 1)
                        dve.wait_ge(logits_ready, START + NT * b + n)
                        steps.link(v.tensor_scalar(ft[:, 0:wd], ps_t[0:C, 0:wd], ncol[:, 0:1], None, ALU.mult))
                        steps.link(split_three(v, steps.link, ft[:, 0:wd], ft_rest[:, 0:wd], f_parts[0][0:C, cols],
                                               f_parts[0][C:P, cols], f_parts[1][C:P, cols]))
                        v.tensor_copy(f_parts[1][0:C, cols], f_parts[0][0:C, cols]).then_inc(ft_ready, 1)
                    dve.wait_ge(logits_ready, START + NT * (b + 1))
                    logits = ps_o[:, 0:TILES * E].rearrange("p (t e) -> p t e", e=E)
                    steps.link(v.reduce_max(most[:, :], logits, AX.X))
                    v.tensor_tensor(prob[:, :, :], logits, bcast(most[:, :], E), ALU.subtract).then_inc(less_max, 1)
                    dve.wait_ge(exp_ready, START + b + 1)
                    steps.link(v.reduce_sum(total[:, :], prob[:, :, :], AX.X))
                    steps.link(v.reciprocal(total[:, :], total[:, :]))
                    steps.link(v.tensor_tensor(prob[:, :, :], prob[:, :, :], bcast(total[:, :], E), ALU.mult))
                    rank_b = rank[:, :].unsqueeze(1).to_broadcast([P, TILES, E])

                    def pick(values, top, chosen):
                        steps.link(v.reduce_max(top, values, AX.X))
                        steps.link(v.tensor_tensor(chosen, values, bcast(top, E), ALU.is_equal))
                        steps.link(v.tensor_tensor(chosen, chosen, rank_b, ALU.mult))
                        steps.link(v.reduce_max(most[:, :], chosen, AX.X))
                        steps.link(v.tensor_tensor(chosen, chosen, bcast(most[:, :], E), ALU.is_equal))
                    pick(prob[:, :, :], first[:, :], is_first[:, :, :])
                    steps.link(v.tensor_scalar(work[:, :, :], is_first[:, :, :], -2.0, None, ALU.mult))
                    steps.link(v.tensor_tensor(work[:, :, :], work[:, :, :], prob[:, :, :], ALU.add))
                    pick(work[:, :, :], second[:, :], is_second[:, :, :])
                    steps.link(v.scalar_tensor_tensor(out=total[:, :], in0=first[:, :], scalar=1e-9, in1=second[:, :],
                                                      op0=ALU.add, op1=ALU.add))
                    steps.link(v.tensor_tensor(is_first[:, :, :], is_first[:, :, :], is_second[:, :, :], ALU.add))
                    steps.link(v.reciprocal(total[:, :], total[:, :]))
                    steps.link(v.tensor_tensor(prob[:, :, :], prob[:, :, :], is_first[:, :, :], ALU.mult))
                    steps.link(v.tensor_tensor(prob[:, :, :], prob[:, :, :], bcast(total[:, :], E), ALU.mult))
                    split_three(v, steps.link, prob[:, :, :], w_rest8[:, :, :], weight_parts[:, :, 0:E],
                                weight_parts[:, :, E:2 * E], weight_parts[:, :, 2 * E:3 * E]).then_inc(weights_ready, 1)
                    for n in range(NT):
                        wd = min(512, SEQP - n * 512)
                        dve.wait_ge(wt_ready, START + NT * b + n + 1)
                        v.tensor_copy(weight_t[:, n * 512:n * 512 + wd], ps_t[0:3 * E, 0:wd]).then_inc(wt_copied, 1)
                    dve.sem_inc(taken_dve, 1)

                    def body(nb, q, width):
                        for k in range(CHUNKS):
                            n = CHUNKS * nb + k
                            dve.wait_ge(gate_ready, START + n + 1)
                            v.tensor_tensor(product[k % 2][:, 0:width], gate[k % 2][:, 0:width], ps_b[k % 2][:, 0:width],
                                            ALU.mult).then_inc(product_ready, 1)
                            dve.wait_ge(product_ready, START + n + 1)
                            dve.wait_ge(down_ready, START + CHUNKS * nb + max(k - RH + 1, 0))
                            v.tensor_tensor(hid[k % RH][:, 0:width], product[k % 2][:, 0:width], ps_w[k % 2][:, 0:width],
                                            ALU.mult).then_inc(hid_ready, 1)
                        tiles = width // P
                        target = acc[:, bass.ds(q * 4, tiles), :] if width == QW else acc[:, TILES - 1:TILES, :]
                        dve.wait_ge(out_turned, START + nb + 1)
                        halves = ps_t[:, 0:width].rearrange("p (t two c) -> p t two c", two=2, c=C)
                        v.tensor_tensor(target, target, halves[:, :, 0, :], ALU.add).then_inc(half_added, 1)
                        dve.wait_ge(half_added, START + nb + 1)
                        v.tensor_tensor(target, target, halves[:, :, 1, :], ALU.add).then_inc(added, 1)
                    all_blocks(dve, b, body)

            @block.tensor
            def _(pe):
                pe.wait_ge(consts, START + CONSTS)
                pe.wait_ge(parts_done, START + 1)
                with pe.Fori(0, B) as b:
                    pe.wait_ge(xn_ready, START + b + 1)
                    pe.wait_ge(added, START + BLOCKS * b)
                    for n in range(NT):
                        ts = range(4 * n, min(4 * n + 4, TILES))
                        pe.wait_ge(ft_ready, START + NT * b + n)
                        pe.sem_inc(taken, 1)
                        for t in ts:
                            ins = nc.tensor.transpose(ps_t[0:C, (t % 4) * P:(t % 4 + 1) * P], sq[:, t, :], ident[:, :])
                        ins.then_inc(xt_ready, 1)
                        pe.wait_ge(ft_ready, START + NT * b + n + 1)
                        pe.sem_inc(taken, 1)
                        for t in ts:
                            ins = nc.tensor.matmul(ps_o[:, t * E:(t + 1) * E], ft[:, (t % 4) * P:(t % 4 + 1) * P], wr[:, :], start=True, stop=True)
                        ins.then_inc(logits_ready, 1)
                    pe.wait_ge(weights_ready, START + b + 1)
                    for n in range(NT):
                        pe.wait_ge(wt_copied, START + NT * b + n)
                        pe.sem_inc(taken, 1)
                        for t in range(4 * n, min(4 * n + 4, TILES)):
                            ins = nc.tensor.matmul(ps_t[0:3 * E, (t % 4) * P:(t % 4 + 1) * P], weight_parts[:, t, :], ident_b[:, :],
                                                   start=True, stop=True)
                        ins.then_inc(wt_ready, 1)
                    pe.wait_ge(wt_copied, START + NT * (b + 1))
                    pe.sem_inc(taken, 1)

                    def body(nb, q, width):
                        tiles = width // P
                        at = lambda a: a[:, bass.ds(q * QW, width)] if width == QW else a[:, QBLOCKS * QW:SEQP]

                        def down(ks):
                            pe.wait_ge(hid_ready, START + CHUNKS * nb + ks[-1] + 1)
                            if ks[0] == 0:
                                pe.wait_ge(out_copied, START + nb)
                            pe.sem_inc(taken, 1)
                            for k in ks:
                                lo = C * (k % 2)
                                nc.tensor.matmul(ps_o[lo:lo + C, 0:width], w2[:, k, :], hid[k % RH][:, 0:width],
                                                 start=(k < 2), stop=(k >= CHUNKS - 2)).then_inc(down_ready, 1)
                        for k in range(CHUNKS):
                            pe.wait_ge(hid_ready, START + CHUNKS * nb + max(k - 1, 0))
                            units = slice(k * P, (k + 1) * P)
                            for n, bank in enumerate((ps_a[k % 2], ps_b[k % 2])):
                                for m in range(3):
                                    ins = nc.tensor.matmul(bank[:, 0:width], w_parts[n][m][:, units], at(f_parts[m // 2]),
                                                           start=(m == 0), stop=(m == 2))
                            nc.tensor.matmul(ps_w[k % 2][:, 0:width], sel_b[:, units], at(weight_t), start=True, stop=True).then_inc(up_ready, 1)
                            if k >= LAG and k % 2:
                                down((k - LAG, k - LAG + 1))
                        for k in range((CHUNKS - LAG + 1) // 2 * 2, CHUNKS, 2):
                            down(tuple(range(k, min(k + 2, CHUNKS))))
                        pe.wait_ge(out_copied, START + nb + 1)
                        for t in range(tiles):
                            ins = nc.tensor.transpose(ps_t[:, t * P:(t + 1) * P], out_t[:, t * P:(t + 1) * P], ident[:, :])
                        ins.then_inc(out_turned, 1)
                    all_blocks(pe, b, body)

            @block.scalar
            def _(act):
                with act.Fori(0, B) as b:
                    act.wait_ge(less_max, START + b + 1)
                    nc.scalar.activation(prob[:, :, :], prob[:, :, :], ACT.Exp).then_inc(exp_ready, 1)

                    def body(nb, q, width):
                        for k in range(CHUNKS):
                            n = CHUNKS * nb + k
                            act.wait_ge(up_ready, START + n + 1)
                            act.wait_ge(product_ready, START + CHUNKS * nb + max(k - 1, 0))
                            nc.scalar.activation(gate[k % 2][:, 0:width], ps_a[k % 2][:, 0:width], ACT.Silu).then_inc(gate_ready, 1)
                        act.wait_ge(down_ready, START + CHUNKS * (nb + 1))
                        act.wait_ge(out_turned, START + nb)
                        nc.scalar.activation(out_t[:, 0:width], ps_o[:, 0:width], ACT.Copy).then_inc(out_copied, 1)
                    all_blocks(act, b, body)
                    act.wait_ge(added, START + BLOCKS * (b + 1))
                    full = (TILES - 1) * P
                    act.dma_start(out[b][0:full, :].rearrange("(t p) c -> p t c", p=P), acc[:, 0:TILES - 1, :]).then_inc(stored, 16)
                    act.dma_start(out[b][full:SEQ, :], acc[0:LAST, TILES - 1, :]).then_inc(stored, 16)
                act.wait_ge(stored, START + 32 * B)


def program(nc, a, out):
    dram = lambda name, shape: nc.dram_tensor(name, shape, F32, kind="Internal").ap()
    tokens, tokens2 = dram("tokens", (B * TOK, C)), dram("tokens2", (B * TOK, C))
    padded = dram("padded", (B, PAD, PAD, C))
    seq0, seq1, x2, base = (dram(n, (B, SEQP, C)) for n in ("seq0", "seq1", "x2", "base"))
    image = lambda t: t.rearrange("(b r c) ch -> b r c ch", b=B, r=SIDE)
    groups = lambda t: t.rearrange("(n g p) c -> n p g c", g=4, p=112)
    S = SIDE

    patch_embed(nc, a["patches"], a["w_patch"], a["patch_norm"], tokens)
    window_attention(nc, "w0", image(tokens), 0, a["norm1_0"], a["wq_0"], a["wk_0"], a["wv_0"], a["wproj_0"],
                     a["bias_0"], None, 1, a["head_mask"], a["ident"])
    mlp(nc, "m0", groups(tokens), groups(tokens2), a["norm2_0"], a["w1_0"], a["w2_0"], a["b2_0"], a["ident"])

    t, t2 = image(tokens), image(tokens2)
    copies(nc, "spread", [[(padded[b, 0:S, 0:S, :], t2[b]) for b in range(B)],
                          [(padded[b, 0:S, S:PAD, :], padded[b, 0:S, 0:SHIFT, :]) for b in range(B)],
                          [(padded[b, S:PAD, :, :], padded[b, 0:SHIFT, :, :]) for b in range(B)]])
    window_attention(nc, "w1", padded, SHIFT, a["norm1_1"], a["wq_1"], a["wk_1"], a["wv_1"], a["wproj_1"],
                     a["bias_1"], a["mask"], 2, a["head_mask"], a["ident"])
    far, near = (slice(SHIFT, S), slice(SHIFT, S)), (slice(0, SHIFT), slice(S, PAD))
    copies(nc, "fold", [[(t[b, r[0], c[0], :], padded[b, r[1], c[1], :]) for b in range(B)
                         for r in (far, near) for c in (far, near)]])
    mlp(nc, "m1", groups(tokens), groups(tokens2), a["norm2_1"], a["w1_1"], a["w2_1"], a["b2_1"], a["ident"])

    flat = tokens2.rearrange("(b t) c -> b t c", b=B)
    copies(nc, "join", [[x for b in range(B) for x in ((seq0[b, 1:SEQ, :], flat[b]), (seq0[b, 0:1, :], a["cls"]),
                                                       (seq0[b, SEQ:SEQP, :], a["zeros"]))]])
    dense_attention(nc, seq0, seq1, a["w_qkv"], a["w_proj"], a["ident"])
    causal_attention(nc, seq1, x2, base, a["f_qkv"], a["f_out"], a["f_norm1"], a["cos"], a["sin"], a["later"],
                     a["later_t"], a["ident"])
    experts(nc, x2, base, out, a["e_w1"], a["e_w2"], a["e_w3"], a["selector"], a["router"],
            a["f_norm2"], a["rank"], a["ident"])


def host_layout(inputs):
    import numpy as np

    a = {k: np.asarray(v) for k, v in inputs.items()}
    f = np.float32
    out = {}
    x = a["x"].reshape(B, SIDE, 4, SIDE, 4).transpose(2, 4, 0, 1, 3).reshape(16, B * TOK)
    out["patches"] = np.concatenate([x, np.ones((1, B * TOK), f)])
    out["w_patch"] = np.concatenate([a["L0_tok_pe_w"].reshape(C, 16).T, a["L0_tok_pe_b"][None]])
    out["patch_norm"] = np.repeat(np.stack([a["L0_tok_pe_ng"], a["L0_tok_pe_nb"]])[None], 112, 0)
    out["ident"] = np.eye(P, dtype=f)
    out["head_mask"] = np.repeat(np.eye(SH, dtype=f), SD, 0)
    yx = np.stack(np.meshgrid(np.arange(WIN), np.arange(WIN), indexing="ij")).reshape(2, -1)
    rel = yx[:, :, None] - yx[:, None, :] + WIN - 1
    rpi = rel[0] * (2 * WIN - 1) + rel[1]
    rows = lambda w, b: np.concatenate([w.T, b[None]])
    for i in range(2):
        out[f"norm1_{i}"] = np.stack([a["L0_tok_n1g"][i], a["L0_tok_n1b"][i]], 1)
        out[f"norm2_{i}"] = np.stack([a["L0_tok_n2g"][i], a["L0_tok_n2b"][i]], 1)
        w, b = a["L0_tok_qkv_w"][i], a["L0_tok_qkv_b"][i]
        for n, name in enumerate(("wq", "wk", "wv")):
            out[f"{name}_{i}"] = rows(w[n * C:(n + 1) * C], b[n * C:(n + 1) * C])
        out[f"wproj_{i}"] = rows(a["L0_tok_proj_w"][i], a["L0_tok_proj_b"][i])
        table = a["L0_tok_rpb"][i][rpi].transpose(0, 2, 1).reshape(NW, SH * NW)
        wide = np.zeros((P, 4, SH * NW), f)
        for h in range(2):
            wide[SLOT * h:SLOT * h + NW] = table[:, None, :]
        out[f"bias_{i}"] = wide[None]
        out[f"w1_{i}"] = rows(a["L0_tok_w1"][i], a["L0_tok_b1"][i])
        out[f"w2_{i}"] = a["L0_tok_w2"][i].T.reshape(2, P, C).transpose(1, 0, 2)
        out[f"b2_{i}"] = a["L0_tok_b2"][i][None]
    region = lambda last: np.where(last & (np.arange(WIN) >= WIN - SHIFT), 1, 0)
    mask = np.zeros((2, P, 4, SH, NW), f)
    for kind in range(2):
        for pair in range(4):
            for h in range(2):
                ry, rx = region(kind == 1), region(2 * pair + h == ROWS - 1)
                reg = (ry[:, None] * 2 + rx[None, :]).reshape(-1)
                m = np.where(reg[:, None] != reg[None, :], f(-100), f(0))
                mask[kind, SLOT * h:SLOT * h + NW, pair] = m[:, None, :]
    out["mask"] = mask.reshape(2, P, 4, SH * NW)
    out["bias_1"] = np.repeat(out["bias_1"], 2, 0)
    out["w_qkv"] = np.concatenate([a["L0_attn_w_qkv"], a["L0_attn_b_qkv"][None]])
    out["w_proj"] = np.concatenate([a["L0_attn_w_proj"], a["L0_attn_b_proj"][None]])
    out["f_qkv"] = np.concatenate([a["L0_ffn_wq"], a["L0_ffn_wk"], a["L0_ffn_wv"]]).T
    out["f_out"] = a["L0_ffn_wo"].T
    out["f_norm1"] = a["L0_ffn_ln1_w"][:, None]
    out["f_norm2"] = a["L0_ffn_ln2_w"][:, None]
    E, unit = a["L0_ffn_w1"].shape[:2]
    hidden = -(-E * unit // P) * P
    wide = lambda w: np.concatenate([w, np.zeros((hidden - len(w), w.shape[1]), f)])
    for n in ("w1", "w3"):
        out[f"e_{n}"] = np.tile(wide(a[f"L0_ffn_{n}"].reshape(E * unit, C)).T, (2, 1))
    out["e_w2"] = wide(a["L0_ffn_w2"].transpose(0, 2, 1).reshape(E * unit, C)).reshape(-1, P, C).transpose(1, 0, 2)
    out["selector"] = np.tile(wide(np.repeat(np.eye(E, dtype=f), unit, 0)).T, (3, 1))
    out["router"] = a["L0_ffn_router_w"].T
    out["rank"] = np.repeat(np.arange(E, 0, -1, dtype=f)[None], P, 0)
    D = 16
    inv_freq = 1.0 / 10000.0 ** (np.arange(0, D, 2, dtype=f) / D)
    angles = np.outer(np.arange(SEQP, dtype=f), inv_freq).astype(f)
    out["cos"] = np.cos(np.concatenate([angles, angles], 1)).astype(f)
    out["sin"] = np.concatenate([-np.sin(angles), np.sin(angles)], 1).astype(f)
    out["later"] = np.triu(np.full((P, P), -1e30, f), 1)
    out["later_t"] = out["later"].T
    out["cls"] = a["cls_tok"].reshape(1, C)
    out["zeros"] = np.zeros((SEQP - SEQ, C), f)
    return {k: np.ascontiguousarray(v) for k, v in out.items()}


def kernel(**inputs):
    import concourse.bacc as _bacc
    from concourse.bass_utils import run_bass_kernel_spmd as _run

    arrays = host_layout(inputs)
    nc = _bacc.Bacc("TRN2", target_bir_lowering=False, num_devices=1)
    args = {k: nc.dram_tensor(f"in_{k}", v.shape, mybir.dt.from_np(v.dtype), kind="ExternalInput").ap()
            for k, v in arrays.items()}
    out = nc.dram_tensor("out_0_dram", (B, SEQ, C), F32, kind="ExternalOutput").ap()
    program(nc, args, out)
    r = _run(nc, [{f"in_{k}": v for k, v in arrays.items()}], core_ids=[0])
    return r.results[0]["out_0_dram"]
```

```python
from contextlib import ExitStack

import concourse.bass as bass
from concourse import mybir

F32 = mybir.dt.float32
BF16 = mybir.dt.bfloat16
U32 = mybir.dt.uint32
ALU = mybir.AluOpType
ACT = mybir.ActivationFunctionType
AX = mybir.AxisListType

B = 8
SIDE = 56
TOK = SIDE * SIDE
C = 64
WIN = 7
NW = WIN * WIN
ROWS = SIDE // WIN
SHIFT = WIN // 2
PAD = SIDE + SHIFT
SH = 8
SD = C // SH
SLOT = 64
LN_EPS = 1e-5
RMS_EPS = 1e-6

SEQ = TOK + 1
P = 128
TILES = -(-SEQ // P)
SEQP = TILES * P
LAST = SEQ - (TILES - 1) * P
GT = 5
GROUPS = TILES // GT
QW = 512
QBLOCKS = SEQP // QW


START = 1


def phase_tools(nc, ctx):
    def sb(name, shape, dt=F32):
        return ctx.enter_context(nc.sbuf_tensor(name, shape, dt))

    def ps(name, shape, dt=F32):
        return ctx.enter_context(nc.psum_tensor(name, shape, dt))

    sems = []

    def sem(name):
        sems.append(nc.alloc_semaphore(name))
        return sems[-1]

    def begin():
        for s in sems:
            nc.gpsimd.sem_inc(s, START)
        nc.all_engine_barrier()

    def clear():
        nc.clear_and_free_semaphores(sems)
        nc.all_engine_barrier()

    ctx.callback(clear)
    return sb, ps, sem, begin


class Steps:

    def __init__(self, eng, sem, per):
        self.eng, self.sem, self.per, self.at = eng, sem, per, 0

    def start(self, i):
        assert self.at in (0, self.per), (self.at, self.per)
        self.i, self.at = i, 0

    def link(self, ins):
        ins.then_inc(self.sem, 1)
        self.at += 1
        self.eng.wait_ge(self.sem, START + self.i * self.per + self.at)


def bcast(ap, n):
    shape = list(ap.shape)
    return ap.unsqueeze(len(shape)).to_broadcast(shape + [n])


def centred_and_variance(nc, steps, x, xs, sq, mean, var, eps, var_ready):
    steps.link(nc.vector.reduce_sum(mean, x, AX.X))
    steps.link(nc.vector.tensor_scalar(mean, mean, 1.0 / C, None, ALU.mult))
    steps.link(nc.vector.tensor_tensor(xs, x, bcast(mean, C), ALU.subtract))
    steps.link(nc.vector.tensor_tensor(sq, xs, xs, ALU.mult))
    steps.link(nc.vector.reduce_sum(var, sq, AX.X))
    nc.vector.tensor_scalar(var, var, 1.0 / C, eps, ALU.mult, ALU.add).then_inc(var_ready, 1)


def patch_embed(nc, patches, w_patch, norm_rows, tokens):
    TP, G = 112, 4
    NG = B * TOK // (TP * G)
    K = 17
    with ExitStack() as ctx:
        sb, ps, sem, begin = phase_tools(nc, ctx)
        w = sb("pe_w", [K, C])
        rows = sb("pe_rows", [TP, 2, C])
        px = [sb(f"pe_px{u}", [K, TP * G]) for u in range(2)]
        xs = [sb(f"pe_xs{u}", [TP, G, C]) for u in range(2)]
        sq = [sb(f"pe_sq{u}", [TP, G, C]) for u in range(2)]
        y = [sb(f"pe_y{u}", [TP, G, C]) for u in range(2)]
        mean = [sb(f"pe_mean{u}", [TP, G]) for u in range(2)]
        var = [sb(f"pe_var{u}", [TP, G]) for u in range(2)]
        rstd = [sb(f"pe_rstd{u}", [TP, G]) for u in range(2)]
        half = sb("pe_half", [TP, G])
        psx = [ps(f"pe_psx{u}", [TP, 512]) for u in range(2)]

        consts = sem("pe_consts")
        half_set = sem("pe_half_set")
        loaded = [sem(f"pe_loaded{u}") for u in range(2)]
        embedded = [sem(f"pe_embedded{u}") for u in range(2)]
        chain = [sem(f"pe_chain{u}") for u in range(2)]
        var_ready = [sem(f"pe_var_ready{u}") for u in range(2)]
        rstd_ready = [sem(f"pe_rstd_ready{u}") for u in range(2)]
        y_ready = [sem(f"pe_y_ready{u}") for u in range(2)]
        stored = [sem(f"pe_stored{u}") for u in range(2)]
        CH = 7
        out_v = tokens.rearrange("(n g p) c -> n p g c", g=G, p=TP)
        begin()
        with nc.Block() as block:
            @block.sync
            def _(sp):
                sp.dma_start(w[:, :], w_patch).then_inc(consts, 16)
                sp.dma_start(rows[:, :, :], norm_rows).then_inc(consts, 16)
                with sp.Fori(0, NG // 2) as i:
                    for u in range(2):
                        sp.wait_ge(embedded[u], START + i)
                        sp.dma_start(px[u][:, :], patches[:, bass.ts(i * 2 + u, TP * G)]).then_inc(loaded[u], 16)

            @block.tensor
            def _(pe):
                pe.wait_ge(consts, START + 32)
                with pe.Fori(0, NG // 2) as i:
                    for u in range(2):
                        pe.wait_ge(loaded[u], START + 16 * i + 16)
                        pe.wait_ge(chain[u], START + CH * i)
                        for g in range(G):
                            last = nc.tensor.matmul(psx[u][:, g * C:(g + 1) * C], px[u][:, g * TP:(g + 1) * TP],
                                                    w[:, :], start=True, stop=True)
                        last.then_inc(embedded[u], 1)

            @block.vector
            def _(dve):
                dve.wait_ge(consts, START + 32)
                steps = [Steps(dve, chain[u], CH) for u in range(2)]
                with dve.Fori(0, NG // 2) as i:
                    for u in range(2):
                        steps[u].start(i)
                        x = psx[u][:, 0:G * C].rearrange("p (g c) -> p g c", c=C)
                        dve.wait_ge(embedded[u], START + i + 1)
                        centred_and_variance(nc, steps[u], x, xs[u][:, :, :], sq[u][:, :, :], mean[u][:, :],
                                             var[u][:, :], LN_EPS, var_ready[u])
                        dve.wait_ge(rstd_ready[u], START + i + 1)
                        steps[u].link(nc.vector.tensor_tensor(xs[u][:, :, :], xs[u][:, :, :], bcast(rstd[u][:, :], C), ALU.mult))
                        g_row = rows[:, 0, :].unsqueeze(1).to_broadcast([TP, G, C])
                        b_row = rows[:, 1, :].unsqueeze(1).to_broadcast([TP, G, C])
                        steps[u].link(nc.vector.tensor_tensor(xs[u][:, :, :], xs[u][:, :, :], g_row, ALU.mult))
                        dve.wait_ge(stored[u], START + 16 * i)
                        nc.vector.tensor_tensor(y[u][:, :, :], xs[u][:, :, :], b_row, ALU.add).then_inc(y_ready[u], 1)

            @block.gpsimd
            def _(pool):
                nc.gpsimd.memset(half[:, :], -0.5).then_inc(half_set, 1)
                pool.wait_ge(half_set, START + 1)
                with pool.Fori(0, NG // 2) as i:
                    for u in range(2):
                        pool.wait_ge(var_ready[u], START + i + 1)
                        nc.gpsimd.tensor_tensor(rstd[u][:, :], var[u][:, :], half[:, :], ALU.pow).then_inc(rstd_ready[u], 1)

            @block.scalar
            def _(act):
                with act.Fori(0, NG // 2) as i:
                    for u in range(2):
                        act.wait_ge(y_ready[u], START + i + 1)
                        act.dma_start(out_v[i * 2 + u], y[u][:, :, :]).then_inc(stored[u], 16)
                for u in range(2):
                    act.wait_ge(stored[u], START + 16 * (NG // 2))


class Row:

    def __init__(self, quad, u):
        self.quad, self.u = quad, u
        self.n = quad * 4 + u
        self.ring4, self.ring2 = u % 4, u % 2
        self.round4 = quad + u // 4
        self.round2 = quad * 2 + u // 2

    def next(self, d):
        return Row(self.quad, self.u + d)


def window_attention(nc, tag, image, offset, norm_cols, w_q, w_k, w_v, w_proj, bias, mask, n_kinds, head_mask, ident_in):
    K = C + 1
    PAIRS = 4
    HJ = SH * NW
    HP = SH // 2
    VW = 2 * SD + 2
    ALL = B * ROWS
    with ExitStack() as ctx:
        sb, ps, sem_, begin = phase_tools(nc, ctx)
        sem = lambda name: sem_(f"{tag}_{name}")
        nm = lambda name: f"{tag}_{name}"
        ident = sb(nm("ident"), [P, P])
        ncol = sb(nm("ncol"), [C, 2])
        wq, wk, wv, wp = (sb(nm(n), [P, C]) for n in ("wq", "wk", "wv", "wp"))
        hm = sb(nm("hm"), [P, SH])
        tab = sb(nm("tab"), [P, n_kinds, PAIRS, HJ])
        mtab = sb(nm("mtab"), [P, n_kinds, PAIRS, HJ]) if mask is not None else None
        n_consts = 9 + (mask is not None)
        half = sb(nm("half"), [P, PAIRS])
        x = [sb(nm(f"x{u}"), [P, PAIRS, C]) for u in range(4)]
        xs = sb(nm("xs"), [P, PAIRS, C])
        sq = sb(nm("sq"), [P, PAIRS, C])
        mean, var, rstd = (sb(nm(n), [P, PAIRS]) for n in ("mean", "var", "rstd"))
        ht = sb(nm("ht"), [P, PAIRS, P])
        qs = sb(nm("qs"), [P, PAIRS, 2, SLOT])
        kx = sb(nm("kx"), [P, PAIRS, SH, NW])
        v2 = [sb(nm(f"v2_{u}"), [P, 8, HP, VW]) for u in range(2)]
        s = sb(nm("s"), [P, PAIRS, SH, NW])
        mx = sb(nm("mx"), [P, PAIRS, SH])
        pr = sb(nm("pr"), [P, PAIRS, SH, SLOT])
        pt = [sb(nm(f"pt{j}"), [P, HP, P]) for j in range(PAIRS)]
        rden = sb(nm("rden"), [P, 2, PAIRS * HP // 2, 2])
        on = sb(nm("on"), [P, PAIRS, C])
        ot = sb(nm("ot"), [P, PAIRS, P])
        y = [sb(nm(f"y{u}"), [P, PAIRS, C]) for u in range(2)]
        bank_t = ps(nm("bank_t"), [P, 512])
        banks_qv = ps(nm("banks_qv"), [P, 2, 512])
        bank_q, bank_v = banks_qv[:, 0, :], banks_qv[:, 1, :]
        bank_k = ps(nm("bank_k"), [P, 512])
        bank_s = ps(nm("bank_s"), [P, PAIRS, 512])

        consts, zeroed, tab_ready, taken = map(sem, ("consts", "zeroed", "tab_ready", "taken"))
        loaded = [sem(f"loaded{u}") for u in range(4)]
        stored = [sem(f"stored{u}") for u in range(2)]
        (norm_chain, soft_chain, div_chain, var_ready, rstd_ready, xn_ready, xt_ready, ht_ready, q_ready, k_ready,
         v_ready, qs_ready, kx_ready, v2_ready, s_ready, sub_ready, exp_ready, ptr_ready, pt_ready, weighed, on_ready,
         ot_ps_ready, ot_ready, y_ps_ready, y_ready) = map(sem, (
             "norm_chain", "soft_chain", "div_chain", "var_ready", "rstd_ready", "xn_ready", "xt_ready", "ht_ready",
             "q_ready", "k_ready", "v_ready", "qs_ready", "kx_ready", "v2_ready", "s_ready", "sub_ready", "exp_ready",
             "ptr_ready", "pt_ready", "weighed", "on_ready", "ot_ps_ready", "ot_ready", "y_ps_ready", "y_ready"))
        padded = [(w[C:P, :], 0.0) for w in (wq, wk, wv, wp)]
        FILLS = len(padded) + 17

        def window_row(b, r):
            rows = image[b, bass.ds(r * WIN + offset, WIN), offset:offset + SIDE, :]
            v = rows.rearrange("r (p two c) ch -> two p r c ch", two=2, c=WIN)
            return [(h, p, v[h, p]) for h in range(2) for p in range(PAIRS)]

        def all_steps(eng, step):
            step(Row(0, 0), 0)
            with eng.Fori(0, B - 1) as b:
                with eng.Fori(0, 2) as j:
                    for u in range(1, 5):
                        step(Row(b * 2 + j, u), j if u == 3 and n_kinds == 2 else 0)
            for u in range(1, ROWS):
                step(Row((B - 1) * 2, u), (n_kinds - 1) * (u == ROWS - 1))

        def exists(row):
            return not isinstance(row.n, int) or 0 <= row.n < ALL

        begin()
        with nc.Block() as block:
            @block.sync
            def _(sp):
                def load(b, r):
                    for h, p, view in window_row(b, r):
                        sp.dma_start(x[r % 4][SLOT * h:SLOT * h + NW, p, :], view).then_inc(loaded[r % 4], 16)

                def store(b, r):
                    sp.wait_ge(y_ready, START + b * ROWS + r + 1)
                    for h, p, view in window_row(b, r):
                        sp.dma_start(view, y[r % 2][SLOT * h:SLOT * h + NW, p, :]).then_inc(stored[r % 2], 16)

                sp.wait_ge(zeroed, START + len(padded))
                for dst, src in ((ident[:, :], ident_in), (ncol[:, :], norm_cols), (wq[0:K, :], w_q), (wk[0:K, :], w_k),
                                 (wv[0:K, :], w_v), (wp[0:K, :], w_proj), (hm[0:C, :], head_mask), (hm[C:P, :], head_mask),
                                 (tab[:, :, :, :], bias.rearrange("k p w n -> p k w n"))):
                    sp.dma_start(dst, src).then_inc(consts, 16)
                if mask is not None:
                    sp.dma_start(mtab[:, :, :, :], mask.rearrange("k p w n -> p k w n")).then_inc(consts, 16)
                sp.wait_ge(zeroed, START + len(padded) + 4)
                for r in range(4):
                    load(0, r)
                with sp.Fori(0, B - 1) as b:
                    for r in range(ROWS):
                        store(b, r)
                        load(b + (r + 4) // ROWS, (r + 4) % ROWS)
                for r in range(ROWS):
                    store(B - 1, r)
                    if r + 4 < ROWS:
                        load(B - 1, r + 4)
                for u in range(2):
                    sp.wait_ge(stored[u], START + 16 * 8 * ALL // 2)

            @block.gpsimd
            def _(pool):
                fills = (padded + [(t[:, :, :], 0.0) for t in x] + [(pr[:, :, :, :], 0.0), (half[:, :], -0.5),
                         (ht[C:P, :, :], 0.0), (ot[C:P, :, :], 0.0), (qs[:, :, :, :], 0.0),
                         (ht[C:K, :, :], 1.0), (ot[C:K, :, :], 1.0)] + [(t[:, :, :, :], 0.0) for t in v2]
                         + [(t[0:SLOT, :, :, 2 * SD:2 * SD + 1], 1.0) for t in v2])
                fills += [(t[SLOT:P, :, :, 2 * SD + 1:VW], 1.0) for t in v2]
                assert len(fills) == FILLS
                for n, (dst, value) in enumerate(fills):
                    pool.wait_ge(zeroed, START + n)
                    nc.gpsimd.memset(dst, value).then_inc(zeroed, 1)

                with pool.Fori(0, ALL) as i:
                    pool.wait_ge(var_ready, START + i + 1)
                    nc.gpsimd.tensor_tensor(rstd[:, :], var[:, :], half[:, :], ALU.pow).then_inc(rstd_ready, 1)

            @block.vector
            def _(dve):
                norm_steps, soft_steps, div_steps = Steps(dve, norm_chain, 5), Steps(dve, soft_chain, 4), Steps(dve, div_chain, 1)

                def centre(row):
                    norm_steps.start(row.n)
                    dve.wait_ge(loaded[row.ring4], START + 16 * 8 * (row.round4 + 1))
                    centred_and_variance(nc, norm_steps, x[row.ring4][:, :, :], xs[:, :, :], sq[:, :, :], mean[:, :],
                                         var[:, :], LN_EPS, var_ready)

                def scale(row):
                    dve.wait_ge(rstd_ready, START + row.n + 1)
                    nc.vector.tensor_tensor(xs[:, :, :], xs[:, :, :], bcast(rstd[:, :], C), ALU.mult).then_inc(xn_ready, 1)

                def spread_keys(row):
                    dve.wait_ge(k_ready, START + row.n + 1)
                    kp = bank_k[:, 0:PAIRS * SLOT].rearrange("c (w j) -> c w j", j=SLOT)
                    for p in range(PAIRS):
                        ins = nc.vector.tensor_tensor(kx[:, p, :, :], kp[:, p, 0:NW].unsqueeze(1).to_broadcast([P, SH, NW]),
                                                      bcast(hm[:, :], NW), ALU.mult)
                    ins.then_inc(kx_ready, 1)

                def softmax(row, kind):
                    soft_steps.start(row.n)
                    for half in range(2):
                        ps_ = slice(2 * half, 2 * half + 2)
                        dve.wait_ge(s_ready, START + 2 * row.n + half + 1)
                        t = tab[:, kind, ps_, :] if isinstance(kind, int) else tab[:, bass.ds(kind, 1), ps_, :].rearrange("p k w n -> p (k w) n")
                        soft_steps.link(nc.vector.tensor_tensor(s[:, ps_, :, :].rearrange("p w h j -> p w (h j)"),
                                                                bank_s[:, ps_, 0:HJ], t, ALU.add))
                        soft_steps.link(nc.vector.reduce_max(mx[:, ps_, :], s[:, ps_, :, :], AX.X))
                        flat = s[:, ps_, :, :].rearrange("p w h j -> p (w h) j")
                        nc.vector.tensor_tensor(flat, flat, bcast(mx[:, ps_, :].rearrange("p w h -> p (w h)"), NW),
                                                ALU.subtract).then_inc(sub_ready, 1)

                def divide(row):
                    div_steps.start(row.n)
                    dve.wait_ge(weighed, START + PAIRS * (row.n + 1))
                    o = banks_qv[:, :, 0:PAIRS * HP * VW].rearrange("p i (n h v) -> p i n h v", h=2, v=VW)
                    own = [(slice(SLOT * h, SLOT * (h + 1)), h) for h in range(2)]
                    for rows, h in own:
                        ins = nc.vector.reciprocal(rden[rows, :, :, :], o[rows, :, :, h, 2 * SD:VW])
                    div_steps.link(ins)
                    to = on[:, :, :].rearrange("p (i w) (a two d) -> p i (w a) two d", i=2, two=2, d=SD)
                    for rows, h in own:
                        for e in range(2):
                            ins = nc.vector.tensor_tensor(to[rows, :, :, e, :], o[rows, :, :, h, e * SD:(e + 1) * SD],
                                                          bcast(rden[rows, :, :, e], SD), ALU.mult)
                    ins.then_inc(on_ready, 1)

                def add_residual(row):
                    dve.wait_ge(y_ps_ready, START + row.n + 1)
                    dve.wait_ge(stored[row.ring2], START + 16 * 8 * row.round2)
                    yp = bank_t[:, 0:PAIRS * C].rearrange("p (w c) -> p w c", c=C)
                    nc.vector.tensor_tensor(y[row.ring2][:, :, :], yp, x[row.ring4][:, :, :], ALU.add).then_inc(y_ready, 1)

                def step(row, kind):
                    softmax(row, kind)
                    if row.u > 0:
                        add_residual(row.next(-1))
                    if exists(row.next(1)):
                        spread_keys(row.next(1))
                    if exists(row.next(2)):
                        centre(row.next(2))
                    divide(row)
                    if exists(row.next(2)):
                        scale(row.next(2))

                dve.wait_ge(consts, START + 16 * n_consts)
                dve.wait_ge(zeroed, START + FILLS)
                if mask is not None:
                    nc.vector.tensor_tensor(tab[:, :, :, :], tab[:, :, :, :], mtab[:, :, :, :], ALU.add).then_inc(tab_ready, 1)
                    dve.wait_ge(tab_ready, START + 1)
                centre(Row(0, 0))
                scale(Row(0, 0))
                spread_keys(Row(0, 0))
                centre(Row(0, 1))
                scale(Row(0, 1))
                all_steps(dve, step)
                add_residual(Row(0, ALL - 1))

            @block.tensor
            def _(pe):
                def settled():
                    pe.sem_inc(taken, 1)

                def transpose_input(row):
                    pe.wait_ge(xn_ready, START + row.n + 1)
                    settled()
                    for p in range(PAIRS):
                        ins = nc.tensor.transpose(bank_k[0:C, p * P:(p + 1) * P], xs[:, p, :], ident[:, :])
                    ins.then_inc(xt_ready, 1)

                def embed(row):
                    pe.wait_ge(ht_ready, START + row.n + 1)
                    pe.wait_ge(v2_ready, START + row.n)
                    settled()
                    for bank, w, h, ready in ((bank_q, wq, 0, None), (bank_k, wk, 1, None),
                                              (bank_k, wk, 0, k_ready), (bank_q, wq, 1, q_ready)):
                        ins = nc.tensor.matmul(bank[C * h:C * (h + 1), 0:PAIRS * SLOT], w[:, :],
                                               ht[:, :, SLOT * h:SLOT * (h + 1)], start=True, stop=True)
                        if ready is not None:
                            ins.then_inc(ready, 1)
                    for w in range(8):
                        for h in range(2):
                            ins = nc.tensor.matmul(bank_v[SLOT * h:SLOT * (h + 1), w * C:(w + 1) * C],
                                                   ht[:, w // 2, SLOT * (w % 2):SLOT * (w % 2) + SLOT], wv[:, :],
                                                   start=True, stop=True)
                    ins.then_inc(v_ready, 1)

                def scores(row):
                    pe.wait_ge(qs_ready, START + row.n + 1)
                    pe.wait_ge(kx_ready, START + row.n + 1)
                    pe.wait_ge(pt_ready, START + PAIRS * row.n)
                    settled()
                    for p in range(PAIRS):
                        ins = nc.tensor.matmul(bank_s[:, p, 0:HJ], qs[:, p, :, :].rearrange("c h t -> c (h t)"),
                                               kx[:, p, :, :].rearrange("c h j -> c (h j)"), start=True, stop=True)
                        if p % 2:
                            ins.then_inc(s_ready, 1)

                def weigh(row, more):
                    def turned(p):
                        pe.wait_ge(pt_ready, START + PAIRS * row.n + p + 1)
                        settled()
                        for a in range(HP):
                            col = (p % 2 * HP + a) * 2 * VW
                            ins = nc.tensor.matmul(banks_qv[:, p // 2, col:col + 2 * VW], pt[p][:, a, :],
                                                   v2[row.ring2][:, 2 * p:2 * p + 2, a, :], start=True, stop=True)
                        ins.then_inc(weighed, 1)

                    pe.wait_ge(v2_ready, START + row.n + 1)
                    if more:
                        pe.wait_ge(qs_ready, START + row.n + 2)
                        pe.wait_ge(v2_ready, START + row.n + 2)
                    settled()
                    for p in range(PAIRS):
                        if p % 2 == 0:
                            pe.wait_ge(exp_ready, START + 2 * row.n + p // 2 + 1)
                            settled()
                        for a in range(HP):
                            ins = nc.tensor.transpose(bank_s[:, p, a * P:(a + 1) * P],
                                                      pr[:, p, 2 * a:2 * a + 2, :].rearrange("p h j -> p (h j)"), ident[:, :])
                        ins.then_inc(ptr_ready, 1)
                        if p >= 1:
                            turned(p - 1)
                    turned(PAIRS - 1)

                def transpose_output(row):
                    pe.wait_ge(on_ready, START + row.n + 1)
                    pe.wait_ge(y_ready, START + row.n)
                    settled()
                    for p in range(PAIRS):
                        ins = nc.tensor.transpose(bank_t[0:C, p * P:(p + 1) * P], on[:, p, :], ident[:, :])
                    ins.then_inc(ot_ps_ready, 1)

                def project(row):
                    pe.wait_ge(ot_ready, START + row.n + 1)
                    settled()
                    for p in range(PAIRS):
                        ins = nc.tensor.matmul(bank_t[:, p * C:(p + 1) * C], ot[:, p, :], wp[:, :], start=True, stop=True)
                    ins.then_inc(y_ps_ready, 1)

                def step(row, kind):
                    more = exists(row.next(1))
                    scores(row)
                    if row.u > 0:
                        transpose_output(row.next(-1))
                    if more:
                        transpose_input(row.next(1))
                    if row.u > 0:
                        project(row.next(-1))
                    if more:
                        embed(row.next(1))
                    weigh(row, more)

                pe.wait_ge(consts, START + 16 * n_consts)
                pe.wait_ge(zeroed, START + FILLS)
                transpose_input(Row(0, 0))
                embed(Row(0, 0))
                all_steps(pe, step)
                transpose_output(Row(0, ALL - 1))
                project(Row(0, ALL - 1))

            @block.scalar
            def _(act):
                def normed(row):
                    act.wait_ge(xt_ready, START + row.n + 1)
                    act.wait_ge(v_ready, START + row.n)
                    nc.scalar.activation(ht[0:C, :, :].rearrange("c w t -> c (w t)"), bank_k[0:C, :], ACT.Identity,
                                         bias=ncol[:, 1:2], scale=ncol[:, 0:1]).then_inc(ht_ready, 1)

                def queries(row):
                    act.wait_ge(q_ready, START + row.n + 1)
                    act.wait_ge(s_ready, START + 2 * row.n)
                    for h in range(2):
                        rows = slice(C * h, C * (h + 1))
                        ins = nc.scalar.activation(qs[rows, :, h, :], bank_q[rows, 0:PAIRS * SLOT].rearrange("c (w t) -> c w t", t=SLOT),
                                                   ACT.Copy, scale=float(SD) ** -0.5)
                    ins.then_inc(qs_ready, 1)

                def values(row):
                    act.wait_ge(v_ready, START + row.n + 1)
                    for e in range(2):
                        src = bank_v[SLOT * e:SLOT * (e + 1), :].rearrange("p (w a two d) -> p (w a) two d", w=8, a=HP, two=2)[:, :, e, :]
                        dst = v2[row.ring2][SLOT * e:SLOT * (e + 1), :, :, e * SD:(e + 1) * SD].rearrange("p w a d -> p (w a) d")
                        ins = nc.scalar.activation(dst, src, ACT.Copy)
                    ins.then_inc(v2_ready, 1)

                def exponentiate(row, half):
                    act.wait_ge(sub_ready, START + 2 * row.n + half + 1)
                    if half == 0:
                        act.wait_ge(weighed, START + PAIRS * row.n)
                    nc.scalar.activation(pr[:, 2 * half:2 * half + 2, :, 0:NW].rearrange("p w h j -> p (w h) j"),
                                         s[:, 2 * half:2 * half + 2, :, :].rearrange("p w h j -> p (w h) j"), ACT.Exp).then_inc(exp_ready, 1)

                def turn(row):
                    for p in range(PAIRS):
                        act.wait_ge(ptr_ready, START + PAIRS * row.n + p + 1)
                        nc.scalar.activation(pt[p][:, :, :].rearrange("p a t -> p (a t)"), bank_s[:, p, :], ACT.Copy).then_inc(pt_ready, 1)

                def outputs(row):
                    act.wait_ge(ot_ps_ready, START + row.n + 1)
                    act.wait_ge(y_ps_ready, START + row.n)
                    nc.scalar.activation(ot[0:C, :, :].rearrange("c w t -> c (w t)"), bank_t[0:C, :], ACT.Copy).then_inc(ot_ready, 1)

                def step(row, kind):
                    if row.u > 0:
                        outputs(row.next(-1))
                    if exists(row.next(1)):
                        normed(row.next(1))
                        queries(row.next(1))
                    exponentiate(row, 0)
                    if exists(row.next(1)):
                        values(row.next(1))
                    exponentiate(row, 1)
                    turn(row)

                act.wait_ge(consts, START + 16 * n_consts)
                act.wait_ge(zeroed, START + FILLS)
                normed(Row(0, 0))
                queries(Row(0, 0))
                values(Row(0, 0))
                all_steps(act, step)
                outputs(Row(0, ALL - 1))


def mlp(nc, tag, src, dst, norm_cols, w_1, w_2, b_2, ident_in):
    TP, G = 112, 4
    NG = B * TOK // (TP * G)
    K, HK = C + 1, 4 * C // P
    with ExitStack() as ctx:
        sb, ps, sem_, begin = phase_tools(nc, ctx)
        sem = lambda name: sem_(f"{tag}_{name}")
        two = lambda name: [sem(f"{name}{u}") for u in range(2)]
        nm = lambda name: f"{tag}_{name}"
        ident = sb(nm("ident"), [P, P])
        ncol = sb(nm("ncol"), [C, 2])
        w1 = sb(nm("w1"), [P, HK, P])
        w2 = sb(nm("w2"), [P, HK, C])
        b2 = sb(nm("b2"), [1, C])
        ones = sb(nm("ones"), [1, TP])
        half = sb(nm("half"), [TP, G])
        pairs = lambda name, shape: [sb(nm(f"{name}{u}"), shape) for u in range(2)]
        x = [sb(nm(f"x{u}"), [TP, G, C]) for u in range(4)]
        xs, sq, y = (pairs(n, [TP, G, C]) for n in ("xs", "sq", "y"))
        mean, var, rstd = (pairs(n, [TP, G]) for n in ("mean", "var", "rstd"))
        ht = pairs("ht", [P, G * TP])
        act_h = pairs("act_h", [P, HK, G * TP])
        ps_t = [ps(nm(f"ps_t{u}"), [P, 512]) for u in range(2)]
        ps_h = [ps(nm(f"ps_h{u}"), [P, HK, 512]) for u in range(2)]
        ps_y = [ps(nm(f"ps_y{u}"), [P, 512]) for u in range(2)]
        consts, filled, taken = sem("consts"), sem("filled"), sem("taken")
        loaded = [sem(f"loaded{u}") for u in range(4)]
        (stored, chain, var_ready, rstd_ready, xn_ready, xt_ready, ht_ready, h_ready, act_ready, y_ps_ready,
         y_ready) = map(two, ("stored", "chain", "var_ready", "rstd_ready", "xn_ready", "xt_ready", "ht_ready",
                              "h_ready", "act_ready", "y_ps_ready", "y_ready"))
        CH = 5
        FILLS = 7
        QUADS = NG // 4

        def all_pairs(eng, step):
            with eng.Fori(0, QUADS - 1) as q:
                for u in (0, 2):
                    step(Row(q, u), Row(q, u + 1))
            for u in (0, 2):
                step(Row(QUADS - 1, u), Row(QUADS - 1, u + 1))

        def exists(group):
            return not isinstance(group.n, int) or group.n < NG

        begin()
        with nc.Block() as block:
            @block.sync
            def _(sp):
                def load(group):
                    sp.dma_start(x[group.ring4][:, :, :], src[group.n]).then_inc(loaded[group.ring4], 16)

                def store(group):
                    sp.wait_ge(y_ready[group.ring2], START + group.round2 + 1)
                    sp.dma_start(dst[group.n], y[group.ring2][:, :, :]).then_inc(stored[group.ring2], 16)

                sp.wait_ge(filled, START + 1)
                for d, a in ((ident[:, :], ident_in), (ncol[:, :], norm_cols), (w1[0:K, :, :], w_1.rearrange("k (h p) -> k h p", p=P)),
                             (w2[:, :, :], w_2), (b2[:, :], b_2)):
                    sp.dma_start(d, a).then_inc(consts, 16)
                for u in range(4):
                    load(Row(0, u))
                with sp.Fori(0, QUADS - 1) as q:
                    for u in range(4):
                        store(Row(q, u))
                        load(Row(q + 1, u))
                for u in range(4):
                    store(Row(QUADS - 1, u))
                for u in range(2):
                    sp.wait_ge(stored[u], START + 16 * (NG // 2))

            @block.gpsimd
            def _(pool):
                for n, (d, value) in enumerate(((w1[C:P, :, :], 0.0), (half[:, :], -0.5), (ones[:, :], 1.0), (ht[0][C:P, :], 0.0),
                                                (ht[1][C:P, :], 0.0), (ht[0][C:K, :], 1.0), (ht[1][C:K, :], 1.0))):
                    pool.wait_ge(filled, START + n)
                    nc.gpsimd.memset(d, value).then_inc(filled, 1)
                pool.wait_ge(filled, START + FILLS)
                with pool.Fori(0, NG // 2) as i:
                    for u in range(2):
                        pool.wait_ge(var_ready[u], START + i + 1)
                        nc.gpsimd.tensor_tensor(rstd[u][:, :], var[u][:, :], half[:, :], ALU.pow).then_inc(rstd_ready[u], 1)

            @block.vector
            def _(dve):
                dve.wait_ge(consts, START + 16 * 5)
                dve.wait_ge(filled, START + FILLS)
                steps = [Steps(dve, chain[u], CH) for u in range(2)]

                def normalise(pair):
                    for group in pair:
                        u = group.ring2
                        steps[u].start(group.round2)
                        dve.wait_ge(loaded[group.ring4], START + 16 * group.round4 + 16)
                        centred_and_variance(nc, steps[u], x[group.ring4][:, :, :], xs[u][:, :, :], sq[u][:, :, :],
                                             mean[u][:, :], var[u][:, :], LN_EPS, var_ready[u])
                    for group in pair:
                        u = group.ring2
                        dve.wait_ge(rstd_ready[u], START + group.round2 + 1)
                        nc.vector.tensor_tensor(xs[u][:, :, :], xs[u][:, :, :], bcast(rstd[u][:, :], C), ALU.mult).then_inc(xn_ready[u], 1)

                def affine(group):
                    i, u = group.round2, group.ring2
                    dve.wait_ge(xt_ready[u], START + i + 1)
                    dve.wait_ge(h_ready[u], START + i)
                    nc.vector.tensor_scalar(ht[u][0:C, :], ps_t[u][0:C, 0:G * TP], ncol[:, 0:1], ncol[:, 1:2],
                                            ALU.mult, ALU.add).then_inc(ht_ready[u], 1)

                def residual(group):
                    i, u = group.round2, group.ring2
                    dve.wait_ge(y_ps_ready[u], START + i + 1)
                    dve.wait_ge(stored[u], START + 16 * i)
                    nc.vector.tensor_tensor(y[u][:, :, :], ps_y[u][0:TP, 0:G * C].rearrange("p (g c) -> p g c", c=C),
                                            x[group.ring4][:, :, :], ALU.add).then_inc(y_ready[u], 1)

                def step(*pair):
                    for group in pair:
                        affine(group)
                    if exists(pair[1].next(2)):
                        normalise([group.next(2) for group in pair])
                    for group in pair:
                        residual(group)
                normalise([Row(0, 0), Row(0, 1)])
                all_pairs(dve, step)

            @block.tensor
            def _(pe):
                pe.wait_ge(consts, START + 16 * 5)
                pe.wait_ge(filled, START + FILLS)

                def turn(group):
                    i, u = group.round2, group.ring2
                    pe.wait_ge(xn_ready[u], START + i + 1)
                    pe.sem_inc(taken, 1)
                    for g in range(G):
                        ins = nc.tensor.transpose(ps_t[u][0:C, g * TP:(g + 1) * TP], xs[u][:, g, :], ident[0:TP, 0:TP])
                    ins.then_inc(xt_ready[u], 1)

                def up(group):
                    i, u = group.round2, group.ring2
                    pe.wait_ge(ht_ready[u], START + i + 1)
                    for k in range(HK):
                        ins = nc.tensor.matmul(ps_h[u][:, k, 0:G * TP], w1[:, k, :], ht[u][:, :], start=True, stop=True)
                    ins.then_inc(h_ready[u], 1)

                def down(group):
                    i, u = group.round2, group.ring2
                    pe.wait_ge(act_ready[u], START + i + 1)
                    for g in range(G):
                        out = ps_y[u][0:TP, g * C:(g + 1) * C]
                        for k in range(HK):
                            nc.tensor.matmul(out, act_h[u][:, k, g * TP:(g + 1) * TP], w2[:, k, :], start=(k == 0), stop=False)
                        ins = nc.tensor.matmul(out, ones[:, :], b2[:, :], start=False, stop=True)
                    ins.then_inc(y_ps_ready[u], 1)

                def step(*pair):
                    for group in pair:
                        up(group)
                    for group in pair:
                        if exists(group.next(2)):
                            turn(group.next(2))
                    for group in pair:
                        down(group)
                for u in range(2):
                    turn(Row(0, u))
                all_pairs(pe, step)

            @block.scalar
            def _(act):
                act.wait_ge(consts, START + 16 * 5)
                act.wait_ge(filled, START + FILLS)
                with act.Fori(0, NG // 2) as i:
                    for u in range(2):
                        act.wait_ge(h_ready[u], START + i + 1)
                        nc.scalar.activation(act_h[u][:, :, :], ps_h[u][:, :, 0:G * TP], ACT.Gelu).then_inc(act_ready[u], 1)


def copies(nc, tag, pairs):
    with ExitStack() as ctx:
        _, _, sem, begin = phase_tools(nc, ctx)
        done = sem(f"{tag}_done")
        begin()
        with nc.Block() as block:
            @block.sync
            def _(sp):
                n = 0
                for step in pairs:
                    for to, frm in step:
                        sp.dma_start(to, frm).then_inc(done, 16)
                        n += 16
                    sp.wait_ge(done, START + n)


Q_PART = (0, 0, 1, 1, 0, 2)
K_PART = (0, 1, 0, 1, 2, 0)
POOL_SLOTS = (4, 5)
LIMIT = 43.0
RING = 3
PROBS = 5


def last_before(halves, n, ring):
    return max(m for m in range(halves) if m % ring == n)


class Work:

    def __init__(self, spans, width, kt_of, q_of, v_of, ident_b=None, later_b=None):
        self.spans, self.width, self.kt_of, self.q_of, self.v_of = spans, width, kt_of, q_of, v_of
        self.ident_b, self.later_b = ident_b, later_b


class Core:

    def __init__(self, nc, sb, ps, sem, dim):
        self.nc, self.dim = nc, dim
        self.ring = ps("ring", [P, RING, 2, 512])
        self.acc = ps("acc", [P, 512])
        self.turned = ps("turned", [P, 512])
        self.pb = [sb(f"probs{n}", [P, 2, QW]) for n in range(PROBS)]
        self.acc_sb = sb("acc_sb", [P, QW])
        self.rec = sb("rec", [P, QW // P, 4])
        self.taken, self.taken_dve = sem("taken"), sem("taken_dve")
        (self.scores_ready, self.exp_done, self.weighed, self.acc_copied, self.acc_turned, self.rec_done,
         self.block_done) = map(sem, ("scores_ready", "exp_done", "weighed", "acc_copied", "acc_turned", "rec_done",
                                      "block_done"))

        self.flag = sb("flag", [P, 1], U32)
        self.bound_part, self.bound_most = sb("bound_part", [P, 1]), sb("bound_most", [P, 1])
        self.row_max = sb("row_max", [P, 2])
        self.neg_max, self.neg_rest = sb("neg_max", [P, 1]), sb("neg_rest", [P, 1])
        (self.bound_part_ready, self.bound_most_ready, self.flag_ready, self.cleared, self.row_scores, self.row_read,
         self.row_step) = map(sem, ("bound_part_ready", "bound_most_ready", "flag_ready", "cleared",
                                         "row_scores", "row_read", "row_step"))

    def clear_shift(self, shift_slots):
        self.nc.vector.memset(shift_slots, 0.0).then_inc(self.cleared, 1)

    def find_flag(self, dve, b, bound):
        nc = self.nc
        nc.vector.reduce_max(self.bound_part[:, :], bound, AX.XY).then_inc(self.bound_part_ready, 1)
        dve.wait_ge(self.bound_most_ready, START + b + 1)
        nc.vector.tensor_scalar(self.flag[:, :], self.bound_most[:, :], LIMIT, None, ALU.is_gt).then_inc(self.flag_ready, 1)
        dve.wait_ge(self.flag_ready, START + b + 1)
        dve.wait_ge(self.cleared, START + b + 1)
        dve.sem_inc(self.taken_dve, 1)

    def read_flag(self, eng):
        return eng.value_load(self.flag[0:1, 0:1], min_val=0, max_val=1)

    def widest_bound(self, pool, b):
        pool.wait_ge(self.bound_part_ready, START + b + 1)
        pool.sem_inc(self.taken, 1)
        self.nc.gpsimd.partition_all_reduce(self.bound_most[:, :], self.bound_part[:, :], P,
                                            bass.bass_isa.ReduceOp.max).then_inc(self.bound_most_ready, 1)

    def tensor_row_scores(self, pe, count, q_tile, keys_of, n_keys):
        pe.wait_ge(self.row_read, START + count)
        pe.sem_inc(self.taken, 1)
        flat = self.ring[:, :, :, :].rearrange("p a b c -> p (a b c)")
        for k0 in range(0, n_keys, 512):
            k1 = min(k0 + 512, n_keys)
            out = flat[:, k0:k1] if k0 < 3072 else self.turned[:, 0:k1 - k0]
            ins = self.nc.tensor.matmul(out, q_tile, keys_of(k0, k1), start=True, stop=True)
        ins.then_inc(self.row_scores, 1)

    def vector_row_max(self, dve, count, n_keys, shift, later=None, diagonal=None):
        v = self.nc.vector
        STEPS = 7
        done = [0]

        def link(ins):
            ins.then_inc(self.row_step, 1)
            done[0] += 1
            dve.wait_ge(self.row_step, START + STEPS * count + done[0])

        dve.wait_ge(self.row_scores, START + count + 1)
        flat = self.ring[:, :, :, :].rearrange("p a b c -> p (a b c)")
        edge = 3072 if later is None else n_keys // P * P - (P if n_keys % P == 0 else 0)
        tail = self.turned[:, 0:n_keys - edge] if edge == 3072 else flat[:, edge:n_keys]
        if later is not None:
            link(v.tensor_tensor(diagonal[:, 0:n_keys - edge], tail, later[:, 0:n_keys - edge], ALU.add))
            tail = diagonal[:, 0:n_keys - edge]
        else:
            link(v.memset(self.neg_rest[:, :], 0.0))
        if edge:
            v.reduce_max(self.row_max[:, 0:1], flat[:, 0:edge], AX.X)
        else:
            v.reduce_max(self.row_max[:, 0:1], tail, AX.X)
        link(v.reduce_max(self.row_max[:, 1:2], tail, AX.X))
        link(v.reduce_max(self.neg_max[:, :], self.row_max[:, :], AX.X, negate=True))
        link(v.tensor_copy(shift(0), self.neg_max[:, :]))
        link(v.tensor_tensor(self.neg_rest[:, :], self.neg_max[:, :], shift(0), ALU.subtract))
        link(v.tensor_copy(shift(1), self.neg_rest[:, :]))
        link(v.tensor_tensor(self.neg_rest[:, :], self.neg_rest[:, :], shift(1), ALU.subtract))
        v.tensor_copy(shift(2), self.neg_rest[:, :]).then_inc(self.row_read, 1)

    def keys(self, kt):
        return LAST if kt == TILES - 1 else P

    def weigh(self, pe, nb, units, work, kt):
        first, diagonal = work.spans[kt]
        if kt == 0:
            pe.wait_ge(self.acc_copied, START + nb)
        pe.wait_ge(self.exp_done, START + 2 * units + 2 * kt + 2)
        pe.sem_inc(self.taken, 1)
        for h in range(4):
            probs = self.pb[(2 * kt + h // 2) % PROBS]
            ins = self.nc.tensor.matmul(self.acc[32 * h:32 * h + self.dim + 1, first:work.width], work.v_of(kt, h),
                                        probs[0:self.keys(kt), h % 2, first:work.width],
                                        start=(kt == 0), stop=(diagonal or kt == len(work.spans) - 1),
                                        skip_group_check=first > 0)
        ins.then_inc(self.weighed, 1)

    def turn_sums(self, pe, nb, work, ident):
        pe.wait_ge(self.acc_copied, START + nb + 1)
        pe.wait_ge(self.block_done, START + nb)
        for t in range(work.width // P):
            ins = self.nc.tensor.transpose(self.turned[:, t * P:(t + 1) * P], self.acc_sb[:, t * P:(t + 1) * P], ident)
        ins.then_inc(self.acc_turned, 1)

    def tensor(self, pe, nb, units, work, before, ident, aside=None):
        nc = self.nc
        for kt, (first, diagonal) in enumerate(work.spans):
            for half in range(2):
                n = 2 * kt + half
                if n >= RING:
                    pe.wait_ge(self.exp_done, START + 2 * units + n - RING + 1)
                elif before is None:
                    pe.wait_ge(self.exp_done, START + 2 * units)
                else:
                    halves = 2 * len(before.spans)
                    pe.wait_ge(self.exp_done, START + 2 * units - halves + last_before(halves, n, RING) + 1)
                for h in (2 * half, 2 * half + 1):
                    ins = nc.tensor.matmul(self.ring[0:self.keys(kt), n % RING, h % 2, first:work.width],
                                           work.kt_of(kt, h), work.q_of(h, first), start=True, stop=True)
                    if diagonal:
                        ins = nc.tensor.matmul(self.ring[0:self.keys(kt), n % RING, h % 2, first:first + P],
                                               work.ident_b[:, 0:self.keys(kt)], work.later_b, start=False, stop=True,
                                               skip_group_check=True)
                ins.then_inc(self.scores_ready, 1)
            if kt == 0 and before is not None:
                self.weigh(pe, nb - 1, units - len(before.spans), before, len(before.spans) - 1)
            if kt == 1 and before is not None:
                self.turn_sums(pe, nb - 1, before, ident)
            if kt >= 1:
                self.weigh(pe, nb, units, work, kt - 1)
            if aside is not None:
                aside(kt)

    def tensor_end(self, pe, nb, units, work, ident):
        self.weigh(pe, nb, units, work, len(work.spans) - 1)
        self.turn_sums(pe, nb, work, ident)

    def scalar(self, act, nb, units, spans, width, before=None):
        for kt, (first, diagonal) in enumerate(spans):
            for half in range(2):
                n = 2 * kt + half
                act.wait_ge(self.scores_ready, START + 2 * units + n + 1)
                if n >= PROBS:
                    act.wait_ge(self.weighed, START + units + (n - PROBS) // 2 + 1)
                elif before is None:
                    act.wait_ge(self.weighed, START + units)
                else:
                    last = last_before(2 * len(before), n, PROBS)
                    act.wait_ge(self.weighed, START + units - len(before) + last // 2 + 1)
                keys = self.keys(kt)
                self.nc.scalar.activation(self.pb[n % PROBS][0:keys, :, first:width],
                                          self.ring[0:keys, n % RING, :, first:width], ACT.Exp).then_inc(self.exp_done, 1)

    def vector(self, dve, nb, units_after, width, out):
        nc = self.nc
        tiles = width // P
        dve.wait_ge(self.weighed, START + units_after)
        dve.wait_ge(self.acc_turned, START + nb)
        nc.vector.tensor_copy(self.acc_sb[:, 0:width], self.acc[:, 0:width]).then_inc(self.acc_copied, 1)
        dve.wait_ge(self.acc_turned, START + nb + 1)
        turned = self.turned[:, 0:width].rearrange("p (t h r) -> p t h r", h=4, r=32)
        nc.vector.reciprocal(self.rec[:, 0:tiles, :], turned[:, :, :, self.dim]).then_inc(self.rec_done, 1)
        dve.wait_ge(self.rec_done, START + nb + 1)
        for t in range(tiles):
            ins = nc.vector.tensor_tensor(out(t), turned[:, t, :, 0:self.dim], bcast(self.rec[:, t, :], self.dim), ALU.mult)
        ins.then_inc(self.block_done, 1)


def dense_attention(nc, src, dst, w_qkv, w_proj, ident_in):
    tag = "da"
    H, D = 16, 4
    HG = H // 4
    K = C + 1
    BLOCKS = QBLOCKS + 1
    ALL = [(0, False)] * TILES
    with ExitStack() as ctx:
        sb_, ps_, sem_, begin = phase_tools(nc, ctx)
        sb = lambda name, shape, dt=F32: sb_(f"{tag}_{name}", shape, dt)
        ps = lambda name, shape: ps_(f"{tag}_{name}", shape)
        sem = lambda name: sem_(f"{tag}_{name}")
        ident = sb("ident", [P, P])
        ident_b = sb("ident_b", [P, P], BF16)
        wqkv, wp = sb("wqkv", [K, 3 * C]), sb("wp", [K, C])
        x, x_res = sb("x", [P, TILES, C]), sb("x_res", [P, TILES, C])
        xs = [sb(f"xs{u}", [P, GT, C]) for u in range(2)]
        sq = sb("sq", [P, GT, C])
        mean, var, rstd, half = (sb(n, [P, GT]) for n in ("mean", "var", "rstd", "half"))
        ht = sb("ht", [K, GT * P])
        part0 = [sb(f"part0_{u}", [P, GT, 2 * C], BF16) for u in range(2)]
        part1, part2 = (sb(f"part{n}", [P, GT, 2 * C], BF16) for n in (1, 2))
        rest = sb("rest", [P, GT, 2 * C])
        qk = [sb(f"qk{u}", [P, GT, 2 * C]) for u in range(2)]
        squares = [sb(f"squares{u}", [P, GT, 2 * C]) for u in range(2)]
        norm2 = sb("norm2", [P, TILES, 2 * H])
        k_part, k_most = sb("k_part", [P, H]), sb("k_most", [P, H])
        bound = sb("bound", [P, TILES, H])
        slots = [sb(f"slots_{n}", [P, TILES, H, 32], BF16) for n in ("q", "k")]
        qt = [sb(f"qt{u}", [P, 4, SEQP], BF16) for u in range(2)]
        kt = [sb(f"kt{u}", [P, SEQP], BF16) for u in range(2)]
        v = sb("v", [P, TILES, H, D + 1])
        rstd_spare = sb("rstd_spare", [1, 1])
        o = sb("o", [P, TILES, C])
        ot = [sb(f"ot{u}", [K, GT * P]) for u in range(2)]
        y = [sb(f"y{u}", [P, GT, C]) for u in range(2)]
        core = Core(nc, sb, ps, sem, D)
        flat_ring = core.ring[:, :, :, :].rearrange("p a b c -> p (a b c)")
        ps_t = flat_ring[:, 0:GT * P]
        ps_qkv = flat_ring[:, 1024:2560].rearrange("p (t c) -> p t c", c=256)
        ps_turn = [flat_ring[:, 0:GT * P], flat_ring[:, 1024:1024 + GT * P]]
        ps_ot = ps_turn
        ps_y = [flat_ring[:, c0:c0 + GT * C].rearrange("p (t c) -> p t c", c=C) for c0 in (2048, 2560)]

        (consts, filled, ident_b_ready, zeroed_acc, loaded, chain, var_ready, rstd_ready, xn_ready, xt_ready, ht_ready,
         qkv_ready, qk_ready, part0_ready, part1_ready, rest_ready, squares_ready, v_ready, parts_ready, slots_ready,
         k_part_ready, k_most_ready, product_ready, bound_ready, shift_ready, turn_ready, turned_out_act, turned_out_dve, row_turn_ready, row_turned_out,
         k_slots_ready, loaded_res, side_ready, side_out, ot_ps_ready, ot_ready, y_ps_ready, y_ready) = map(sem, (
             "consts", "filled", "ident_b_ready", "zeroed_acc", "loaded", "chain", "var_ready", "rstd_ready",
             "xn_ready", "xt_ready", "ht_ready", "qkv_ready", "qk_ready", "part0_ready", "part1_ready", "rest_ready",
             "squares_ready", "v_ready", "parts_ready", "slots_ready", "k_part_ready", "k_most_ready",
             "product_ready", "bound_ready", "shift_ready", "turn_ready", "turned_out_act", "turned_out_dve", "row_turn_ready",
             "row_turned_out", "k_slots_ready", "loaded_res", "side_ready", "side_out", "ot_ps_ready",
             "ot_ready", "y_ps_ready", "y_ready"))
        stored = [sem(f"stored{u}") for u in range(2)]
        OF_KIND = ((GROUPS + 1) // 2, GROUPS // 2)
        CH = 5
        tile_view = lambda a, b: a[b].rearrange("(t p) c -> p t c", p=P)
        fills = [(half[:, :], -0.5), (ht[C:K, :], 1.0), (ot[0][C:K, :], 1.0), (ot[1][C:K, :], 1.0), (v[:, :, :, D:D + 1], 1.0), (qt[0][:, :, :], 0.0),
                 (qt[1][:, :, :], 0.0), (kt[0][:, :], 0.0), (slots[0][:, :, :, :], 0.0), (slots[1][:, :, :, :], 0.0),
                 (slots[1][:, :, :, 24:27], 1.0)]
        FILLS = len(fills)

        def copy_turned(eng, copy, b, units):
            u, out = (0, turned_out_act) if eng is nc.scalar else (1, turned_out_dve)
            for n in units:
                w, g = (1, n) if n < GROUPS else (0, n - GROUPS)
                cols = slice(GT * P * g, GT * P * (g + 1))
                eng.wait_ge(turn_ready, START + 2 * GROUPS * b + n + 1)
                if w:
                    ins = copy(kt[0][:, cols], ps_turn[u])
                else:
                    for h in range(4):
                        rows = slice(32 * h, 32 * h + 32)
                        ins = copy(qt[0][rows, h, cols], ps_turn[u][rows, :])
                ins.then_inc(out, 1)

        def lay_out(eng, w, slot, part, parts, tiles):
            src_p = parts[part][:, :, w * C:(w + 1) * C].rearrange("p t (h d) -> p t h d", d=D)
            return eng.tensor_copy(slots[w][:, tiles, :, slot * D:(slot + 1) * D], src_p)

        begin()
        with nc.Block() as block:
            @block.sync
            def _(sp):
                for d, a in ((ident[:, :], ident_in), (wqkv[:, :], w_qkv), (wp[:, :], w_proj)):
                    sp.dma_start(d, a).then_inc(consts, 16)
                with sp.Fori(0, B) as b:
                    sp.wait_ge(xn_ready, START + GROUPS * b)
                    sp.dma_start(x[:, :, :], tile_view(src, b)).then_inc(loaded, 16)
                    sp.wait_ge(y_ready, START + GROUPS * b)
                    sp.dma_start(x_res[:, :, :], tile_view(src, b)).then_inc(loaded_res, 16)

            @block.gpsimd
            def _(pool):
                for n, (d, value) in enumerate(fills):
                    pool.wait_ge(filled, START + n)
                    nc.gpsimd.memset(d, value).then_inc(filled, 1)
                pool.wait_ge(filled, START + FILLS)
                with pool.Fori(0, B) as b:

                    def power(g):
                        pool.wait_ge(var_ready, START + GROUPS * b + g + 1)
                        nc.gpsimd.tensor_tensor(rstd[:, :], var[:, :], half[:, :], ALU.pow).then_inc(rstd_ready, 1)

                    power(0)
                    for g in range(GROUPS):
                        if g + 1 < GROUPS:
                            power(g + 1)
                        pool.wait_ge(parts_ready, START + GROUPS * b + g + 1)
                        pool.sem_inc(core.taken, 1)
                        for slot in POOL_SLOTS:
                            ins = lay_out(nc.gpsimd, 1, slot, K_PART[slot], (part0[g % 2], part1, part2), slice(GT * g, GT * g + GT))
                        ins.then_inc(k_slots_ready, 1)
                    pool.wait_ge(k_part_ready, START + b + 1)
                    pool.sem_inc(core.taken, 1)
                    nc.gpsimd.partition_all_reduce(k_most[:, :], k_part[:, :], P, bass.bass_isa.ReduceOp.max).then_inc(k_most_ready, 1)
                    core.widest_bound(pool, b)

            @block.vector
            def _(dve):
                dve.wait_ge(consts, START + 16 * 3)
                dve.wait_ge(filled, START + FILLS)
                nc.vector.tensor_copy(ident_b[:, :], ident[:, :]).then_inc(ident_b_ready, 1)
                steps = Steps(dve, chain, CH)
                with dve.Fori(0, B) as b:
                    dve.wait_ge(loaded, START + 16 * b + 16)

                    def normalise(g):
                        n = GROUPS * b + g
                        steps.start(n)
                        centred_and_variance(nc, steps, x[:, GT * g:GT * g + GT, :], xs[g % 2][:, :, :], sq[:, :, :], mean[:, :],
                                             var[:, :], LN_EPS, var_ready)
                        dve.wait_ge(rstd_ready, START + n + 1)
                        nc.vector.tensor_tensor(xs[g % 2][:, :, :], xs[g % 2][:, :, :], bcast(rstd[:, :], C), ALU.mult).then_inc(xn_ready, 1)

                    normalise(0)
                    for g in range(GROUPS):
                        if g + 1 < GROUPS:
                            normalise(g + 1)
                        n = GROUPS * b + g
                        tiles = slice(GT * g, GT * g + GT)
                        parts = (part0[g % 2], part1, part2)
                        dve.wait_ge(part0_ready, START + n + 1)
                        dve.wait_ge(qk_ready, START + n + 1)
                        nc.vector.tensor_tensor(rest[:, :, :], qk[g % 2][:, :, :], parts[0][:, :, :], ALU.subtract).then_inc(rest_ready, 1)
                        dve.wait_ge(rest_ready, START + n + 1)
                        dve.wait_ge(k_slots_ready, START + n)
                        nc.vector.tensor_copy(parts[1][:, :, :], rest[:, :, :]).then_inc(part1_ready, 1)
                        dve.wait_ge(part1_ready, START + n + 1)
                        nc.vector.tensor_tensor(parts[2][:, :, :], rest[:, :, :], parts[1][:, :, :], ALU.subtract).then_inc(parts_ready, 1)
                        dve.wait_ge(parts_ready, START + n + 1)
                        for slot in range(6):
                            lay_out(nc.vector, 0, slot, Q_PART[slot], parts, tiles)
                            if slot not in POOL_SLOTS:
                                lay_out(nc.vector, 1, slot, K_PART[slot], parts, tiles)
                        dve.wait_ge(squares_ready, START + n + 1)
                        nc.vector.reduce_sum(norm2[:, tiles, :], squares[g % 2][:, :, :].rearrange("p t (h d) -> p t h d", d=D), AX.X).then_inc(slots_ready, 1)
                    dve.wait_ge(slots_ready, START + GROUPS * (b + 1))
                    nc.vector.reduce_max(k_part[:, :], norm2[:, :, H:2 * H].rearrange("p t h -> p h t"), AX.X).then_inc(k_part_ready, 1)
                    core.clear_shift(slots[0][:, :, :, 24:27])
                    copy_turned(nc.vector, nc.vector.tensor_copy, b, (1, 3))
                    dve.wait_ge(k_most_ready, START + b + 1)
                    nc.vector.tensor_tensor(bound[:, :, :], norm2[:, :, 0:H], k_most[:, :].unsqueeze(1).to_broadcast([P, TILES, H]),
                                            ALU.mult).then_inc(product_ready, 1)
                    dve.wait_ge(bound_ready, START + b + 1)
                    core.find_flag(dve, b, bound[:, :, :])

                    def take_turned(m):
                        for g in range(GROUPS):
                            cols = slice(GT * P * g, GT * P * (g + 1))
                            dve.wait_ge(row_turn_ready, START + GROUPS * m + g + 1)
                            for h in range(4):
                                rows = slice(32 * h, 32 * h + 32)
                                nc.vector.tensor_copy(qt[1][rows, h, cols], ps_turn[0][rows, :])
                            nc.vector.tensor_copy(kt[1][:, cols], ps_turn[1]).then_inc(row_turned_out, 1)

                    flag = core.read_flag(dve)
                    with dve.If(flag > 0):
                        with dve.Fori(0, HG) as hg:
                            m = b * HG + hg
                            take_turned(m)
                            dve.sem_inc(core.taken_dve, 1)
                            with dve.Fori(0, TILES) as t:
                                for h in range(4):
                                    core.vector_row_max(dve, (m * TILES + t) * 4 + h, SEQ,
                                                        lambda n: slots[0][:, bass.ds(t, 1), bass.ds(hg * 4 + h, 1), 24 + n:25 + n]
                                                        .rearrange("p a b c -> p (a b c)"))
                    with dve.Else():
                        nc.vector.tensor_scalar(slots[0][:, :, :, 24], bound[:, :, :], -1.0, None, ALU.mult)
                        dve.sem_inc(row_turned_out, GROUPS * HG)
                        dve.sem_inc(core.row_read, TILES * H)
                        dve.sem_inc(core.row_step, 7 * TILES * H)
                    nc.vector.memset(rstd_spare[:, :], 0.0).then_inc(shift_ready, 1)
                    copy_turned(nc.vector, nc.vector.tensor_copy, b, (5, 7, 9))

                    def block(hg, qb, width):
                        nb = (b * HG + hg) * BLOCKS + qb
                        if hg + 1 < HG:
                            side = 2 * ((b * (HG - 1) + hg) * BLOCKS + qb)
                            cols = bass.ds(qb * QW, width)
                            dve.wait_ge(side_ready, START + side + 1)
                            for h in range(4):
                                rows = slice(32 * h, 32 * h + 32)
                                ins = nc.vector.tensor_copy(qt[(hg + 1) % 2][rows, h, cols], core.turned[rows, 0:width])
                            ins.then_inc(side_out, 1)
                            dve.wait_ge(side_ready, START + side + 2)
                            nc.vector.tensor_copy(kt[(hg + 1) % 2][:, cols], core.turned[:, 0:width]).then_inc(side_out, 1)
                        core.vector(dve, nb, TILES * nb + TILES, width,
                                    lambda t: o[:, bass.ds(qb * 4 + t, 1), hg * 16:hg * 16 + 16].rearrange("p t (h d) -> p (t h) d", d=D))

                    for hg in range(HG):
                        with dve.Fori(0, QBLOCKS) as qb:
                            block(hg, qb, QW)
                        block(hg, QBLOCKS, P)
                    dve.wait_ge(loaded_res, START + 16 * b + 16)
                    for g in range(GROUPS):
                        n = GROUPS * b + g
                        dve.wait_ge(y_ps_ready, START + n + 1)
                        dve.wait_ge(stored[g % 2], START + 16 * (OF_KIND[g % 2] * b + g // 2))
                        nc.vector.tensor_tensor(y[g % 2][:, :, :], ps_y[g % 2], x_res[:, GT * g:GT * g + GT, :], ALU.add).then_inc(y_ready, 1)

            @block.tensor
            def _(pe):
                pe.wait_ge(consts, START + 16 * 3)
                pe.wait_ge(filled, START + FILLS)
                pe.wait_ge(ident_b_ready, START + 1)
                nc.tensor.matmul(core.acc[:, :], kt[0][:, 0:P], kt[0][:, 0:512], start=True, stop=True).then_inc(zeroed_acc, 1)
                with pe.Fori(0, B) as b:
                    for g in range(GROUPS):
                        n = GROUPS * b + g
                        pe.wait_ge(xn_ready, START + n + 1)
                        pe.sem_inc(core.taken, 1)
                        for t in range(GT):
                            ins = nc.tensor.transpose(ps_t[0:C, t * P:(t + 1) * P], xs[g % 2][:, t, :], ident[:, :])
                        ins.then_inc(xt_ready, 1)
                        pe.wait_ge(ht_ready, START + n + 1)
                        pe.wait_ge(v_ready, START + n)
                        for t in range(GT):
                            ins = nc.tensor.matmul(ps_qkv[:, t, 0:3 * C], ht[:, t * P:(t + 1) * P], wqkv[:, :], start=True, stop=True)
                        ins.then_inc(qkv_ready, 1)

                    def turn_unit(n):
                        w, g = (1, n) if n < GROUPS else (0, n - GROUPS)
                        pe.wait_ge((turned_out_act, turned_out_dve)[n % 2], START + GROUPS * b + n // 2)
                        for t in range(GT):
                            part = slots[w][:, GT * g + t, 0:4, :].rearrange("p h s -> p (h s)")
                            ins = nc.tensor.matmul(ps_turn[n % 2][:, t * P:(t + 1) * P], part, ident_b[:, :], start=True, stop=True)
                        ins.then_inc(turn_ready, 1)

                    def turn_for_maxima(m, hg):
                        for g in range(GROUPS):
                            pe.wait_ge(row_turned_out, START + GROUPS * m + g)
                            for w in range(2):
                                for t in range(GT):
                                    part = slots[w][:, GT * g + t, bass.ds(hg * 4, 4), :].rearrange("p h s -> p (h s)")
                                    ins = nc.tensor.matmul(ps_turn[w][:, t * P:(t + 1) * P], part, ident_b[:, :],
                                                           start=True, stop=True)
                            ins.then_inc(row_turn_ready, 1)

                    pe.wait_ge(v_ready, START + GROUPS * (b + 1))
                    pe.wait_ge(core.exp_done, START + 2 * TILES * BLOCKS * HG * b)
                    pe.wait_ge(k_slots_ready, START + GROUPS * (b + 1))
                    for n in range(GROUPS):
                        turn_unit(n)
                    for out, units in ((turned_out_act, 3), (turned_out_dve, 2)):
                        pe.wait_ge(out, START + GROUPS * b + units)
                    pe.wait_ge(core.flag_ready, START + b + 1)
                    pe.sem_inc(core.taken, 1)
                    flag = core.read_flag(pe)
                    with pe.If(flag > 0):
                        with pe.Fori(0, HG) as hg:
                            m = b * HG + hg
                            pe.wait_ge(core.row_read, START + m * TILES * 4)
                            turn_for_maxima(m, hg)
                            pe.wait_ge(row_turned_out, START + GROUPS * (m + 1))
                            pe.sem_inc(core.taken, 1)
                            with pe.Fori(0, TILES) as t:
                                for h in range(4):
                                    core.tensor_row_scores(pe, (m * TILES + t) * 4 + h, qt[1][:, h, bass.ds(t * P, P)],
                                                           lambda k0, k1: kt[1][:, k0:k1], SEQ)
                    with pe.Else():
                        pe.sem_inc(row_turn_ready, GROUPS * HG)
                        pe.sem_inc(core.row_scores, TILES * H)
                    pe.wait_ge(shift_ready, START + b + 1)
                    pe.sem_inc(core.taken, 1)
                    for n in range(GROUPS, 2 * GROUPS):
                        turn_unit(n)
                    for out in (turned_out_act, turned_out_dve):
                        pe.wait_ge(out, START + GROUPS * (b + 1))
                    pe.sem_inc(core.taken, 1)

                    def work_of(hg, qb, width):
                        u = hg % 2
                        return Work(ALL, width, lambda t, h: kt[u][:, t * P:t * P + core.keys(t)],
                                    lambda h, _: qt[u][:, h, bass.ds(qb * QW, width)],
                                    lambda t, h: v[0:core.keys(t), t, 4 * hg + h, :])

                    def block(hg, qb, width, before):
                        nb = (b * HG + hg) * BLOCKS + qb

                        def turn_next(step):
                            if step not in (6, 12, 18):
                                return
                            w = (step - 6) // 6
                            side = 2 * ((b * (HG - 1) + hg) * BLOCKS + qb)
                            pe.wait_ge(core.block_done, START + nb)
                            pe.wait_ge(side_out, START + side + w)
                            pe.sem_inc(core.taken, 1)
                            if w == 2:
                                return
                            for t in range(width // P):
                                part = slots[w][:, bass.ds(qb * 4 + t, 1), 4 * (hg + 1):4 * (hg + 2), :].rearrange("p t h s -> p (t h s)")
                                ins = nc.tensor.matmul(core.turned[:, t * P:(t + 1) * P], part, ident_b[:, :], start=True, stop=True)
                            ins.then_inc(side_ready, 1)

                        work = work_of(hg, qb, width)
                        core.tensor(pe, nb, TILES * nb, work, before, ident[:, :], turn_next if hg + 1 < HG else None)
                        return work

                    before = None
                    for hg in range(HG):
                        if hg:
                            pe.wait_ge(side_out, START + 2 * (b * (HG - 1) + hg) * BLOCKS)
                            pe.sem_inc(core.taken, 1)
                        before = block(hg, 0, QW, before)
                        with pe.Fori(0, QBLOCKS - 1) as i:
                            block(hg, i + 1, QW, before)
                        before = block(hg, QBLOCKS, P, before)
                    nb = (b + 1) * HG * BLOCKS - 1
                    core.tensor_end(pe, nb, TILES * nb, before, ident[:, :])
                    pe.wait_ge(core.exp_done, START + 2 * TILES * BLOCKS * HG * (b + 1))

                    def turn_output(g):
                        pe.wait_ge(ot_ready, START + GROUPS * b + max(g - 1, 0))
                        pe.sem_inc(core.taken, 1)
                        for t in range(GT):
                            ins = nc.tensor.transpose(ps_ot[g % 2][0:C, t * P:(t + 1) * P], o[:, GT * g + t, :], ident[:, :])
                        ins.then_inc(ot_ps_ready, 1)

                    pe.wait_ge(core.block_done, START + BLOCKS * HG * (b + 1))
                    turn_output(0)
                    for g in range(GROUPS):
                        n = GROUPS * b + g
                        if g + 1 < GROUPS:
                            turn_output(g + 1)
                        pe.wait_ge(ot_ready, START + n + 1)
                        pe.wait_ge(y_ready, START + n - (g > 0))
                        pe.sem_inc(core.taken, 1)
                        for t in range(GT):
                            ins = nc.tensor.matmul(ps_y[g % 2][:, t, :], ot[g % 2][:, t * P:(t + 1) * P], wp[:, :], start=True, stop=True)
                        ins.then_inc(y_ps_ready, 1)

            @block.scalar
            def _(act):
                act.wait_ge(consts, START + 16 * 3)
                act.wait_ge(filled, START + FILLS)
                with act.Fori(0, B) as b:
                    for g in range(GROUPS):
                        n = GROUPS * b + g
                        tiles = slice(GT * g, GT * g + GT)
                        act.wait_ge(xt_ready, START + n + 1)
                        act.wait_ge(qkv_ready, START + n)
                        nc.scalar.activation(ht[0:C, :], ps_t[0:C, :], ACT.Copy).then_inc(ht_ready, 1)
                        act.wait_ge(qkv_ready, START + n + 1)
                        act.wait_ge(slots_ready, START + n - (g > 0))
                        act.wait_ge(k_slots_ready, START + n - (g > 0))
                        nc.scalar.activation(qk[g % 2][:, :, :], ps_qkv[:, 0:GT, 0:2 * C], ACT.Copy).then_inc(qk_ready, 1)
                        nc.scalar.activation(part0[g % 2][:, :, :], ps_qkv[:, 0:GT, 0:2 * C], ACT.Copy).then_inc(part0_ready, 1)
                        nc.scalar.activation(squares[g % 2][:, :, :], ps_qkv[:, 0:GT, 0:2 * C], ACT.Square).then_inc(squares_ready, 1)
                        for t in range(GT):
                            ins = nc.scalar.activation(v[:, GT * g + t, :, 0:D], ps_qkv[:, t, 2 * C:3 * C].rearrange("p (h d) -> p h d", d=D), ACT.Copy)
                        ins.then_inc(v_ready, 1)
                    to = lambda out, in_: nc.scalar.activation(out, in_, ACT.Copy)
                    copy_turned(nc.scalar, to, b, (0, 2, 4))
                    act.wait_ge(product_ready, START + b + 1)
                    nc.scalar.activation(bound[:, :, :], bound[:, :, :], ACT.Sqrt).then_inc(bound_ready, 1)
                    copy_turned(nc.scalar, to, b, (6, 8))
                    with act.Fori(0, HG) as hg:
                        m = b * HG + hg
                        core.scalar(act, m * BLOCKS, TILES * m * BLOCKS, ALL, QW)
                        with act.Fori(0, QBLOCKS - 1) as i:
                            nb = m * BLOCKS + 1 + i
                            core.scalar(act, nb, TILES * nb, ALL, QW, ALL)
                        nb = m * BLOCKS + QBLOCKS
                        core.scalar(act, nb, TILES * nb, ALL, P, ALL)

                    def copy_output(g):
                        n = GROUPS * b + g
                        act.wait_ge(ot_ps_ready, START + n + 1)
                        act.wait_ge(y_ps_ready, START + n - (g > 0))
                        nc.scalar.activation(ot[g % 2][0:C, :], ps_ot[g % 2][0:C, :], ACT.Copy).then_inc(ot_ready, 1)

                    copy_output(0)
                    for g in range(GROUPS):
                        n = GROUPS * b + g
                        if g + 1 < GROUPS:
                            copy_output(g + 1)
                        act.wait_ge(y_ready, START + n + 1)
                        act.dma_start(tile_view(dst, b)[:, GT * g:GT * g + GT, :], y[g % 2][:, :, :]).then_inc(stored[g % 2], 16)
                for u in range(2):
                    act.wait_ge(stored[u], START + 16 * OF_KIND[u] * B)


def causal_attention(nc, src, x2, base, w_qkv, w_out, norm_col, cos, sin, later_in, later_t_in,
                     ident_in):
    tag = "ca"
    H, HK, D = 4, 2, 16
    NH = H + HK
    BLOCKS = QBLOCKS + 1
    WD = P
    spans = [[(P * max(kt - 4 * q, 0), kt >= 4 * q) for kt in range(4 * q + 4)] for q in range(QBLOCKS)]
    spans.append([(0, kt == TILES - 1) for kt in range(TILES)])
    before = [sum(map(len, spans[:q])) for q in range(BLOCKS + 1)]
    with ExitStack() as ctx:
        sb_, ps_, sem_, begin = phase_tools(nc, ctx)
        sb = lambda name, shape, dt=F32: sb_(f"{tag}_{name}", shape, dt)
        ps = lambda name, shape: ps_(f"{tag}_{name}", shape)
        sem = lambda name: sem_(f"{tag}_{name}")
        ident = sb("ident", [P, P])
        ident_b = sb("ident_b", [P, P], BF16)
        later, later_t, diagonal = (sb(n, [P, P]) for n in ("later", "later_t", "diagonal"))
        later_b = sb("later_b", [P, P], BF16)
        wqkv, wo, ncol = sb("wqkv", [C, 2 * C]), sb("wo", [C, C]), sb("ncol", [C, 1])
        tcos, tsin = sb("tcos", [P, TILES, D]), sb("tsin", [P, TILES, D])
        x, x_res = sb("x", [P, TILES, C]), sb("x_res", [P, TILES, C])
        z = sb("z", [P, TILES, C])
        xs = [sb(f"xs{u}", [P, GT, C]) for u in range(2)]
        sq = sb("sq", [P, GT, C])
        mean, var, rstd, half = (sb(n, [P, GT]) for n in ("mean", "var", "rstd", "half"))
        var2, rstd2 = sb("var2", [P, GT]), sb("rstd2", [P, GT])
        ht = sb("ht", [C, GT * P])
        qk = [sb(f"qk{u}", [P, GT, NH, D]) for u in range(2)]
        turned_qk = sb("turned_qk", [P, GT, NH, D])
        parts = [sb(f"part{n}", [P, GT, NH * D], BF16) for n in range(3)]
        rest, squares = sb("rest", [P, GT, NH * D]), sb("squares", [P, GT, NH * D])
        norm2 = sb("norm2", [P, TILES, NH])
        k_part, k_most = sb("k_part", [P, HK]), sb("k_most", [P, HK])
        bound = sb("bound", [P, TILES, H])
        spare = sb("spare", [1, 1])
        slots = sb("slots", [P, TILES, NH, WD], BF16)
        qkt = sb("qkt", [P, NH, SEQP], BF16)
        v = sb("v", [P, TILES, HK, D + 1])
        o = sb("o", [P, TILES, C])
        ot = [sb(f"ot{u}", [C, GT * P]) for u in range(2)]
        y, y_base = ([sb(f"{n}{u}", [P, GT, C]) for u in range(2)] for n in ("y", "y_base"))
        core = Core(nc, sb, ps, sem, D)
        flat_ring = core.ring[:, :, :, :].rearrange("p a b c -> p (a b c)")
        ps_t = flat_ring[:, 0:GT * P]
        ps_qkv = flat_ring[:, 1024:1024 + GT * P].rearrange("p (t c) -> p t c", c=P)
        ps_turn = [flat_ring[:, 1024 * n:1024 * n + NH * P].rearrange("p (h c) -> p h c", c=P) for n in range(2)]
        ps_ot = [flat_ring[:, 1024 * n:1024 * n + GT * P] for n in range(2)]
        ps_y = [flat_ring[:, c0:c0 + GT * C].rearrange("p (t c) -> p t c", c=C) for c0 in (2048, 2560)]
        names = ("consts", "filled", "ident_b_ready", "zeroed_acc", "loaded", "chain", "var_ready", "rstd_ready",
                 "var2_ready", "rstd2_ready", "xn_ready", "xt_ready", "ht_ready", "qkv_ready", "qk_ready", "v_ready",
                 "rotated", "part0_ready", "part1_ready", "rest_ready", "squares_ready", "parts_ready", "slots_ready",
                 "k_part_ready", "k_most_ready", "product_ready", "bound_ready", "shift_ready", "turn_ready",
                 "turned_out_act", "turned_out_dve", "rotary_chain", "k_slots_ready", "loaded_res", "row_turn_ready", "row_turned_out", "ot_ps_ready", "ot_ready", "y_ps_ready", "y_ready", "base_ready")
        (consts, filled, ident_b_ready, zeroed_acc, loaded, chain, var_ready, rstd_ready, var2_ready, rstd2_ready,
         xn_ready, xt_ready, ht_ready, qkv_ready, qk_ready, v_ready, rotated, part0_ready, part1_ready, rest_ready,
         squares_ready, parts_ready, slots_ready, k_part_ready, k_most_ready, product_ready, bound_ready, shift_ready,
         turn_ready, turned_out_act, turned_out_dve, rotary_chain, k_slots_ready, loaded_res, row_turn_ready, row_turned_out, ot_ps_ready, ot_ready, y_ps_ready, y_ready, base_ready) = map(sem, names)
        stored = [sem(f"stored{u}") for u in range(2)]
        OF_KIND = ((GROUPS + 1) // 2, GROUPS // 2)
        CH = 8
        EVEN, ODD = (TILES + 1) // 2, TILES // 2
        tile_view = lambda a, b: a[b].rearrange("(t p) c -> p t c", p=P)
        fills = [(half[:, :], -0.5), (v[:, :, :, D:D + 1], 1.0), (slots[:, :, :, :], 0.0),
                 (slots[:, :, H:NH, 6 * D:6 * D + 3], 1.0), (qkt[:, 0, 0:512], 0.0)]
        FILLS = len(fills)
        tables = ((ident[:, :], ident_in), (wqkv[:, :], w_qkv), (wo[:, :], w_out), (ncol[:, :], norm_col),
                  (later[:, :], later_in), (later_t[:, :], later_t_in), (tcos[:, :, :], cos.rearrange("(t p) d -> p t d", p=P)),
                  (tsin[:, :, :], sin.rearrange("(t p) d -> p t d", p=P)))
        CONSTS = 16 * len(tables)

        def lay_out(eng, h0, h1, slot, part, tiles):
            src_p = parts[part][:, :, h0 * D:h1 * D].rearrange("p t (h d) -> p t h d", d=D)
            return eng.tensor_copy(slots[:, tiles, h0:h1, slot * D:(slot + 1) * D], src_p)

        begin()
        with nc.Block() as block:
            @block.sync
            def _(sp):
                for d, a in tables:
                    sp.dma_start(d, a).then_inc(consts, 16)
                with sp.Fori(0, B) as b:
                    sp.wait_ge(xn_ready, START + GROUPS * b)
                    sp.dma_start(x[:, :, :], tile_view(src, b)).then_inc(loaded, 16)
                    sp.wait_ge(base_ready, START + GROUPS * b)
                    sp.dma_start(x_res[:, :, :], tile_view(src, b)).then_inc(loaded_res, 16)

            @block.gpsimd
            def _(pool):
                for n, (d, value) in enumerate(fills):
                    pool.wait_ge(filled, START + n)
                    nc.gpsimd.memset(d, value).then_inc(filled, 1)
                pool.wait_ge(filled, START + FILLS)
                with pool.Fori(0, B) as b:

                    def powers(g):
                        n = GROUPS * b + g
                        pool.wait_ge(var_ready, START + n + 1)
                        nc.gpsimd.tensor_tensor(rstd[:, :], var[:, :], half[:, :], ALU.pow).then_inc(rstd_ready, 1)
                        pool.wait_ge(var2_ready, START + n + 1)
                        nc.gpsimd.tensor_tensor(rstd2[:, :], var2[:, :], half[:, :], ALU.pow).then_inc(rstd2_ready, 1)

                    powers(0)
                    for g in range(GROUPS):
                        if g + 1 < GROUPS:
                            powers(g + 1)
                        pool.wait_ge(parts_ready, START + GROUPS * b + g + 1)
                        pool.sem_inc(core.taken, 1)
                        for slot in POOL_SLOTS:
                            ins = lay_out(nc.gpsimd, H, NH, slot, K_PART[slot], slice(GT * g, GT * g + GT))
                        ins.then_inc(k_slots_ready, 1)
                    pool.wait_ge(k_part_ready, START + b + 1)
                    pool.sem_inc(core.taken, 1)
                    nc.gpsimd.partition_all_reduce(k_most[:, :], k_part[:, :], P, bass.bass_isa.ReduceOp.max).then_inc(k_most_ready, 1)
                    core.widest_bound(pool, b)

            @block.vector
            def _(dve):
                dve.wait_ge(consts, START + CONSTS)
                dve.wait_ge(filled, START + FILLS)
                nc.vector.tensor_copy(ident_b[:, :], ident[:, :]).then_inc(ident_b_ready, 1)
                nc.vector.tensor_copy(later_b[:, :], later_t[:, :]).then_inc(ident_b_ready, 1)
                steps, rotary = Steps(dve, chain, CH), Steps(dve, rotary_chain, 2)
                with dve.Fori(0, B) as b:
                    dve.wait_ge(loaded, START + 16 * b + 16)

                    def centre(g):
                        n = GROUPS * b + g
                        tiles = slice(GT * g, GT * g + GT)
                        h = xs[g % 2][:, :, :]
                        steps.start(n)
                        centred_and_variance(nc, steps, x[:, tiles, :], h, sq[:, :, :], mean[:, :], var[:, :],
                                             LN_EPS, var_ready)

                    def layer_norm(g):
                        n = GROUPS * b + g
                        tiles = slice(GT * g, GT * g + GT)
                        h = xs[g % 2][:, :, :]
                        dve.wait_ge(rstd_ready, START + n + 1)
                        steps.link(nc.vector.tensor_tensor(z[:, tiles, :], h, bcast(rstd[:, :], C), ALU.mult))
                        steps.link(nc.vector.tensor_tensor(sq[:, :, :], z[:, tiles, :], z[:, tiles, :], ALU.mult))
                        steps.link(nc.vector.reduce_sum(var2[:, :], sq[:, :, :], AX.X))
                        nc.vector.tensor_scalar(var2[:, :], var2[:, :], 1.0 / C, RMS_EPS, ALU.mult, ALU.add).then_inc(var2_ready, 1)

                    def rms_norm(g):
                        n = GROUPS * b + g
                        tiles = slice(GT * g, GT * g + GT)
                        h = xs[g % 2][:, :, :]
                        dve.wait_ge(rstd2_ready, START + n + 1)
                        nc.vector.tensor_tensor(h, z[:, tiles, :], bcast(rstd2[:, :], C), ALU.mult).then_inc(xn_ready, 1)

                    centre(0)
                    layer_norm(0)
                    rms_norm(0)
                    for g in range(GROUPS):
                        more = g + 1 < GROUPS
                        if more:
                            centre(g + 1)
                        n = GROUPS * b + g
                        tiles = slice(GT * g, GT * g + GT)
                        rotary.start(n)
                        dve.wait_ge(qk_ready, START + n + 1)
                        t = qk[g % 2]
                        c_b = tcos[:, tiles, :].unsqueeze(2).to_broadcast([P, GT, NH, D])
                        nc.vector.tensor_tensor(turned_qk[:, :, :, 0:D // 2], t[:, :, :, D // 2:D],
                                                tsin[:, tiles, 0:D // 2].unsqueeze(2).to_broadcast([P, GT, NH, D // 2]), ALU.mult)
                        rotary.link(nc.vector.tensor_tensor(turned_qk[:, :, :, D // 2:D], t[:, :, :, 0:D // 2],
                                                            tsin[:, tiles, D // 2:D].unsqueeze(2).to_broadcast([P, GT, NH, D // 2]), ALU.mult))
                        rotary.link(nc.vector.tensor_tensor(t[:, :, :, :], t[:, :, :, :], c_b, ALU.mult))
                        flat_qk = t[:, :, :, :].rearrange("p t h d -> p t (h d)")
                        nc.vector.tensor_tensor(flat_qk, flat_qk, turned_qk[:, :, :, :].rearrange("p t h d -> p t (h d)"), ALU.add).then_inc(rotated, 1)
                        if more:
                            layer_norm(g + 1)
                        dve.wait_ge(part0_ready, START + n + 1)
                        dve.wait_ge(rotated, START + n + 1)
                        nc.vector.tensor_tensor(rest[:, :, :], flat_qk, parts[0][:, :, :], ALU.subtract).then_inc(rest_ready, 1)
                        dve.wait_ge(rest_ready, START + n + 1)
                        dve.wait_ge(k_slots_ready, START + n)
                        nc.vector.tensor_copy(parts[1][:, :, :], rest[:, :, :]).then_inc(part1_ready, 1)
                        dve.wait_ge(part1_ready, START + n + 1)
                        nc.vector.tensor_tensor(parts[2][:, :, :], rest[:, :, :], parts[1][:, :, :], ALU.subtract).then_inc(parts_ready, 1)
                        if more:
                            rms_norm(g + 1)
                        dve.wait_ge(parts_ready, START + n + 1)
                        for slot in range(6):
                            lay_out(nc.vector, 0, H, slot, Q_PART[slot], tiles)
                            if slot not in POOL_SLOTS:
                                lay_out(nc.vector, H, NH, slot, K_PART[slot], tiles)
                        dve.wait_ge(squares_ready, START + n + 1)
                        nc.vector.reduce_sum(norm2[:, tiles, :], squares[:, :, :].rearrange("p t (h d) -> p t h d", d=D), AX.X).then_inc(slots_ready, 1)
                    dve.wait_ge(slots_ready, START + GROUPS * (b + 1))
                    nc.vector.reduce_max(k_part[:, :], norm2[:, :, H:NH].rearrange("p t h -> p h t"), AX.X).then_inc(k_part_ready, 1)
                    core.clear_shift(slots[:, :, 0:H, 6 * D:6 * D + 3])
                    dve.wait_ge(k_most_ready, START + b + 1)
                    for e in range(HK):
                        ins = nc.vector.tensor_scalar(bound[:, :, 2 * e:2 * e + 2], norm2[:, :, 2 * e:2 * e + 2], k_most[:, e:e + 1], None, ALU.mult)
                    ins.then_inc(product_ready, 1)
                    dve.wait_ge(bound_ready, START + b + 1)
                    core.find_flag(dve, b, bound[:, :, :])

                    def take_turned_for_maxima():
                        for t in range(TILES):
                            dve.wait_ge(row_turn_ready, START + TILES * b + t + 1)
                            nc.vector.tensor_copy(qkt[:, :, t * P:(t + 1) * P], ps_turn[t % 2]).then_inc(row_turned_out, 1)

                    flag = core.read_flag(dve)
                    with dve.If(flag > 0):
                        take_turned_for_maxima()
                        for t in range(TILES):
                            for h in range(H):
                                core.vector_row_max(dve, (b * TILES + t) * H + h, t * P + P if t < TILES - 1 else SEQ,
                                                    lambda n: slots[:, t, h, 6 * D + n:6 * D + n + 1], later, diagonal)
                    with dve.Else():
                        nc.vector.tensor_scalar(slots[:, :, 0:H, 6 * D], bound[:, :, :], -1.0, None, ALU.mult)
                        dve.sem_inc(row_turned_out, TILES)
                        dve.sem_inc(core.row_read, TILES * H)
                        dve.sem_inc(core.row_step, 7 * TILES * H)
                    nc.vector.memset(spare[:, :], 0.0).then_inc(shift_ready, 1)
                    for t in range(1, TILES, 2):
                        dve.wait_ge(turn_ready, START + TILES * b + t + 1)
                        nc.vector.tensor_copy(qkt[:, :, t * P:(t + 1) * P], ps_turn[1]).then_inc(turned_out_dve, 1)
                    for q in range(BLOCKS):
                        width = QW if q < QBLOCKS else P
                        units = before[BLOCKS] * b + before[q]
                        core.vector(dve, BLOCKS * b + q, units + len(spans[q]), width,
                                    lambda t: o[:, 4 * q + t, :].rearrange("p (h d) -> p h d", d=D))
                    dve.wait_ge(loaded_res, START + 16 * b + 16)
                    for g in range(GROUPS):
                        n = GROUPS * b + g
                        dve.wait_ge(y_ps_ready, START + n + 1)
                        dve.wait_ge(stored[g % 2], START + 32 * (OF_KIND[g % 2] * b + g // 2))
                        nc.vector.tensor_tensor(y[g % 2][:, :, :], ps_y[g % 2], z[:, GT * g:GT * g + GT, :], ALU.add).then_inc(y_ready, 1)
                        dve.wait_ge(y_ready, START + n + 1)
                        nc.vector.tensor_tensor(y_base[g % 2][:, :, :], y[g % 2][:, :, :], x_res[:, GT * g:GT * g + GT, :], ALU.add).then_inc(base_ready, 1)

            @block.tensor
            def _(pe):
                pe.wait_ge(consts, START + CONSTS)
                pe.wait_ge(filled, START + FILLS)
                pe.wait_ge(ident_b_ready, START + 2)
                nc.tensor.matmul(core.acc[:, :], qkt[:, 0, 0:P], qkt[:, 0, 0:512], start=True, stop=True).then_inc(zeroed_acc, 1)
                with pe.Fori(0, B) as b:
                    for g in range(GROUPS):
                        n = GROUPS * b + g
                        pe.wait_ge(xn_ready, START + n + 1)
                        pe.sem_inc(core.taken, 1)
                        for t in range(GT):
                            ins = nc.tensor.transpose(ps_t[0:C, t * P:(t + 1) * P], xs[g % 2][:, t, :], ident[:, :])
                        ins.then_inc(xt_ready, 1)
                        pe.wait_ge(ht_ready, START + n + 1)
                        pe.wait_ge(v_ready, START + n)
                        pe.sem_inc(core.taken, 1)
                        for t in range(GT):
                            ins = nc.tensor.matmul(ps_qkv[:, t, :], ht[:, t * P:(t + 1) * P], wqkv[:, :], start=True, stop=True)
                        ins.then_inc(qkv_ready, 1)
                    def turn(ready, copied):
                        for t in range(TILES):
                            pe.wait_ge(*copied(t))
                            for h in range(NH):
                                ins = nc.tensor.matmul(ps_turn[t % 2][:, h, :], slots[:, t, h, :], ident_b[:, :], start=True, stop=True)
                            ins.then_inc(ready, 1)

                    pe.wait_ge(v_ready, START + GROUPS * (b + 1))
                    pe.wait_ge(k_slots_ready, START + GROUPS * (b + 1))
                    pe.wait_ge(core.flag_ready, START + b + 1)
                    pe.sem_inc(core.taken, 1)
                    flag = core.read_flag(pe)
                    with pe.If(flag > 0):
                        turn(row_turn_ready, lambda t: (row_turned_out, START + TILES * b + max(t - 1, 0)))
                        pe.wait_ge(row_turned_out, START + TILES * (b + 1))
                        for t in range(TILES):
                            for h in range(H):
                                core.tensor_row_scores(pe, (b * TILES + t) * H + h, qkt[:, h, t * P:(t + 1) * P],
                                                       lambda k0, k1: qkt[:, H + h // 2, k0:k1], t * P + P if t < TILES - 1 else SEQ)
                    with pe.Else():
                        pe.sem_inc(row_turn_ready, TILES)
                        pe.sem_inc(core.row_scores, TILES * H)
                    pe.wait_ge(shift_ready, START + b + 1)
                    turn(turn_ready, lambda t: (turned_out_dve, START + ODD * b + t // 2) if t % 2
                         else (turned_out_act, START + EVEN * b + t // 2))
                    pe.wait_ge(turned_out_act, START + EVEN * (b + 1))
                    pe.wait_ge(turned_out_dve, START + ODD * (b + 1))
                    pe.sem_inc(core.taken, 1)
                    work = None
                    for q in range(BLOCKS):
                        width = QW if q < QBLOCKS else P
                        last, work = work, Work(spans[q], width, lambda t, h: qkt[:, H + h // 2, t * P:t * P + core.keys(t)],
                                                lambda h, first, q=q, width=width: qkt[:, h, QW * q + first:QW * q + width],
                                                lambda t, h: v[0:core.keys(t), t, h // 2, :], ident_b, later_b[:, :])
                        nb, units = BLOCKS * b + q, before[BLOCKS] * b + before[q]
                        core.tensor(pe, nb, units, work, last, ident[:, :])
                    core.tensor_end(pe, nb, units, work, ident[:, :])

                    def turn_output(g):
                        pe.wait_ge(ot_ready, START + GROUPS * b + max(g - 1, 0))
                        pe.sem_inc(core.taken, 1)
                        for t in range(GT):
                            ins = nc.tensor.transpose(ps_ot[g % 2][0:C, t * P:(t + 1) * P], o[:, GT * g + t, :], ident[:, :])
                        ins.then_inc(ot_ps_ready, 1)

                    pe.wait_ge(core.block_done, START + BLOCKS * (b + 1))
                    turn_output(0)
                    for g in range(GROUPS):
                        n = GROUPS * b + g
                        if g + 1 < GROUPS:
                            turn_output(g + 1)
                        pe.wait_ge(ot_ready, START + n + 1)
                        pe.wait_ge(y_ready, START + n - (g > 0))
                        pe.sem_inc(core.taken, 1)
                        for t in range(GT):
                            ins = nc.tensor.matmul(ps_y[g % 2][:, t, :], ot[g % 2][:, t * P:(t + 1) * P], wo[:, :], start=True, stop=True)
                        ins.then_inc(y_ps_ready, 1)

            @block.scalar
            def _(act):
                act.wait_ge(consts, START + CONSTS)
                act.wait_ge(filled, START + FILLS)
                with act.Fori(0, B) as b:

                    def project(g):
                        n = GROUPS * b + g
                        act.wait_ge(xt_ready, START + n + 1)
                        act.wait_ge(qkv_ready, START + n)
                        nc.scalar.activation(ht[:, :], ps_t[0:C, :], ACT.Identity, scale=ncol[:, 0:1]).then_inc(ht_ready, 1)
                        act.wait_ge(qkv_ready, START + n + 1)
                        act.wait_ge(parts_ready, START + n - (g > 0))
                        nc.scalar.activation(qk[g % 2][:, :, 0:H, :].rearrange("p t h d -> p t (h d)"), ps_qkv[:, :, 0:H * D], ACT.Copy,
                                             scale=float(D) ** -0.5)
                        nc.scalar.activation(qk[g % 2][:, :, H:NH, :].rearrange("p t h d -> p t (h d)"), ps_qkv[:, :, H * D:NH * D],
                                             ACT.Copy).then_inc(qk_ready, 1)
                        for e in range(HK):
                            ins = nc.scalar.activation(v[:, GT * g:GT * g + GT, e, 0:D], ps_qkv[:, :, (NH + e) * D:(NH + e + 1) * D], ACT.Copy)
                        ins.then_inc(v_ready, 1)

                    project(0)
                    for g in range(GROUPS):
                        n = GROUPS * b + g
                        act.wait_ge(rotated, START + n + 1)
                        act.wait_ge(slots_ready, START + n)
                        act.wait_ge(k_slots_ready, START + n)
                        flat_qk = qk[g % 2][:, :, :, :].rearrange("p t h d -> p t (h d)")
                        nc.scalar.activation(parts[0][:, :, :], flat_qk, ACT.Copy).then_inc(part0_ready, 1)
                        nc.scalar.activation(squares[:, :, :], flat_qk, ACT.Square).then_inc(squares_ready, 1)
                        if g + 1 < GROUPS:
                            project(g + 1)
                    act.wait_ge(product_ready, START + b + 1)
                    nc.scalar.activation(bound[:, :, :], bound[:, :, :], ACT.Sqrt).then_inc(bound_ready, 1)
                    for t in range(0, TILES, 2):
                        act.wait_ge(turn_ready, START + TILES * b + t + 1)
                        nc.scalar.activation(qkt[:, :, t * P:(t + 1) * P], ps_turn[0], ACT.Copy).then_inc(turned_out_act, 1)
                    for q in range(BLOCKS):
                        width = QW if q < QBLOCKS else P
                        core.scalar(act, BLOCKS * b + q, before[BLOCKS] * b + before[q], spans[q], width,
                                    spans[q - 1] if q else None)

                    def copy_output(g):
                        n = GROUPS * b + g
                        act.wait_ge(ot_ps_ready, START + n + 1)
                        act.wait_ge(y_ps_ready, START + n - (g > 0))
                        nc.scalar.activation(ot[g % 2][:, :], ps_ot[g % 2][0:C, :], ACT.Copy).then_inc(ot_ready, 1)

                    copy_output(0)
                    for g in range(GROUPS):
                        n = GROUPS * b + g
                        if g + 1 < GROUPS:
                            copy_output(g + 1)
                        act.wait_ge(base_ready, START + n + 1)
                        act.wait_ge(y_ready, START + n + 1)
                        act.dma_start(tile_view(x2, b)[:, GT * g:GT * g + GT, :], y[g % 2][:, :, :]).then_inc(stored[g % 2], 16)
                        act.dma_start(tile_view(base, b)[:, GT * g:GT * g + GT, :], y_base[g % 2][:, :, :]).then_inc(stored[g % 2], 16)
                for u in range(2):
                    act.wait_ge(stored[u], START + 32 * OF_KIND[u] * B)


def split_three(v, link, whole, rest, first, second, third, third_rows=None):
    link(v.tensor_copy(first, whole))
    link(v.tensor_tensor(rest, whole, first, ALU.subtract))
    link(v.tensor_copy(second, rest))
    if third_rows is not None:
        rest, second = rest[third_rows], second[third_rows]
    return v.tensor_tensor(third, rest, second, ALU.subtract)


def experts(nc, x2, base, out, w_1, w_2, w_3, selector, w_router, norm_col, rank_in, ident_in):
    tag = "moe"
    E = w_router.shape[1]
    HIDDEN = w_1.shape[1]
    CHUNKS = HIDDEN // P
    LAG = 3
    BLOCKS = QBLOCKS + 1
    with ExitStack() as ctx:
        sb_, ps_, sem_, begin = phase_tools(nc, ctx)
        sb = lambda name, shape, dt=F32: sb_(f"{tag}_{name}", shape, dt)
        ps = lambda name, shape: ps_(f"{tag}_{name}", shape)
        sem = lambda name: sem_(f"{tag}_{name}")
        ident = sb("ident", [P, P])
        ident_b = sb("ident_b", [P, P], BF16)
        w_whole = [sb(f"w_whole{n}", [P, HIDDEN]) for n in range(2)]
        w_rest = sb("w_rest", [P, HIDDEN])
        w_parts = [[sb(f"w{n}_part{m}", [P, HIDDEN], BF16) for m in range(3)] for n in range(2)]
        w2 = sb("w2", [P, CHUNKS, C])
        sel = sb("sel", [3 * E, HIDDEN])
        sel_b = sb("sel_b", [3 * E, HIDDEN], BF16)
        wr, ncol, rank = sb("wr", [C, E]), sb("ncol", [C, 1]), sb("rank", [P, E])
        half = sb("half", [P, TILES])
        zero, spare = sb("zero", [P, 1]), sb("spare", [P, 1])
        x = sb("x", [P, TILES, C])
        acc = sb("acc", [P, TILES, C])
        sq = sb("sq", [P, TILES, C])
        var, rstd = sb("var", [P, TILES]), sb("rstd", [P, TILES])
        ft = [sb(f"ft{u}", [C, 512]) for u in range(2)]
        ft_rest = sb("ft_rest", [C, 512])
        f_parts = [sb(f"f_part{m}", [P, SEQP], BF16) for m in range(2)]
        prob = sb("prob", [P, TILES, E])
        w_rest8 = sb("w_rest8", [P, TILES, E])
        weight_parts = sb("weight_parts", [P, TILES, 3 * E], BF16)
        weight_t = sb("weight_t", [3 * E, SEQP], BF16)
        most, total = sb("most", [P, TILES]), sb("total", [P, TILES])
        first, second = sb("first", [P, TILES]), sb("second", [P, TILES])
        is_first, is_second, work = (sb(n, [P, TILES, E]) for n in ("is_first", "is_second", "work"))
        gate = [sb(f"gate{n}", [P, QW]) for n in range(2)]
        product = [sb(f"product{n}", [P, QW]) for n in range(2)]
        RH = 5
        hid = [sb(f"hid{n}", [P, QW]) for n in range(RH)]
        out_t = sb("out_t", [P, QW])
        ps_a = [ps(f"ps_a{n}", [P, 512]) for n in range(2)]
        ps_b = [ps(f"ps_b{n}", [P, 512]) for n in range(2)]
        ps_w = [ps(f"ps_w{n}", [P, 512]) for n in range(2)]
        ps_o, ps_t = ps("ps_o", [P, 512]), ps("ps_t", [P, 512])
        turned = (ps_t, ps_w[0])
        names = ("consts", "filled", "taken", "loaded", "chain", "var_ready", "rstd_ready", "xn_ready", "xt_ready",
                 "ft_ready", "logits_ready", "less_max", "exp_ready", "wt_ready", "wt_copied", "parts_chain",
                 "weights_ready", "up_ready", "gate_ready", "product_ready", "hid_ready", "down_ready", "out_copied",
                 "out_turned", "added", "stored", "taken_dve", "parts_done", "half_added")
        (consts, filled, taken, loaded, chain, var_ready, rstd_ready, xn_ready, xt_ready, ft_ready, logits_ready,
         less_max, exp_ready, wt_ready, wt_copied, parts_chain, weights_ready, up_ready, gate_ready, product_ready,
         hid_ready, down_ready, out_copied, out_turned, added, stored, taken_dve, parts_done, half_added) = map(sem, names)
        NT = -(-TILES // 4)
        CH = 21 + 5 + 5 * NT
        tile_view = lambda a, b: a[b].rearrange("(t p) c -> p t c", p=P)
        tables = ((ident[:, :], ident_in), (w_whole[0][:, :], w_1), (w_whole[1][:, :], w_3), (w2[:, :, :], w_2),
                  (sel[:, :], selector), (wr[:, :], w_router), (ncol[:, :], norm_col), (rank[:, :], rank_in))
        CONSTS = 16 * len(tables)

        def all_blocks(eng, b, body, end):
            body(b * BLOCKS, 0, 0, QW, None)
            with eng.Fori(0, (QBLOCKS - 1) // 2) as i:
                for u in (1, 2):
                    body(b * BLOCKS + u + i * 2, i * 2 + u, u % 2, QW, QW)
            for q in range(1 + (QBLOCKS - 1) // 2 * 2, QBLOCKS):
                body(b * BLOCKS + q, q, q % 2, QW, QW)
            body(b * BLOCKS + QBLOCKS, QBLOCKS, QBLOCKS % 2, P, QW)
            end(b * BLOCKS + QBLOCKS, QBLOCKS, P)

        begin()
        with nc.Block() as block:
            @block.sync
            def _(sp):
                for d, a in tables:
                    sp.dma_start(d, a).then_inc(consts, 16)
                with sp.Fori(0, B) as b:
                    sp.wait_ge(xn_ready, START + b)
                    sp.dma_start(x[:, :, :], tile_view(x2, b)).then_inc(loaded, 16)
                    sp.wait_ge(stored, START + 32 * b)
                    sp.dma_start(acc[:, :, :], tile_view(base, b)).then_inc(loaded, 16)

            @block.gpsimd
            def _(pool):
                nc.gpsimd.memset(half[:, :], -0.5).then_inc(filled, 1)
                pool.wait_ge(filled, START + 1)
                nc.gpsimd.memset(zero[:, :], 0.0).then_inc(filled, 1)
                with pool.Fori(0, B) as b:
                    pool.wait_ge(var_ready, START + b + 1)
                    nc.gpsimd.tensor_tensor(rstd[:, :], var[:, :], half[:, :], ALU.pow).then_inc(rstd_ready, 1)

            @block.vector
            def _(dve):
                dve.wait_ge(consts, START + CONSTS)
                dve.wait_ge(filled, START + 1)
                v = nc.vector
                v.tensor_copy(ident_b[:, :], ident[:, :])
                v.tensor_copy(sel_b[:, :], sel[:, :])
                prepare = Steps(dve, parts_chain, 6)
                for n in range(2):
                    prepare.start(n)
                    a, b_, c_ = (t[:, :] for t in w_parts[n])
                    last = split_three(v, prepare.link, w_whole[n][:, :], w_rest[:, :], a, b_, c_[0:C, :], slice(0, C))
                    prepare.link(last)
                    prepare.link(v.tensor_copy(c_[C:P, :], a[C:P, :]))
                    prepare.link(v.memset(work[:, 0:1, 0:1], 0.0))
                v.memset(most[:, 0:1], 0.0).then_inc(parts_done, 1)
                dve.wait_ge(parts_done, START + 1)
                steps = Steps(dve, chain, CH)
                with dve.Fori(0, B) as b:
                    steps.start(b)
                    dve.wait_ge(loaded, START + 32 * b + 32)
                    steps.link(v.tensor_tensor(sq[:, :, :], x[:, :, :], x[:, :, :], ALU.mult))
                    steps.link(v.reduce_sum(var[:, :], sq[:, :, :], AX.X))
                    v.tensor_scalar(var[:, :], var[:, :], 1.0 / C, RMS_EPS, ALU.mult, ALU.add).then_inc(var_ready, 1)
                    dve.wait_ge(rstd_ready, START + b + 1)
                    v.tensor_tensor(sq[:, :, :], x[:, :, :], bcast(rstd[:, :], C), ALU.mult).then_inc(xn_ready, 1)
                    for n in range(NT):
                        wd = min(512, SEQP - n * 512)
                        cols = slice(n * 512, n * 512 + wd)
                        dve.wait_ge(xt_ready, START + NT * b + n + 1)
                        dve.wait_ge(logits_ready, START + NT * b + max(n - 1, 0))
                        t = ft[n % 2][:, 0:wd]
                        steps.link(v.tensor_scalar(t, turned[n % 2][0:C, 0:wd], ncol[:, 0:1], None, ALU.mult))
                        steps.link(split_three(v, steps.link, t, ft_rest[:, 0:wd], f_parts[0][0:C, cols],
                                               f_parts[0][C:P, cols], f_parts[1][C:P, cols]))
                        v.tensor_copy(f_parts[1][0:C, cols], f_parts[0][0:C, cols]).then_inc(ft_ready, 1)
                    dve.wait_ge(logits_ready, START + NT * (b + 1))
                    logits = ps_o[:, 0:TILES * E].rearrange("p (t e) -> p t e", e=E)
                    steps.link(v.reduce_max(most[:, :], logits, AX.X))
                    v.tensor_tensor(prob[:, :, :], logits, bcast(most[:, :], E), ALU.subtract).then_inc(less_max, 1)
                    dve.wait_ge(exp_ready, START + b + 1)
                    steps.link(v.reduce_sum(total[:, :], prob[:, :, :], AX.X))
                    steps.link(v.reciprocal(total[:, :], total[:, :]))
                    steps.link(v.tensor_tensor(prob[:, :, :], prob[:, :, :], bcast(total[:, :], E), ALU.mult))
                    rank_b = rank[:, :].unsqueeze(1).to_broadcast([P, TILES, E])

                    def pick(values, top, chosen):
                        steps.link(v.reduce_max(top, values, AX.X))
                        steps.link(v.tensor_tensor(chosen, values, bcast(top, E), ALU.is_equal))
                        steps.link(v.tensor_tensor(chosen, chosen, rank_b, ALU.mult))
                        steps.link(v.reduce_max(most[:, :], chosen, AX.X))
                        steps.link(v.tensor_tensor(chosen, chosen, bcast(most[:, :], E), ALU.is_equal))
                    pick(prob[:, :, :], first[:, :], is_first[:, :, :])
                    steps.link(v.tensor_scalar(work[:, :, :], is_first[:, :, :], -2.0, None, ALU.mult))
                    steps.link(v.tensor_tensor(work[:, :, :], work[:, :, :], prob[:, :, :], ALU.add))
                    pick(work[:, :, :], second[:, :], is_second[:, :, :])
                    steps.link(v.scalar_tensor_tensor(out=total[:, :], in0=first[:, :], scalar=1e-9, in1=second[:, :],
                                                      op0=ALU.add, op1=ALU.add))
                    steps.link(v.tensor_tensor(is_first[:, :, :], is_first[:, :, :], is_second[:, :, :], ALU.add))
                    steps.link(v.reciprocal(total[:, :], total[:, :]))
                    steps.link(v.tensor_tensor(prob[:, :, :], prob[:, :, :], is_first[:, :, :], ALU.mult))
                    steps.link(v.tensor_tensor(prob[:, :, :], prob[:, :, :], bcast(total[:, :], E), ALU.mult))
                    split_three(v, steps.link, prob[:, :, :], w_rest8[:, :, :], weight_parts[:, :, 0:E],
                                weight_parts[:, :, E:2 * E], weight_parts[:, :, 2 * E:3 * E]).then_inc(weights_ready, 1)
                    for n in range(NT):
                        wd = min(512, SEQP - n * 512)
                        dve.wait_ge(wt_ready, START + NT * b + n + 1)
                        v.tensor_copy(weight_t[:, n * 512:n * 512 + wd], ps_t[0:3 * E, 0:wd]).then_inc(wt_copied, 1)
                    dve.sem_inc(taken_dve, 1)

                    def add_sums(nb, q, width):
                        target = acc[:, bass.ds(q * 4, width // P), :]
                        dve.wait_ge(out_turned, START + nb + 1)
                        halves = ps_t[:, 0:width].rearrange("p (t two c) -> p t two c", two=2, c=C)
                        v.tensor_tensor(target, target, halves[:, :, 0, :], ALU.add).then_inc(half_added, 1)
                        dve.wait_ge(half_added, START + nb + 1)
                        v.tensor_tensor(target, target, halves[:, :, 1, :], ALU.add).then_inc(added, 1)

                    def body(nb, q, odd, width, width_before):
                        for k in range(CHUNKS):
                            n = CHUNKS * nb + k
                            u = (k + odd) % 2
                            dve.wait_ge(gate_ready, START + n + 1)
                            v.tensor_tensor(product[u][:, 0:width], gate[u][:, 0:width], ps_b[u][:, 0:width],
                                            ALU.mult).then_inc(product_ready, 1)
                            dve.wait_ge(product_ready, START + n + 1)
                            dve.wait_ge(down_ready, START + CHUNKS * nb + max(k - RH + 1, 0))
                            v.tensor_tensor(hid[k % RH][:, 0:width], product[u][:, 0:width], ps_w[u][:, 0:width],
                                            ALU.mult).then_inc(hid_ready, 1)
                            if k == 2 and width_before is not None:
                                add_sums(nb - 1, q - 1, width_before)
                    all_blocks(dve, b, body, add_sums)

            @block.tensor
            def _(pe):
                pe.wait_ge(consts, START + CONSTS)
                pe.wait_ge(parts_done, START + 1)
                with pe.Fori(0, B) as b:
                    pe.wait_ge(xn_ready, START + b + 1)
                    pe.wait_ge(added, START + BLOCKS * b)

                    def turn_tiles(n):
                        pe.wait_ge(ft_ready, START + NT * b + max(n - 1, 0))
                        pe.sem_inc(taken, 1)
                        for t in range(4 * n, min(4 * n + 4, TILES)):
                            ins = nc.tensor.transpose(turned[n % 2][0:C, (t % 4) * P:(t % 4 + 1) * P], sq[:, t, :], ident[:, :])
                        ins.then_inc(xt_ready, 1)

                    turn_tiles(0)
                    for n in range(NT):
                        if n + 1 < NT:
                            turn_tiles(n + 1)
                        pe.wait_ge(ft_ready, START + NT * b + n + 1)
                        pe.sem_inc(taken, 1)
                        for t in range(4 * n, min(4 * n + 4, TILES)):
                            ins = nc.tensor.matmul(ps_o[:, t * E:(t + 1) * E], ft[n % 2][:, (t % 4) * P:(t % 4 + 1) * P], wr[:, :], start=True, stop=True)
                        ins.then_inc(logits_ready, 1)
                    pe.wait_ge(weights_ready, START + b + 1)
                    for n in range(NT):
                        pe.wait_ge(wt_copied, START + NT * b + n)
                        pe.sem_inc(taken, 1)
                        for t in range(4 * n, min(4 * n + 4, TILES)):
                            ins = nc.tensor.matmul(ps_t[0:3 * E, (t % 4) * P:(t % 4 + 1) * P], weight_parts[:, t, :], ident_b[:, :],
                                                   start=True, stop=True)
                        ins.then_inc(wt_ready, 1)
                    pe.wait_ge(wt_copied, START + NT * (b + 1))
                    pe.sem_inc(taken, 1)

                    def down(nb, width, ks):
                        pe.wait_ge(hid_ready, START + CHUNKS * nb + ks[-1] + 1)
                        if ks[0] == 0:
                            pe.wait_ge(out_copied, START + nb)
                        pe.sem_inc(taken, 1)
                        for k in ks:
                            lo = C * (k % 2)
                            nc.tensor.matmul(ps_o[lo:lo + C, 0:width], w2[:, k, :], hid[k % RH][:, 0:width],
                                             start=(k < 2), stop=(k >= CHUNKS - 2)).then_inc(down_ready, 1)

                    def turn_sums(nb, width):
                        pe.wait_ge(out_copied, START + nb + 1)
                        pe.wait_ge(added, START + nb)
                        pe.sem_inc(taken, 1)
                        for t in range(width // P):
                            ins = nc.tensor.transpose(ps_t[:, t * P:(t + 1) * P], out_t[:, t * P:(t + 1) * P], ident[:, :])
                        ins.then_inc(out_turned, 1)

                    def body(nb, q, odd, width, width_before):
                        at = lambda a: a[:, bass.ds(q * QW, width)]
                        for k in range(CHUNKS):
                            u = (k + odd) % 2
                            pe.wait_ge(hid_ready, START + CHUNKS * nb + (k - 1 if width_before is not None else max(k - 1, 0)))
                            units = slice(k * P, (k + 1) * P)
                            for n, bank in enumerate((ps_a[u], ps_b[u])):
                                for m in range(3):
                                    ins = nc.tensor.matmul(bank[:, 0:width], w_parts[n][m][:, units], at(f_parts[m // 2]),
                                                           start=(m == 0), stop=(m == 2))
                            nc.tensor.matmul(ps_w[u][:, 0:width], sel_b[:, units], at(weight_t), start=True, stop=True).then_inc(up_ready, 1)
                            if k == 0 and width_before is not None:
                                down(nb - 1, width_before, (CHUNKS - 1,))
                            if k == 1 and width_before is not None:
                                turn_sums(nb - 1, width_before)
                            if k >= LAG and k % 2:
                                down(nb, width, (k - LAG, k - LAG + 1))
                        down(nb, width, (CHUNKS - 3, CHUNKS - 2))

                    def end(nb, q, width):
                        down(nb, width, (CHUNKS - 1,))
                        turn_sums(nb, width)
                    assert CHUNKS % 2 == 1 and LAG == 3
                    all_blocks(pe, b, body, end)

            @block.scalar
            def _(act):
                act.wait_ge(filled, START + 2)
                with act.Fori(0, B) as b:
                    act.wait_ge(less_max, START + b + 1)
                    nc.scalar.activation(prob[:, :, :], prob[:, :, :], ACT.Exp).then_inc(exp_ready, 1)

                    def copy_sums(nb, q, width):
                        act.wait_ge(down_ready, START + CHUNKS * (nb + 1))
                        act.wait_ge(out_turned, START + nb)
                        nc.scalar.activation(out_t[:, 0:width], ps_o[:, 0:width], ACT.Copy).then_inc(out_copied, 1)

                    def body(nb, q, odd, width, width_before):
                        nc.scalar.activation(spare[:, :], zero[:, :], ACT.Silu)
                        for k in range(CHUNKS):
                            n = CHUNKS * nb + k
                            u = (k + odd) % 2
                            act.wait_ge(up_ready, START + n + 1)
                            act.wait_ge(product_ready, START + CHUNKS * nb + (k - 1 if width_before is not None else max(k - 1, 0)))
                            nc.scalar.activation(gate[u][:, 0:width], ps_a[u][:, 0:width], ACT.Silu).then_inc(gate_ready, 1)
                            if k == 0 and width_before is not None:
                                copy_sums(nb - 1, q - 1, width_before)
                    all_blocks(act, b, body, copy_sums)
                    act.wait_ge(added, START + BLOCKS * (b + 1))
                    full = (TILES - 1) * P
                    act.dma_start(out[b][0:full, :].rearrange("(t p) c -> p t c", p=P), acc[:, 0:TILES - 1, :]).then_inc(stored, 16)
                    act.dma_start(out[b][full:SEQ, :], acc[0:LAST, TILES - 1, :]).then_inc(stored, 16)
                act.wait_ge(stored, START + 32 * B)


def program(nc, a, out):
    dram = lambda name, shape: nc.dram_tensor(name, shape, F32, kind="Internal").ap()
    tokens, tokens2 = dram("tokens", (B * TOK, C)), dram("tokens2", (B * TOK, C))
    padded = dram("padded", (B, PAD, PAD, C))
    seq0, seq1, x2, base = (dram(n, (B, SEQP, C)) for n in ("seq0", "seq1", "x2", "base"))
    image = lambda t: t.rearrange("(b r c) ch -> b r c ch", b=B, r=SIDE)
    groups = lambda t: t.rearrange("(n g p) c -> n p g c", g=4, p=112)
    S = SIDE

    patch_embed(nc, a["patches"], a["w_patch"], a["patch_norm"], tokens)
    window_attention(nc, "w0", image(tokens), 0, a["norm1_0"], a["wq_0"], a["wk_0"], a["wv_0"], a["wproj_0"],
                     a["bias_0"], None, 1, a["head_mask"], a["ident"])
    mlp(nc, "m0", groups(tokens), groups(tokens2), a["norm2_0"], a["w1_0"], a["w2_0"], a["b2_0"], a["ident"])

    t, t2 = image(tokens), image(tokens2)
    copies(nc, "spread", [[(padded[b, 0:S, 0:S, :], t2[b]) for b in range(B)],
                          [(padded[b, 0:S, S:PAD, :], padded[b, 0:S, 0:SHIFT, :]) for b in range(B)],
                          [(padded[b, S:PAD, :, :], padded[b, 0:SHIFT, :, :]) for b in range(B)]])
    window_attention(nc, "w1", padded, SHIFT, a["norm1_1"], a["wq_1"], a["wk_1"], a["wv_1"], a["wproj_1"],
                     a["bias_1"], a["mask"], 2, a["head_mask"], a["ident"])
    far, near = (slice(SHIFT, S), slice(SHIFT, S)), (slice(0, SHIFT), slice(S, PAD))
    copies(nc, "fold", [[(t[b, r[0], c[0], :], padded[b, r[1], c[1], :]) for b in range(B)
                         for r in (far, near) for c in (far, near)]])
    mlp(nc, "m1", groups(tokens), groups(tokens2), a["norm2_1"], a["w1_1"], a["w2_1"], a["b2_1"], a["ident"])

    flat = tokens2.rearrange("(b t) c -> b t c", b=B)
    copies(nc, "join", [[x for b in range(B) for x in ((seq0[b, 1:SEQ, :], flat[b]), (seq0[b, 0:1, :], a["cls"]),
                                                       (seq0[b, SEQ:SEQP, :], a["zeros"]))]])
    dense_attention(nc, seq0, seq1, a["w_qkv"], a["w_proj"], a["ident"])
    causal_attention(nc, seq1, x2, base, a["f_qkv"], a["f_out"], a["f_norm1"], a["cos"], a["sin"], a["later"],
                     a["later_t"], a["ident"])
    experts(nc, x2, base, out, a["e_w1"], a["e_w2"], a["e_w3"], a["selector"], a["router"],
            a["f_norm2"], a["rank"], a["ident"])


def host_layout(inputs):
    import numpy as np

    a = {k: np.asarray(v) for k, v in inputs.items()}
    f = np.float32
    out = {}
    x = a["x"].reshape(B, SIDE, 4, SIDE, 4).transpose(2, 4, 0, 1, 3).reshape(16, B * TOK)
    out["patches"] = np.concatenate([x, np.ones((1, B * TOK), f)])
    out["w_patch"] = np.concatenate([a["L0_tok_pe_w"].reshape(C, 16).T, a["L0_tok_pe_b"][None]])
    out["patch_norm"] = np.repeat(np.stack([a["L0_tok_pe_ng"], a["L0_tok_pe_nb"]])[None], 112, 0)
    out["ident"] = np.eye(P, dtype=f)
    out["head_mask"] = np.repeat(np.eye(SH, dtype=f), SD, 0)
    yx = np.stack(np.meshgrid(np.arange(WIN), np.arange(WIN), indexing="ij")).reshape(2, -1)
    rel = yx[:, :, None] - yx[:, None, :] + WIN - 1
    rpi = rel[0] * (2 * WIN - 1) + rel[1]
    rows = lambda w, b: np.concatenate([w.T, b[None]])
    for i in range(2):
        out[f"norm1_{i}"] = np.stack([a["L0_tok_n1g"][i], a["L0_tok_n1b"][i]], 1)
        out[f"norm2_{i}"] = np.stack([a["L0_tok_n2g"][i], a["L0_tok_n2b"][i]], 1)
        w, b = a["L0_tok_qkv_w"][i], a["L0_tok_qkv_b"][i]
        for n, name in enumerate(("wq", "wk", "wv")):
            out[f"{name}_{i}"] = rows(w[n * C:(n + 1) * C], b[n * C:(n + 1) * C])
        out[f"wproj_{i}"] = rows(a["L0_tok_proj_w"][i], a["L0_tok_proj_b"][i])
        table = a["L0_tok_rpb"][i][rpi].transpose(0, 2, 1).reshape(NW, SH * NW)
        wide = np.zeros((P, 4, SH * NW), f)
        for h in range(2):
            wide[SLOT * h:SLOT * h + NW] = table[:, None, :]
        out[f"bias_{i}"] = wide[None]
        out[f"w1_{i}"] = rows(a["L0_tok_w1"][i], a["L0_tok_b1"][i])
        out[f"w2_{i}"] = a["L0_tok_w2"][i].T.reshape(2, P, C).transpose(1, 0, 2)
        out[f"b2_{i}"] = a["L0_tok_b2"][i][None]
    region = lambda last: np.where(last & (np.arange(WIN) >= WIN - SHIFT), 1, 0)
    mask = np.zeros((2, P, 4, SH, NW), f)
    for kind in range(2):
        for pair in range(4):
            for h in range(2):
                ry, rx = region(kind == 1), region(2 * pair + h == ROWS - 1)
                reg = (ry[:, None] * 2 + rx[None, :]).reshape(-1)
                m = np.where(reg[:, None] != reg[None, :], f(-100), f(0))
                mask[kind, SLOT * h:SLOT * h + NW, pair] = m[:, None, :]
    out["mask"] = mask.reshape(2, P, 4, SH * NW)
    out["bias_1"] = np.repeat(out["bias_1"], 2, 0)
    out["w_qkv"] = np.concatenate([a["L0_attn_w_qkv"], a["L0_attn_b_qkv"][None]])
    out["w_proj"] = np.concatenate([a["L0_attn_w_proj"], a["L0_attn_b_proj"][None]])
    out["f_qkv"] = np.concatenate([a["L0_ffn_wq"], a["L0_ffn_wk"], a["L0_ffn_wv"]]).T
    out["f_out"] = a["L0_ffn_wo"].T
    out["f_norm1"] = a["L0_ffn_ln1_w"][:, None]
    out["f_norm2"] = a["L0_ffn_ln2_w"][:, None]
    E, unit = a["L0_ffn_w1"].shape[:2]
    hidden = -(-E * unit // P) * P
    wide = lambda w: np.concatenate([w, np.zeros((hidden - len(w), w.shape[1]), f)])
    for n in ("w1", "w3"):
        out[f"e_{n}"] = np.tile(wide(a[f"L0_ffn_{n}"].reshape(E * unit, C)).T, (2, 1))
    out["e_w2"] = wide(a["L0_ffn_w2"].transpose(0, 2, 1).reshape(E * unit, C)).reshape(-1, P, C).transpose(1, 0, 2)
    out["selector"] = np.tile(wide(np.repeat(np.eye(E, dtype=f), unit, 0)).T, (3, 1))
    out["router"] = a["L0_ffn_router_w"].T
    out["rank"] = np.repeat(np.arange(E, 0, -1, dtype=f)[None], P, 0)
    D = 16
    inv_freq = 1.0 / 10000.0 ** (np.arange(0, D, 2, dtype=f) / D)
    angles = np.outer(np.arange(SEQP, dtype=f), inv_freq).astype(f)
    out["cos"] = np.cos(np.concatenate([angles, angles], 1)).astype(f)
    out["sin"] = np.concatenate([-np.sin(angles), np.sin(angles)], 1).astype(f)
    out["later"] = np.triu(np.full((P, P), -1e30, f), 1)
    out["later_t"] = out["later"].T
    out["cls"] = a["cls_tok"].reshape(1, C)
    out["zeros"] = np.zeros((SEQP - SEQ, C), f)
    return {k: np.ascontiguousarray(v) for k, v in out.items()}


def kernel(**inputs):
    import concourse.bacc as _bacc
    from concourse.bass_utils import run_bass_kernel_spmd as _run

    arrays = host_layout(inputs)
    nc = _bacc.Bacc("TRN2", target_bir_lowering=False, num_devices=1)
    args = {k: nc.dram_tensor(f"in_{k}", v.shape, mybir.dt.from_np(v.dtype), kind="ExternalInput").ap()
            for k, v in arrays.items()}
    out = nc.dram_tensor("out_0_dram", (B, SEQ, C), F32, kind="ExternalOutput").ap()
    program(nc, args, out)
    r = _run(nc, [{f"in_{k}": v for k, v in arrays.items()}], core_ids=[0])
    return r.results[0]["out_0_dram"]
```
